# Optimizing a Trainium2 kernel written in Bass

```python
import numpy as np
import jax
import jax.numpy as jnp

def _softmax(x, axis=-1):
    return jax.nn.softmax(x, axis=axis)

def _gelu(x):
    return jax.nn.gelu(x, approximate=True)

def _silu(x):
    return jax.nn.silu(x)

def _sigmoid(x):
    return jax.nn.sigmoid(x)

def _layernorm(x, axis=-1, eps=1e-05):
    m = jnp.mean(x, axis=axis, keepdims=True)
    v = jnp.var(x, axis=axis, keepdims=True)
    return (x - m) / jnp.sqrt(v + eps)

def _scatter_add(tgt, idx, src, axis=0):
    return tgt.at[idx].add(src)

def _segment_sum(src, seg, n):
    return jax.ops.segment_sum(src, seg, n)
kernel_name = 'mk_xattn_seq_d4_seqx_r8_eb9db1'

def setup_inputs(seed: int=0):
    np.random.seed(seed)
    _w = jnp.asarray

    def _rec_inputs():
        import jax
        import jax.numpy as jnp
        _rk = jax.random.key(seed)
        x = -0.0002928 + 1 * jax.random.normal(jax.random.fold_in(_rk, 1), (4, 256, 128), jnp.float32)
        _lenS = 256 - jax.random.randint(jax.random.fold_in(_rk, 7), (4,), 0, max(1, 256 // 4) + 1, jnp.int32)
        _lenS2 = 256 - jax.random.randint(jax.random.fold_in(_rk, 8), (4,), 0, max(1, 256 // 4) + 1, jnp.int32)
        _ctx_1024P = jax.random.normal(jax.random.fold_in(_rk, 11), (4, 16, 128), jnp.float32)
        _ctx_1024c = jax.random.dirichlet(jax.random.fold_in(_rk, 511), 0.3 * jnp.ones((16,), jnp.float32), (4, 256))
        _ctx_1024t = jnp.einsum('bsk,bkd->bsd', _ctx_1024c, _ctx_1024P)
        _ctx_1024t = _ctx_1024t * jax.lax.rsqrt(jnp.mean(jnp.square(_ctx_1024t)) + 1e-12) * 0.953939
        ctx_1024 = -1.39393e-06 + 0.999914 * (_ctx_1024t + 0.3 * jax.random.normal(jax.random.fold_in(_rk, 611), (4, 256, 128), jnp.float32))
        fside_1x16xSxS2_0 = 8.74812e-06 + 0.100005 * jax.random.normal(jax.random.fold_in(_rk, 13), (1, 16, 256, 256), jnp.float32)
        itok_BxS2_4_31999 = jax.random.randint(jax.random.fold_in(_rk, 14), (4, 256), 4, 4000, jnp.int32)
        _ctxb_2048x64P = jax.random.normal(jax.random.fold_in(_rk, 15), (4, 16, 64), jnp.float32)
        _ctxb_2048x64c = jax.random.dirichlet(jax.random.fold_in(_rk, 515), 0.3 * jnp.ones((16,), jnp.float32), (4, 256))
        _ctxb_2048x64t = jnp.einsum('bsk,bkd->bsd', _ctxb_2048x64c, _ctxb_2048x64P)
        _ctxb_2048x64t = _ctxb_2048x64t * jax.lax.rsqrt(jnp.mean(jnp.square(_ctxb_2048x64t)) + 1e-12) * 0.953939
        ctxb_2048x64 = 0.50053 + 0.288505 * (_ctxb_2048x64t + 0.3 * jax.random.normal(jax.random.fold_in(_rk, 615), (4, 256, 64), jnp.float32))
        _validS = jnp.arange(256)[None, :] < _lenS[:, None]
        _validS2 = jnp.arange(256)[None, :] < _lenS2[:, None]
        _causal = jnp.tril(jnp.ones((256, 256), dtype=bool))
        mask_BxSxS2_bk1 = jnp.broadcast_to(_validS2[:, None, :], (4, 256, 256))
        mask_1xS2_if1 = jnp.where(jnp.ones((1, 256), dtype=bool), 1, 0).astype(jnp.int32)
        return (x, ctx_1024, fside_1x16xSxS2_0, itok_BxS2_4_31999, ctxb_2048x64, mask_BxSxS2_bk1, mask_1xS2_if1)
    x, ctx_1024, fside_1x16xSxS2_0, itok_BxS2_4_31999, ctxb_2048x64, mask_BxSxS2_bk1, mask_1xS2_if1 = _rec_inputs()

    def _L0_xattn_setup():
        import jax, jax.numpy as jnp
        import numpy as np
        EPS = 1e-05

        def _layernorm(x, g, b):
            m = jnp.mean(x, axis=-1, keepdims=True)
            v = jnp.mean((x - m) ** 2, axis=-1, keepdims=True)
            return (x - m) / jnp.sqrt(v + EPS) * g + b

        def _mha(x, kv, Wq, Wk, Wv, mask, causal):
            m = mask[:, None]
            Q = jnp.einsum('bsd,hdk->bhsk', x, Wq) * m
            K = jnp.einsum('bsd,hdk->bhsk', kv, Wk) * m
            V = jnp.einsum('bsd,hdk->bhsk', kv, Wv) * m
            energy = jnp.einsum('bhsk,bhtk->bhst', Q, K)
            S = energy.shape[-1]
            lengths = jnp.sum(energy[:, :, 0, :] != 0, axis=-1)
            cols = jnp.arange(S)
            energy = jnp.where(cols[None, None, None, :] >= lengths[:, :, None, None], -jnp.inf, energy)
            if causal:
                energy = jnp.where(cols[None, :] > cols[:, None], -jnp.inf, energy)
            dk = Wq.shape[-1]
            score = jax.nn.softmax(energy / jnp.sqrt(jnp.asarray(dk, energy.dtype)), axis=-1)
            out = jnp.einsum('bhst,bhtk->bhsk', score, V) * m
            B, H, Sx, dkk = out.shape
            return out.transpose(0, 2, 1, 3).reshape(B, Sx, H * dkk)
        key = jax.random.key(seed)
        ks = jax.random.split(key, 20)
        B, S, D, H = (2, 256, 128, 16)
        dk = D // H
        sd = 0.02
        inp = {'x': jax.random.normal(ks[0], (B, S, D), jnp.float32), 'context': jax.random.normal(ks[1], (B, S, D), jnp.float32), 'Wq1': jax.random.normal(ks[2], (H, D, dk), jnp.float32) * sd, 'Wk1': jax.random.normal(ks[3], (H, D, dk), jnp.float32) * sd, 'Wv1': jax.random.normal(ks[4], (H, D, dk), jnp.float32) * sd, 'Wq2': jax.random.normal(ks[5], (H, D, dk), jnp.float32) * sd, 'Wk2': jax.random.normal(ks[6], (H, D, dk), jnp.float32) * sd, 'Wv2': jax.random.normal(ks[7], (H, D, dk), jnp.float32) * sd, 'ln1_g': jnp.ones((D,), jnp.float32), 'ln1_b': jnp.zeros((D,), jnp.float32), 'ln2_g': jnp.ones((D,), jnp.float32), 'ln2_b': jnp.zeros((D,), jnp.float32), 'ln3_g': jnp.ones((D,), jnp.float32), 'ln3_b': jnp.zeros((D,), jnp.float32), 'fc1_w': jax.random.normal(ks[8], (D, D), jnp.float32) * sd, 'fc1_b': jnp.zeros((D,), jnp.float32), 'fc2_w': jax.random.normal(ks[9], (D, D), jnp.float32) * sd, 'fc2_b': jnp.zeros((D,), jnp.float32)}
        return inp
    _L0_xattn_all = _L0_xattn_setup()
    _L0_xattn_in = {k: v for k, v in _L0_xattn_all.items() if k in ('Wq1', 'Wk1', 'Wv1', 'Wq2', 'Wk2', 'Wv2', 'ln1_g', 'ln1_b', 'ln2_g', 'ln2_b', 'ln3_g', 'ln3_b', 'fc1_w', 'fc1_b', 'fc2_w', 'fc2_b')}
    del _L0_xattn_all

    def _L1_xattn_setup():
        import jax, jax.numpy as jnp
        import numpy as np
        B, L, S, D, H, FF = (2, 256, 256, 128, 16, 512)
        HD = D // H
        TEMP = float(D) ** 0.5
        EPS = 1e-05

        def _layernorm(x, g, b):
            mu = jnp.mean(x, axis=-1, keepdims=True)
            var = jnp.mean(jnp.square(x - mu), axis=-1, keepdims=True)
            return (x - mu) * jax.lax.rsqrt(var + EPS) * g + b

        def _mha(q_in, k_in, v_in, wq, bq, wk, bk, wv, bv, wo, bo, mask, bias):
            b, ql = (q_in.shape[0], q_in.shape[1])
            kl = k_in.shape[1]
            q = (q_in @ wq + bq).reshape(b, ql, H, HD).transpose(0, 2, 1, 3)
            k = (k_in @ wk + bk).reshape(b, kl, H, HD).transpose(0, 2, 1, 3)
            v = (v_in @ wv + bv).reshape(b, kl, H, HD).transpose(0, 2, 1, 3)
            attn = jnp.einsum('bhqd,bhkd->bhqk', q, k) / TEMP
            if bias is not None:
                attn = attn + bias
            if mask is not None:
                attn = jnp.where(mask[:, None, :, :], -jnp.inf, attn)
            attn = jax.nn.softmax(attn, axis=-1)
            out = jnp.einsum('bhqk,bhkd->bhqd', attn, v)
            out = out.transpose(0, 2, 1, 3).reshape(b, ql, H * HD)
            return out @ wo + bo
        key = jax.random.key(seed)
        ks = jax.random.split(key, 32)
        w = lambda k, shape, s=0.02: jax.random.normal(k, shape, jnp.float32) * s
        inp = {}
        inp['tgt'] = jax.random.normal(ks[0], (B, L, D), jnp.float32)
        inp['src'] = jax.random.normal(ks[1], (B, S, D), jnp.float32)
        causal = jnp.triu(jnp.ones((L, L), dtype=bool), 1)
        inp['tgt_mask'] = jnp.broadcast_to(causal, (B, L, L))
        inp['attn_bias'] = w(ks[2], (1, H, L, L), 0.1)
        inp['attn_2d_bias'] = w(ks[3], (1, H, L, S), 0.1)
        inp['sa_wq'] = w(ks[4], (D, D))
        inp['sa_bq'] = jnp.zeros((D,))
        inp['sa_wk'] = w(ks[5], (D, D))
        inp['sa_bk'] = jnp.zeros((D,))
        inp['sa_wv'] = w(ks[6], (D, D))
        inp['sa_bv'] = jnp.zeros((D,))
        inp['sa_wo'] = w(ks[7], (D, D))
        inp['sa_bo'] = jnp.zeros((D,))
        inp['sa_g'] = jnp.ones((D,))
        inp['sa_b'] = jnp.zeros((D,))
        inp['ca_wq'] = w(ks[8], (D, D))
        inp['ca_bq'] = jnp.zeros((D,))
        inp['ca_wk'] = w(ks[9], (D, D))
        inp['ca_bk'] = jnp.zeros((D,))
        inp['ca_wv'] = w(ks[10], (D, D))
        inp['ca_bv'] = jnp.zeros((D,))
        inp['ca_wo'] = w(ks[11], (D, D))
        inp['ca_bo'] = jnp.zeros((D,))
        inp['ca_g'] = jnp.ones((D,))
        inp['ca_b'] = jnp.zeros((D,))
        inp['ff_w1'] = w(ks[12], (D, FF))
        inp['ff_b1'] = jnp.zeros((FF,))
        inp['ff_w2'] = w(ks[13], (FF, D))
        inp['ff_b2'] = jnp.zeros((D,))
        inp['ff_g'] = jnp.ones((D,))
        inp['ff_b'] = jnp.zeros((D,))
        return inp
    _L1_xattn_all = _L1_xattn_setup()
    _L1_xattn_in = {k: v for k, v in _L1_xattn_all.items() if k in ('attn_2d_bias', 'sa_wq', 'sa_bq', 'sa_wk', 'sa_bk', 'sa_wv', 'sa_bv', 'sa_wo', 'sa_bo', 'sa_g', 'sa_b', 'ca_wq', 'ca_bq', 'ca_wk', 'ca_bk', 'ca_wv', 'ca_bv', 'ca_wo', 'ca_bo', 'ca_g', 'ca_b', 'ff_w1', 'ff_b1', 'ff_w2', 'ff_b2', 'ff_g', 'ff_b')}
    del _L1_xattn_all

    def _L2_xattn_setup():
        import jax, jax.numpy as jnp
        import numpy as np
        BATCH, T, H, S, P, NH = (4, 256, 128, 64, 64, 8)
        HD = H // NH

        def _layernorm(x, g, b):
            mu = jnp.mean(x, axis=-1, keepdims=True)
            var = jnp.mean((x - mu) ** 2, axis=-1, keepdims=True)
            return (x - mu) * jax.lax.rsqrt(var + 1e-05) * g + b

        def _mha(q_in, kv_in, W_qkv, b_qkv, W_o, b_o):
            Wq, Wk, Wv = jnp.split(W_qkv, 3, axis=0)
            bq, bk, bv = jnp.split(b_qkv, 3, axis=0)

            def heads(x, W, b):
                y = x @ W.T + b
                return y.reshape(y.shape[0], y.shape[1], NH, HD).transpose(0, 2, 1, 3)
            q, k, v = (heads(q_in, Wq, bq), heads(kv_in, Wk, bk), heads(kv_in, Wv, bv))
            scores = jnp.einsum('bhqd,bhkd->bhqk', q, k) * (1.0 / np.sqrt(HD))
            attn = jax.nn.softmax(scores, axis=-1)
            out = jnp.einsum('bhqk,bhkd->bhqd', attn, v)
            out = out.transpose(0, 2, 1, 3).reshape(q_in.shape)
            return out @ W_o.T + b_o
        key = jax.random.key(seed)
        ks = jax.random.split(key, 16)
        sH = 1.0 / np.sqrt(H)
        d = {}
        d['builder_state'] = jax.random.normal(ks[0], (BATCH, T, H), jnp.float32)
        d['base_state'] = jax.random.normal(ks[1], (BATCH, T, H), jnp.float32)
        d['input_ids'] = jax.random.randint(ks[2], (BATCH, T), 0, 4000)
        d['program_probs'] = jax.random.uniform(ks[3], (BATCH, T, P), jnp.float32)
        d['A'] = jax.random.normal(ks[4], (S, S), jnp.float32) * (0.5 / np.sqrt(S))
        d['Bmat'] = jax.random.normal(ks[5], (H, S), jnp.float32) * sH
        d['Cmat'] = jax.random.normal(ks[6], (S, H), jnp.float32) * (1.0 / np.sqrt(S))
        d['W_in'] = jax.random.normal(ks[7], (H, H), jnp.float32) * sH
        d['b_in'] = jnp.zeros((H,), jnp.float32)
        d['W_qkv'] = jax.random.normal(ks[8], (3 * H, H), jnp.float32) * sH
        d['b_qkv'] = jnp.zeros((3 * H,), jnp.float32)
        d['W_o'] = jax.random.normal(ks[9], (H, H), jnp.float32) * sH
        d['b_o'] = jnp.zeros((H,), jnp.float32)
        d['W_prog'] = jax.random.normal(ks[10], (H, P), jnp.float32) * (1.0 / np.sqrt(P))
        d['b_prog'] = jnp.zeros((H,), jnp.float32)
        d['g1'] = jnp.ones((H,), jnp.float32)
        d['beta1'] = jnp.zeros((H,), jnp.float32)
        d['g2'] = jnp.ones((H,), jnp.float32)
        d['beta2'] = jnp.zeros((H,), jnp.float32)
        return d
    _L2_xattn_all = _L2_xattn_setup()
    _L2_xattn_in = {k: v for k, v in _L2_xattn_all.items() if k in ('A', 'Bmat', 'Cmat', 'W_in', 'b_in', 'W_qkv', 'b_qkv', 'W_o', 'b_o', 'W_prog', 'b_prog', 'g1', 'beta1', 'g2', 'beta2')}
    del _L2_xattn_all

    def _L3_xattn_setup():
        import jax, jax.numpy as jnp
        import numpy as np
        NEG = 10000000000.0

        def layer_norm(x, g, b, eps):
            m = jnp.mean(x, axis=-1, keepdims=True)
            v = jnp.mean(jnp.square(x - m), axis=-1, keepdims=True)
            return (x - m) * jax.lax.rsqrt(v + eps) * g + b

        def mha(q, k, v, mask, num_heads):
            B, T, E = q.shape
            S = k.shape[1]
            D = E // num_heads
            qh = q.reshape(B, T, num_heads, D).transpose(0, 2, 1, 3)
            kh = k.reshape(B, S, num_heads, D).transpose(0, 2, 1, 3)
            vh = v.reshape(B, S, num_heads, D).transpose(0, 2, 1, 3)
            scores = jnp.einsum('bhqd,bhkd->bhqk', qh, kh) * (1.0 / np.sqrt(D))
            scores = scores * mask - (1.0 - mask) * NEG
            attn = jax.nn.softmax(scores, axis=-1)
            out = jnp.einsum('bhqk,bhkd->bhqd', attn, vh)
            return out.transpose(0, 2, 1, 3).reshape(B, T, E)
        NUM_HEADS = 16
        key = jax.random.key(seed)
        ks = jax.random.split(key, 16)
        B, T, S, E, F, H = (1, 256, 256, 128, 512, 16)
        std = 0.02
        inp = {'target': jax.random.normal(ks[0], (B, T, E), jnp.float32), 'context': jax.random.normal(ks[1], (B, S, E), jnp.float32), 'target_pad_mask': jnp.ones((B, T), jnp.int32), 'context_pad_mask': jnp.ones((B, S), jnp.int32), 'Wqkv': jax.random.normal(ks[2], (E, 3 * E), jnp.float32) * std, 'Wo1': jax.random.normal(ks[3], (E, E), jnp.float32) * (std / np.sqrt(24.0)), 'bo1': jnp.zeros((E,), jnp.float32), 'g1': jnp.ones((E,), jnp.float32), 'b1': jnp.zeros((E,), jnp.float32), 'Wq': jax.random.normal(ks[4], (E, E), jnp.float32) * std, 'Wk': jax.random.normal(ks[5], (E, E), jnp.float32) * std, 'Wv': jax.random.normal(ks[6], (E, E), jnp.float32) * std, 'Wo2': jax.random.normal(ks[7], (E, E), jnp.float32) * (std / np.sqrt(24.0)), 'bo2': jnp.zeros((E,), jnp.float32), 'g2': jnp.ones((E,), jnp.float32), 'b2': jnp.zeros((E,), jnp.float32), 'W1': jax.random.normal(ks[8], (E, F), jnp.float32) * std, 'bf1': jnp.zeros((F,), jnp.float32), 'W2': jax.random.normal(ks[9], (F, E), jnp.float32) * std, 'bf2': jnp.zeros((E,), jnp.float32), 'g3': jnp.ones((E,), jnp.float32), 'b3': jnp.zeros((E,), jnp.float32)}
        return inp
    _L3_xattn_all = _L3_xattn_setup()
    _L3_xattn_in = {k: v for k, v in _L3_xattn_all.items() if k in ('Wqkv', 'Wo1', 'bo1', 'g1', 'b1', 'Wq', 'Wk', 'Wv', 'Wo2', 'bo2', 'g2', 'b2', 'W1', 'bf1', 'W2', 'bf2', 'g3', 'b3')}
    del _L3_xattn_all
    return {'x': x, 'ctx_1024': ctx_1024, 'fside_1x16xSxS2_0': fside_1x16xSxS2_0, 'itok_BxS2_4_31999': itok_BxS2_4_31999, 'ctxb_2048x64': ctxb_2048x64, 'mask_BxSxS2_bk1': mask_BxSxS2_bk1, 'mask_1xS2_if1': mask_1xS2_if1, 'L0_xattn_Wq1': _L0_xattn_in['Wq1'], 'L0_xattn_Wk1': _L0_xattn_in['Wk1'], 'L0_xattn_Wv1': _L0_xattn_in['Wv1'], 'L0_xattn_Wq2': _L0_xattn_in['Wq2'], 'L0_xattn_Wk2': _L0_xattn_in['Wk2'], 'L0_xattn_Wv2': _L0_xattn_in['Wv2'], 'L0_xattn_ln1_g': _L0_xattn_in['ln1_g'], 'L0_xattn_ln1_b': _L0_xattn_in['ln1_b'], 'L0_xattn_ln2_g': _L0_xattn_in['ln2_g'], 'L0_xattn_ln2_b': _L0_xattn_in['ln2_b'], 'L0_xattn_ln3_g': _L0_xattn_in['ln3_g'], 'L0_xattn_ln3_b': _L0_xattn_in['ln3_b'], 'L0_xattn_fc1_w': _L0_xattn_in['fc1_w'], 'L0_xattn_fc1_b': _L0_xattn_in['fc1_b'], 'L0_xattn_fc2_w': _L0_xattn_in['fc2_w'], 'L0_xattn_fc2_b': _L0_xattn_in['fc2_b'], 'L1_xattn_attn_2d_bias': _L1_xattn_in['attn_2d_bias'], 'L1_xattn_sa_wq': _L1_xattn_in['sa_wq'], 'L1_xattn_sa_bq': _L1_xattn_in['sa_bq'], 'L1_xattn_sa_wk': _L1_xattn_in['sa_wk'], 'L1_xattn_sa_bk': _L1_xattn_in['sa_bk'], 'L1_xattn_sa_wv': _L1_xattn_in['sa_wv'], 'L1_xattn_sa_bv': _L1_xattn_in['sa_bv'], 'L1_xattn_sa_wo': _L1_xattn_in['sa_wo'], 'L1_xattn_sa_bo': _L1_xattn_in['sa_bo'], 'L1_xattn_sa_g': _L1_xattn_in['sa_g'], 'L1_xattn_sa_b': _L1_xattn_in['sa_b'], 'L1_xattn_ca_wq': _L1_xattn_in['ca_wq'], 'L1_xattn_ca_bq': _L1_xattn_in['ca_bq'], 'L1_xattn_ca_wk': _L1_xattn_in['ca_wk'], 'L1_xattn_ca_bk': _L1_xattn_in['ca_bk'], 'L1_xattn_ca_wv': _L1_xattn_in['ca_wv'], 'L1_xattn_ca_bv': _L1_xattn_in['ca_bv'], 'L1_xattn_ca_wo': _L1_xattn_in['ca_wo'], 'L1_xattn_ca_bo': _L1_xattn_in['ca_bo'], 'L1_xattn_ca_g': _L1_xattn_in['ca_g'], 'L1_xattn_ca_b': _L1_xattn_in['ca_b'], 'L1_xattn_ff_w1': _L1_xattn_in['ff_w1'], 'L1_xattn_ff_b1': _L1_xattn_in['ff_b1'], 'L1_xattn_ff_w2': _L1_xattn_in['ff_w2'], 'L1_xattn_ff_b2': _L1_xattn_in['ff_b2'], 'L1_xattn_ff_g': _L1_xattn_in['ff_g'], 'L1_xattn_ff_b': _L1_xattn_in['ff_b'], 'L2_xattn_A': _L2_xattn_in['A'], 'L2_xattn_Bmat': _L2_xattn_in['Bmat'], 'L2_xattn_Cmat': _L2_xattn_in['Cmat'], 'L2_xattn_W_in': _L2_xattn_in['W_in'], 'L2_xattn_b_in': _L2_xattn_in['b_in'], 'L2_xattn_W_qkv': _L2_xattn_in['W_qkv'], 'L2_xattn_b_qkv': _L2_xattn_in['b_qkv'], 'L2_xattn_W_o': _L2_xattn_in['W_o'], 'L2_xattn_b_o': _L2_xattn_in['b_o'], 'L2_xattn_W_prog': _L2_xattn_in['W_prog'], 'L2_xattn_b_prog': _L2_xattn_in['b_prog'], 'L2_xattn_g1': _L2_xattn_in['g1'], 'L2_xattn_beta1': _L2_xattn_in['beta1'], 'L2_xattn_g2': _L2_xattn_in['g2'], 'L2_xattn_beta2': _L2_xattn_in['beta2'], 'L3_xattn_Wqkv': _L3_xattn_in['Wqkv'], 'L3_xattn_Wo1': _L3_xattn_in['Wo1'], 'L3_xattn_bo1': _L3_xattn_in['bo1'], 'L3_xattn_g1': _L3_xattn_in['g1'], 'L3_xattn_b1': _L3_xattn_in['b1'], 'L3_xattn_Wq': _L3_xattn_in['Wq'], 'L3_xattn_Wk': _L3_xattn_in['Wk'], 'L3_xattn_Wv': _L3_xattn_in['Wv'], 'L3_xattn_Wo2': _L3_xattn_in['Wo2'], 'L3_xattn_bo2': _L3_xattn_in['bo2'], 'L3_xattn_g2': _L3_xattn_in['g2'], 'L3_xattn_b2': _L3_xattn_in['b2'], 'L3_xattn_W1': _L3_xattn_in['W1'], 'L3_xattn_bf1': _L3_xattn_in['bf1'], 'L3_xattn_W2': _L3_xattn_in['W2'], 'L3_xattn_bf2': _L3_xattn_in['bf2'], 'L3_xattn_g3': _L3_xattn_in['g3'], 'L3_xattn_b3': _L3_xattn_in['b3']}

def reference(x, ctx_1024, fside_1x16xSxS2_0, itok_BxS2_4_31999, ctxb_2048x64, mask_BxSxS2_bk1, mask_1xS2_if1, L0_xattn_Wq1, L0_xattn_Wk1, L0_xattn_Wv1, L0_xattn_Wq2, L0_xattn_Wk2, L0_xattn_Wv2, L0_xattn_ln1_g, L0_xattn_ln1_b, L0_xattn_ln2_g, L0_xattn_ln2_b, L0_xattn_ln3_g, L0_xattn_ln3_b, L0_xattn_fc1_w, L0_xattn_fc1_b, L0_xattn_fc2_w, L0_xattn_fc2_b, L1_xattn_attn_2d_bias, L1_xattn_sa_wq, L1_xattn_sa_bq, L1_xattn_sa_wk, L1_xattn_sa_bk, L1_xattn_sa_wv, L1_xattn_sa_bv, L1_xattn_sa_wo, L1_xattn_sa_bo, L1_xattn_sa_g, L1_xattn_sa_b, L1_xattn_ca_wq, L1_xattn_ca_bq, L1_xattn_ca_wk, L1_xattn_ca_bk, L1_xattn_ca_wv, L1_xattn_ca_bv, L1_xattn_ca_wo, L1_xattn_ca_bo, L1_xattn_ca_g, L1_xattn_ca_b, L1_xattn_ff_w1, L1_xattn_ff_b1, L1_xattn_ff_w2, L1_xattn_ff_b2, L1_xattn_ff_g, L1_xattn_ff_b, L2_xattn_A, L2_xattn_Bmat, L2_xattn_Cmat, L2_xattn_W_in, L2_xattn_b_in, L2_xattn_W_qkv, L2_xattn_b_qkv, L2_xattn_W_o, L2_xattn_b_o, L2_xattn_W_prog, L2_xattn_b_prog, L2_xattn_g1, L2_xattn_beta1, L2_xattn_g2, L2_xattn_beta2, L3_xattn_Wqkv, L3_xattn_Wo1, L3_xattn_bo1, L3_xattn_g1, L3_xattn_b1, L3_xattn_Wq, L3_xattn_Wk, L3_xattn_Wv, L3_xattn_Wo2, L3_xattn_bo2, L3_xattn_g2, L3_xattn_b2, L3_xattn_W1, L3_xattn_bf1, L3_xattn_W2, L3_xattn_bf2, L3_xattn_g3, L3_xattn_b3):
    import jax
    import jax.numpy as jnp

    def _L0_xattn_ref(x, context, Wq1, Wk1, Wv1, Wq2, Wk2, Wv2, ln1_g, ln1_b, ln2_g, ln2_b, ln3_g, ln3_b, fc1_w, fc1_b, fc2_w, fc2_b):
        import jax, jax.numpy as jnp
        import numpy as np
        EPS = 1e-05

        def _layernorm(x, g, b):
            m = jnp.mean(x, axis=-1, keepdims=True)
            v = jnp.mean((x - m) ** 2, axis=-1, keepdims=True)
            return (x - m) / jnp.sqrt(v + EPS) * g + b

        def _mha(x, kv, Wq, Wk, Wv, mask, causal):
            m = mask[:, None]
            Q = jnp.einsum('bsd,hdk->bhsk', x, Wq) * m
            K = jnp.einsum('bsd,hdk->bhsk', kv, Wk) * m
            V = jnp.einsum('bsd,hdk->bhsk', kv, Wv) * m
            energy = jnp.einsum('bhsk,bhtk->bhst', Q, K)
            S = energy.shape[-1]
            lengths = jnp.sum(energy[:, :, 0, :] != 0, axis=-1)
            cols = jnp.arange(S)
            energy = jnp.where(cols[None, None, None, :] >= lengths[:, :, None, None], -jnp.inf, energy)
            if causal:
                energy = jnp.where(cols[None, :] > cols[:, None], -jnp.inf, energy)
            dk = Wq.shape[-1]
            score = jax.nn.softmax(energy / jnp.sqrt(jnp.asarray(dk, energy.dtype)), axis=-1)
            out = jnp.einsum('bhst,bhtk->bhsk', score, V) * m
            B, H, Sx, dkk = out.shape
            return out.transpose(0, 2, 1, 3).reshape(B, Sx, H * dkk)
        mask0 = 1.0 - jnp.all(x == 0, axis=2, keepdims=True).astype(x.dtype)
        z = _mha(x, x, Wq1, Wk1, Wv1, mask0, causal=True)
        x1 = _layernorm(x + z, ln1_g, ln1_b)
        mask1 = 1.0 - jnp.all(x1 == 0, axis=2, keepdims=True).astype(x1.dtype)
        z = _mha(x1, context, Wq2, Wk2, Wv2, mask1, causal=False)
        x2 = _layernorm(x1 + z, ln2_g, ln2_b)
        z = jnp.maximum(x2 @ fc1_w.T + fc1_b, 0.0) * mask0
        z = (z @ fc2_w.T + fc2_b) * mask0
        return _layernorm(x2 + z, ln3_g, ln3_b)

    def _L1_xattn_ref(tgt, src, tgt_mask, attn_bias, attn_2d_bias, sa_wq, sa_bq, sa_wk, sa_bk, sa_wv, sa_bv, sa_wo, sa_bo, sa_g, sa_b, ca_wq, ca_bq, ca_wk, ca_bk, ca_wv, ca_bv, ca_wo, ca_bo, ca_g, ca_b, ff_w1, ff_b1, ff_w2, ff_b2, ff_g, ff_b):
        import jax, jax.numpy as jnp
        import numpy as np
        B, L, S, D, H, FF = (2, 256, 256, 128, 16, 512)
        HD = D // H
        TEMP = float(D) ** 0.5
        EPS = 1e-05

        def _layernorm(x, g, b):
            mu = jnp.mean(x, axis=-1, keepdims=True)
            var = jnp.mean(jnp.square(x - mu), axis=-1, keepdims=True)
            return (x - mu) * jax.lax.rsqrt(var + EPS) * g + b

        def _mha(q_in, k_in, v_in, wq, bq, wk, bk, wv, bv, wo, bo, mask, bias):
            b, ql = (q_in.shape[0], q_in.shape[1])
            kl = k_in.shape[1]
            q = (q_in @ wq + bq).reshape(b, ql, H, HD).transpose(0, 2, 1, 3)
            k = (k_in @ wk + bk).reshape(b, kl, H, HD).transpose(0, 2, 1, 3)
            v = (v_in @ wv + bv).reshape(b, kl, H, HD).transpose(0, 2, 1, 3)
            attn = jnp.einsum('bhqd,bhkd->bhqk', q, k) / TEMP
            if bias is not None:
                attn = attn + bias
            if mask is not None:
                attn = jnp.where(mask[:, None, :, :], -jnp.inf, attn)
            attn = jax.nn.softmax(attn, axis=-1)
            out = jnp.einsum('bhqk,bhkd->bhqd', attn, v)
            out = out.transpose(0, 2, 1, 3).reshape(b, ql, H * HD)
            return out @ wo + bo
        att = _mha(tgt, tgt, tgt, sa_wq, sa_bq, sa_wk, sa_bk, sa_wv, sa_bv, sa_wo, sa_bo, tgt_mask, attn_bias)
        out = _layernorm(att + tgt, sa_g, sa_b)
        att = _mha(tgt, src, src, ca_wq, ca_bq, ca_wk, ca_bk, ca_wv, ca_bv, ca_wo, ca_bo, None, attn_2d_bias)
        out = _layernorm(att + out, ca_g, ca_b)
        ff = jax.nn.relu(jax.nn.relu(out @ ff_w1 + ff_b1) @ ff_w2 + ff_b2)
        out = _layernorm(ff + out, ff_g, ff_b)
        return out

    def _L2_xattn_ref(builder_state, base_state, input_ids, program_probs, A, Bmat, Cmat, W_in, b_in, W_qkv, b_qkv, W_o, b_o, W_prog, b_prog, g1, beta1, g2, beta2):
        import jax, jax.numpy as jnp
        import numpy as np
        BATCH, T, H, S, P, NH = (4, 256, 128, 64, 64, 8)
        HD = H // NH

        def _layernorm(x, g, b):
            mu = jnp.mean(x, axis=-1, keepdims=True)
            var = jnp.mean((x - mu) ** 2, axis=-1, keepdims=True)
            return (x - mu) * jax.lax.rsqrt(var + 1e-05) * g + b

        def _mha(q_in, kv_in, W_qkv, b_qkv, W_o, b_o):
            Wq, Wk, Wv = jnp.split(W_qkv, 3, axis=0)
            bq, bk, bv = jnp.split(b_qkv, 3, axis=0)

            def heads(x, W, b):
                y = x @ W.T + b
                return y.reshape(y.shape[0], y.shape[1], NH, HD).transpose(0, 2, 1, 3)
            q, k, v = (heads(q_in, Wq, bq), heads(kv_in, Wk, bk), heads(kv_in, Wv, bv))
            scores = jnp.einsum('bhqd,bhkd->bhqk', q, k) * (1.0 / np.sqrt(HD))
            attn = jax.nn.softmax(scores, axis=-1)
            out = jnp.einsum('bhqk,bhkd->bhqd', attn, v)
            out = out.transpose(0, 2, 1, 3).reshape(q_in.shape)
            return out @ W_o.T + b_o
        residual = builder_state
        x = _layernorm(builder_state, g1, beta1)
        base_n = _layernorm(base_state, g1, beta1)
        x = residual + _mha(x, base_n, W_qkv, b_qkv, W_o, b_o)
        residual = x
        xn = _layernorm(x, g2, beta2)
        U = (xn @ W_in.T + b_in) @ Bmat

        def step(s, u_t):
            s = jax.nn.silu(s @ A.T) + u_t
            return (s, s)
        _, states = jax.lax.scan(step, jnp.zeros((builder_state.shape[0], S), U.dtype), U.transpose(1, 0, 2))
        ssm_out = jnp.einsum('tbs,sh->bth', states, Cmat)
        x = residual + ssm_out
        mod = program_probs.mean(axis=1) @ W_prog.T + b_prog
        return x + mod[:, None, :]

    def _L3_xattn_ref(target, context, target_pad_mask, context_pad_mask, Wqkv, Wo1, bo1, g1, b1, Wq, Wk, Wv, Wo2, bo2, g2, b2, W1, bf1, W2, bf2, g3, b3):
        import jax, jax.numpy as jnp
        import numpy as np
        NEG = 10000000000.0

        def layer_norm(x, g, b, eps):
            m = jnp.mean(x, axis=-1, keepdims=True)
            v = jnp.mean(jnp.square(x - m), axis=-1, keepdims=True)
            return (x - m) * jax.lax.rsqrt(v + eps) * g + b

        def mha(q, k, v, mask, num_heads):
            B, T, E = q.shape
            S = k.shape[1]
            D = E // num_heads
            qh = q.reshape(B, T, num_heads, D).transpose(0, 2, 1, 3)
            kh = k.reshape(B, S, num_heads, D).transpose(0, 2, 1, 3)
            vh = v.reshape(B, S, num_heads, D).transpose(0, 2, 1, 3)
            scores = jnp.einsum('bhqd,bhkd->bhqk', qh, kh) * (1.0 / np.sqrt(D))
            scores = scores * mask - (1.0 - mask) * NEG
            attn = jax.nn.softmax(scores, axis=-1)
            out = jnp.einsum('bhqk,bhkd->bhqd', attn, vh)
            return out.transpose(0, 2, 1, 3).reshape(B, T, E)
        NUM_HEADS = 16
        B, T, E = target.shape
        S = context.shape[1]
        tpad = target_pad_mask.astype(target.dtype)
        cpad = context_pad_mask.astype(target.dtype)
        causal = (jnp.arange(T)[:, None] >= jnp.arange(T)[None, :]).astype(target.dtype)
        self_mask = causal[None, None, :, :] * tpad[:, None, None, :]
        q, k, v = jnp.split(target @ Wqkv, 3, axis=-1)
        x = mha(q, k, v, self_mask, NUM_HEADS) @ Wo1 + bo1
        target = layer_norm(x + target, g1, b1, 1e-05)
        cross_mask = jnp.broadcast_to(cpad[:, None, None, :], (B, 1, 1, S))
        x = mha(target @ Wq, context @ Wk, context @ Wv, cross_mask, NUM_HEADS) @ Wo2 + bo2
        target = layer_norm(x + target, g2, b2, 1e-05)
        h = jax.nn.gelu(target @ W1 + bf1, approximate=False)
        x = h @ W2 + bf2
        return layer_norm(x + target, g3, b3, 1e-06)
    x = _L0_xattn_ref(x, ctx_1024, L0_xattn_Wq1, L0_xattn_Wk1, L0_xattn_Wv1, L0_xattn_Wq2, L0_xattn_Wk2, L0_xattn_Wv2, L0_xattn_ln1_g, L0_xattn_ln1_b, L0_xattn_ln2_g, L0_xattn_ln2_b, L0_xattn_ln3_g, L0_xattn_ln3_b, L0_xattn_fc1_w, L0_xattn_fc1_b, L0_xattn_fc2_w, L0_xattn_fc2_b)
    x = _L1_xattn_ref(x, ctx_1024, mask_BxSxS2_bk1, fside_1x16xSxS2_0, L1_xattn_attn_2d_bias, L1_xattn_sa_wq, L1_xattn_sa_bq, L1_xattn_sa_wk, L1_xattn_sa_bk, L1_xattn_sa_wv, L1_xattn_sa_bv, L1_xattn_sa_wo, L1_xattn_sa_bo, L1_xattn_sa_g, L1_xattn_sa_b, L1_xattn_ca_wq, L1_xattn_ca_bq, L1_xattn_ca_wk, L1_xattn_ca_bk, L1_xattn_ca_wv, L1_xattn_ca_bv, L1_xattn_ca_wo, L1_xattn_ca_bo, L1_xattn_ca_g, L1_xattn_ca_b, L1_xattn_ff_w1, L1_xattn_ff_b1, L1_xattn_ff_w2, L1_xattn_ff_b2, L1_xattn_ff_g, L1_xattn_ff_b)
    x = _L2_xattn_ref(x, ctx_1024, itok_BxS2_4_31999, ctxb_2048x64, L2_xattn_A, L2_xattn_Bmat, L2_xattn_Cmat, L2_xattn_W_in, L2_xattn_b_in, L2_xattn_W_qkv, L2_xattn_b_qkv, L2_xattn_W_o, L2_xattn_b_o, L2_xattn_W_prog, L2_xattn_b_prog, L2_xattn_g1, L2_xattn_beta1, L2_xattn_g2, L2_xattn_beta2)
    x = _L3_xattn_ref(x, ctx_1024, mask_1xS2_if1, mask_1xS2_if1, L3_xattn_Wqkv, L3_xattn_Wo1, L3_xattn_bo1, L3_xattn_g1, L3_xattn_b1, L3_xattn_Wq, L3_xattn_Wk, L3_xattn_Wv, L3_xattn_Wo2, L3_xattn_bo2, L3_xattn_g2, L3_xattn_b2, L3_xattn_W1, L3_xattn_bf1, L3_xattn_W2, L3_xattn_bf2, L3_xattn_g3, L3_xattn_b3)
    return x

_drawn_inputs = setup_inputs


def setup_inputs(seed=0):
    import zlib

    import numpy as np

    out = dict(_drawn_inputs(seed))
    spreads = {'L0_xattn_ln1_g': (1.0, 0.2),
     'L0_xattn_ln1_b': (0.0, 0.1),
     'L0_xattn_ln2_g': (1.0, 0.2),
     'L0_xattn_ln2_b': (0.0, 0.1),
     'L0_xattn_ln3_g': (1.0, 0.2),
     'L0_xattn_ln3_b': (0.0, 0.1),
     'L0_xattn_fc1_b': (0.0, 0.8),
     'L0_xattn_fc2_b': (0.0, 0.1),
     'L1_xattn_sa_bq': (0.0, 0.8),
     'L1_xattn_sa_bk': (0.0, 2.0),
     'L1_xattn_sa_bv': (0.0, 0.43),
     'L1_xattn_sa_bo': (0.0, 0.1),
     'L1_xattn_sa_g': (1.0, 0.2),
     'L1_xattn_sa_b': (0.0, 0.1),
     'L1_xattn_ca_bq': (0.0, 2.0),
     'L1_xattn_ca_bk': (0.0, 2.0),
     'L1_xattn_ca_bv': (0.0, 0.515),
     'L1_xattn_ca_bo': (0.0, 0.1),
     'L1_xattn_ca_g': (1.0, 0.2),
     'L1_xattn_ca_b': (0.0, 0.1),
     'L1_xattn_ff_b1': (0.0, 0.475),
     'L1_xattn_ff_b2': (0.0, 0.1),
     'L1_xattn_ff_g': (1.0, 0.2),
     'L1_xattn_ff_b': (0.0, 0.1),
     'L2_xattn_b_in': (0.0, 0.1),
     'L2_xattn_b_qkv': (0.0, 0.1),
     'L2_xattn_b_o': (0.0, 0.1),
     'L2_xattn_b_prog': (0.0, 0.1),
     'L2_xattn_g1': (1.0, 0.2),
     'L2_xattn_beta1': (0.0, 0.1),
     'L2_xattn_g2': (1.0, 0.2),
     'L2_xattn_beta2': (0.0, 0.1),
     'L3_xattn_bo1': (0.0, 0.1),
     'L3_xattn_g1': (1.0, 0.2),
     'L3_xattn_b1': (0.0, 0.1),
     'L3_xattn_bo2': (0.0, 0.1),
     'L3_xattn_g2': (1.0, 0.2),
     'L3_xattn_b2': (0.0, 0.1),
     'L3_xattn_bf1': (0.0, 0.389),
     'L3_xattn_bf2': (0.0, 0.1),
     'L3_xattn_g3': (1.0, 0.2),
     'L3_xattn_b3': (0.0, 0.1)}
    factors = {'fside_1x16xSxS2_0': 8.0,
     'L0_xattn_Wq1': 8.0,
     'L0_xattn_Wk1': 8.0,
     'L0_xattn_Wq2': 8.0,
     'L0_xattn_Wk2': 8.0,
     'L1_xattn_attn_2d_bias': 31.728,
     'L1_xattn_sa_wq': 8.0,
     'L1_xattn_sa_wk': 8.0,
     'L1_xattn_sa_wv': 3.516,
     'L1_xattn_ca_wq': 8.0,
     'L1_xattn_ca_wk': 8.0,
     'L1_xattn_ca_wv': 3.005,
     'L3_xattn_Wqkv': 8.0,
     'L3_xattn_Wo1': 8.0,
     'L3_xattn_Wq': 8.0,
     'L3_xattn_Wk': 8.0,
     'L3_xattn_Wv': 8.0,
     'L3_xattn_Wo2': 8.0}
    for name, (base, spread) in spreads.items():
        noise = np.random.default_rng([zlib.crc32(name.encode()), seed]).standard_normal(out[name].shape)
        drawn = base * np.exp(spread * noise) if base else spread * noise
        out[name] = jnp.asarray(drawn.astype(out[name].dtype))
    for name, factor in factors.items():
        out[name] = (out[name] * factor).astype(out[name].dtype)
    return out
```

```python
from contextlib import ExitStack

import numpy as np
import concourse.bass as bass
from concourse import mybir

F32 = mybir.dt.float32
BF16 = mybir.dt.bfloat16
ACT = mybir.ActivationFunctionType
ALU = mybir.AluOpType
AX = mybir.AxisListType

P = 128
B = 4
S = 256
QT = S // P
STREAMS = 2
TURNS = B // STREAMS
NS = 64
FF = 512
FC = FF // P
BLOCK = 16
STREAMED = 64
PRIMED = 1
MASKED = -1e30
UNMASKED_MIN = 1e29

WEIGHTS = {
    "l0": [("q1", 128), ("k1", 128), ("v1", 128), ("q2", 128), ("k2", 128), ("v2", 128), ("fc1", 128), ("fc2", 128)],
    "l1": [("q1", 128), ("k1", 128), ("v1", 128), ("o1", 128), ("q2", 128), ("k2", 128), ("v2", 128), ("o2", 128),
           ("ff1", FF), ("ff2", FF)],
    "l2": [("q1", 128), ("k1", 128), ("v1", 128), ("o1", 128), ("in", 128), ("bmat", NS)],
    "l3": [("q1", 128), ("k1", 128), ("v1", 128), ("o1", 128), ("q2", 128), ("k2", 128), ("v2", 128), ("o2", 128),
           ("ff1", FF), ("ff2", FF)],
}
ROWS = ["l0_g1", "l0_b1", "l0_g2", "l0_b2", "l0_g3", "l0_b3", "l0_fc2b",
        "l1_bv1", "l1_bo1", "l1_g1", "l1_b1", "l1_bv2", "l1_bo2", "l1_g2", "l1_b2", "l1_ff2b", "l1_g3", "l1_b3",
        "l2_bv1", "l2_bo1", "l2_g1", "l2_b1", "l2_g2", "l2_b2", "l2_bprog",
        "l3_bo1", "l3_g1", "l3_b1", "l3_bo2", "l3_g2", "l3_b2", "l3_ff2b", "l3_g3", "l3_b3", "zero"]
COLS = ["l0_fc1b", "l1_bq1", "l1_bk1", "l1_bq2", "l1_bk2", "l1_ff1b0", "l1_ff1b1", "l1_ff1b2", "l1_ff1b3",
        "l2_bq1", "l2_bk1", "l2_bin", "l3_ff1b0", "l3_ff1b1", "l3_ff1b2", "l3_ff1b3", "zero"]


class Attention:

    def __init__(self, name, layer, n, heads, scale, mask=None, lengths=False, bias=None, biased_qkv=False,
                 keys="CT"):
        self.name, self.layer, self.n, self.heads, self.scale = name, layer, n, heads, scale
        self.mask, self.lengths, self.bias, self.keys = mask, lengths, bias, keys
        self.width = P // heads
        self.per_quadrant = heads // 4
        self.parts = self.per_quadrant // 2
        self.groups = QT * 2 * self.parts
        self.guard = lengths or bias == 0
        self.bq = f"{layer}_bq{n}" if biased_qkv else "zero"
        self.bk = f"{layer}_bk{n}" if biased_qkv else "zero"
        self.bv = f"{layer}_bv{n}" if biased_qkv else "zero"

    def group(self, g):
        qt, m = divmod(g, 2 * self.parts)
        r, p = divmod(m, 2)
        out = []
        for u in range(2):
            for v in range(2):
                i, j = 2 * p + u, 2 * r + v
                out.append((u, v, i, j))
        return qt, m, out


L0S = Attention("l0s", "l0", 1, 16, 8.0 ** -0.5, mask="causal", lengths=True, keys="XT")
L0C = Attention("l0c", "l0", 2, 16, 8.0 ** -0.5, lengths=True)
L1S = Attention("l1s", "l1", 1, 16, 128.0 ** -0.5, mask="target", bias=0, biased_qkv=True, keys="XT")
L1C = Attention("l1c", "l1", 2, 16, 128.0 ** -0.5, bias=1, biased_qkv=True)
L2A = Attention("l2a", "l2", 1, 8, 0.25, biased_qkv=True)
L3S = Attention("l3s", "l3", 1, 16, 8.0 ** -0.5, mask="self3", keys="XT")
L3C = Attention("l3c", "l3", 2, 16, 8.0 ** -0.5, mask="cross3")


def prepare(a):
    return ["project_q", "project_k", "project_v"] + (["energies0", "lengths"] if a.lengths else [])


def finish(a):
    if a is L0S:
        return ["normalize", "l0_ln1", "apply l0_ln1", "turn X1 XT", "turn CM CT"]
    if a is L0C:
        return ["normalize", "l0_ln2", "apply l0_ln2", "turn X2 ZT", "l0_fc1", "l0_fc2", "apply l0_fc2", "turn X XT"]
    if a is L1S:
        return ["normalize", "turn Z ZT", "out_projection", "apply out_projection", "turn C CT"]
    if a is L1C:
        return ["normalize", "turn Z ZT", "out_projection", "apply out_projection", "turn X2 ZT", "ff1 0", "ff1 1",
                "ff2", "apply ff2", "l2_ln_x", "apply l2_ln_x", "turn X1 XT",
                "l2_ln_base", "apply l2_ln_base", "turn Z CT"]
    if a is L2A:
        return ["normalize", "turn Z ZT", "out_projection", "apply out_projection", "turn X1 XT", "l2_in", "l2_u"]
    if a is L3S:
        return ["normalize", "turn Z ZT", "out_projection", "apply out_projection", "turn X1 XT"]
    return ["normalize", "turn Z ZT", "out_projection", "apply out_projection", "turn X2 ZT", "ff1 0", "ff1 1",
            "ff2", "apply ff2"]


ON_PE = {"project_q", "project_k", "project_v", "energies0", "lengths", "turn", "l0_fc1", "l0_fc2",
         "out_projection", "ff1", "ff2", "l2_in", "l2_u", "mod", "target"}
NORMS = {"l0_ln1", "l0_ln2", "l0_fc2", "out_projection", "ff2", "l2_ln_x", "l2_ln_base"}


class Step:

    def __init__(self, what, stream, attention, job, counts):
        self.what, *self.args = what.split()
        self.s, self.a, self.job = stream, attention, job
        counts["step"] += 1
        self.k = counts["step"]
        self.on_pe = self.what in ON_PE
        if self.on_pe:
            counts["product"] += 1
        self.product = counts["product"]
        if self.what in NORMS:
            counts["norm"] += 1
        self.norm = counts["norm"]


class Plan:

    def __init__(self, attentions, load):
        self.jobs = [(a, s) for a in attentions for s in range(STREAMS)]
        self.base = [sum(a.groups for a, _ in self.jobs[:n]) for n in range(len(self.jobs) + 1)]
        self.groups = self.base[-1]
        self.order = []
        self.counts = {"step": 0, "product": 0, "norm": 0}
        self.operands = {}
        self.normalized = {}
        groups = [(n, g) for n, (a, _) in enumerate(self.jobs) for g in range(a.groups)]
        for s in range(STREAMS):
            for what in load:
                self.step(what, s, None, None)
        self.prepare(0)
        self.order += [("scores", *groups[0]), ("scores", *groups[1])]
        for n, (a, s) in enumerate(self.jobs):
            chain = []
            if n > 0:
                chain += [(w, n - 1) for w in finish(self.jobs[n - 1][0])]
            if n + 1 < len(self.jobs):
                chain += [(w, n + 1) for w in prepare(self.jobs[n + 1][0])]
            places = 3 * (a.groups - 2) + 1
            done, place = 0, 0
            for g in range(a.groups):
                gi = self.base[n] + g
                for part in ("turn", "scores", "values"):
                    if part != "scores":
                        self.order.append((part, n, g))
                    elif gi + 2 < self.groups:
                        self.order.append((part, *groups[gi + 2]))
                    place += 1
                    upto = min(len(chain), -(-len(chain) * place // places))
                    for w, j in chain[done:upto]:
                        self.step(w, self.jobs[j][1], self.jobs[j][0], j)
                    done = max(done, upto)
        n = len(self.jobs) - 1
        for what in finish(self.jobs[n][0]):
            self.step(what, self.jobs[n][1], self.jobs[n][0], n)

    def prepare(self, n):
        for what in prepare(self.jobs[n][0]):
            self.step(what, self.jobs[n][1], self.jobs[n][0], n)

    def step(self, what, s, a, job):
        step = Step(what, s, a, job, self.counts)
        if what.split()[0] in ("project_v", "lengths"):
            self.operands[job] = step.k
        if what == "normalize":
            self.normalized[job] = step.k
        self.order.append(("step", step, None))


PLAN1 = Plan([L0S, L0C, L1S, L1C, L2A], ["load", "turn X XT"])
PLAN3 = Plan([L3S, L3C], ["load3", "mod", "target", "turn X XT", "turn C CT"])


def build(nc, t, tallies):
    ctx = ExitStack()
    with ctx:
        def sb(name, shape, dt=F32):
            return ctx.enter_context(nc.sbuf_tensor(name, shape, dt))

        def pb(name, shape, dt=F32):
            return ctx.enter_context(nc.psum_tensor(name, shape, dt))

        def sem(name):
            return ctx.enter_context(nc.semaphore(name))

        x_all = sb("x_all", [P, B, S])
        c_all = sb("c_all", [P, B, S])
        probs_all = sb("probs_all", [P, B, QT * NS])
        target_mask = sb("target_mask", [P, B, QT * S], mybir.dt.uint8)
        width = {k: sum(n for _, n in v) for k, v in WEIGHTS.items()}
        w_sb = {k: sb(f"w_{k}", [P, width[k]]) for k in WEIGHTS}
        w64 = sb("w64", [NS, 3 * P])
        rows = sb("rows", [P, len(ROWS), P])
        cols = sb("cols", [P, len(COLS)])
        pair_bias = [sb(f"pair_bias{i}", [P, QT, 4, 4 * S]) for i in range(2)]
        mask3_in = sb("mask3_in", [P, S], mybir.dt.int32)
        ident = sb("ident", [P, P])
        head_rows = sb("head_rows", [P, 4 + 2])
        quadrants = sb("quadrants", [P, 4])
        iota = sb("iota", [16, S])
        ident16 = sb("ident16", [P, P], BF16)
        head_select = sb("head_select", [P, 16, P], BF16)
        causal = sb("causal", [P, QT, 2 * S], BF16)
        ones = sb("ones", [P, P])
        minus_half = sb("minus_half", [P, QT])
        key_keep = sb("key_keep", [P, S])
        self3 = sb("self3", [P, QT, 2 * S], BF16)
        cross3 = sb("cross3", [P, QT, 2 * S], BF16)
        tok = {n: [sb(f"{n}{s}", [P, QT, P]) for s in range(STREAMS)] for n in ("X", "X1", "C", "CM")}
        for n in ("X2", "Z"):
            tok[n] = [sb(n, [P, QT, P])] * STREAMS
        tok["O"] = tok["CM"]
        feat = {n: [sb(f"{n}{s}", [P, S]) for s in range(STREAMS)] for n in ("XT", "CT")}
        feat["ZT"] = [sb("ZT", [P, S])] * STREAMS
        hidden = sb("hidden", [P, FC, S])
        row_max = [sb(f"row_max{s}", [P, 2, QT]) for s in range(STREAMS)]
        row_keep = [sb(f"row_keep{s}", [P, 2, QT]) for s in range(STREAMS)]
        target = [sb(f"target{s}", [P, QT, 2 * S], BF16) for s in range(STREAMS)]
        states_b = [sb(f"states_b{s}", [NS, S]) for s in range(STREAMS)]
        probs_b = [sb(f"probs_b{s}", [P, QT, NS]) for s in range(STREAMS)]
        mod_b = [sb(f"mod_b{s}", [NS, P]) for s in range(STREAMS)]
        q_heads = [sb(f"q_heads{i}", [P, 4, S]) for i in range(2)]
        keys = [sb(f"keys{i}", [P, S]) for i in range(2)]
        values = [sb(f"values{i}", [P, QT, 16 * 9 + STREAMED]) for i in range(2)]
        values_l2 = [sb(f"values_l2{i}", [P, QT, 8 * 17 + STREAMED]) for i in range(2)]
        q_row0 = sb("q_row0", [P, 16])
        nonzero = sb("nonzero", [P, QT, 16])
        length_mask = [sb(f"length_mask{i}", [P, S], BF16) for i in range(2)]
        biased = [sb(f"biased{i}", [P, 4, S]) for i in range(2)]
        keep2 = biased[0][:, :, :].rearrange("p (t r) k -> p t (r k)", t=QT)
        causal_in = biased[1][:, 0:2, :]
        minus_max = sb("minus_max", [P, 2, 4])
        minus_max_raw = sb("minus_max_raw", [P, 2, 4])
        probs = [sb(f"probs{i}", [P, 4, S]) for i in range(2)]
        probs_t = [sb(f"probs_t{i}", [P, 4 * S]) for i in range(2)]
        inverse = sb("inverse", [P, QT, 16])
        stats = sb("stats", [P, QT, 6])
        moments = sb("moments", [P, QT, 2])
        variance = sb("variance", [P, QT])
        rstd = sb("rstd", [P, QT])
        unused = sb("unused", [P, 5])
        spacer = sb("spacer", [P, 1])
        eps_tile = {e: sb(f"eps{n}", [P, QT]) for n, e in enumerate((1e-5, 1e-6))}
        centred = sb("centred", [P, QT, P])
        residual = x_all
        u_all = sb("u_all", [NS, B + S * B])
        h_all = pair_bias[0][0:NS, 0, 0, :]
        u_block = [sb(f"u_block{i}", [NS, BLOCK * B]) for i in range(1)]
        h_ring = sb("h_ring", [NS, (BLOCK + 1) * B])

        scores = pb("scores", [P, 4, 512])
        turned = pb("turned", [P, 2, 512])
        mixed = pb("mixed", [P, 512])
        chain_ps = pb("chain_ps", [P, 512])

        loaded = {k: sem(f"loaded_{k}") for k in ("tokens", "consts", "vectors", "l0", "masks", "l1", "bias", "l2", "l3")}
        consts_made = sem("consts_made")
        consts_cast = sem("consts_cast")
        out_stored = sem("out_stored")
        signals = {}
        for ph in (1, 3):
            signals[ph] = {n: sem(f"{n}_p{ph}") for n in (
                "step_done", "product_ready", "variance_ready", "eps_added", "scores_ready",
                "max_ready", "probs_ready", "turned_ready", "kept0", "kept1", "mixed_ready")}
        vector_link = sem("vector_link")
        vector_link1, vector_link3 = sem("vector_link1"), sem("vector_link3")
        drive_ready, h_ready, u_ready, h_saved = sem("drive_ready"), sem("h_ready"), sem("u_ready"), sem("h_saved")
        z_ready, states_ready = sem("z_ready"), sem("states_ready")

        def row(name):
            return rows[:, ROWS.index(name), :].unsqueeze(1).to_broadcast([P, QT, P])

        def col(name):
            i = COLS.index(name)
            return cols[:, i:i + 1]

        def weight(layer, name):
            at = 0
            for n, w in WEIGHTS[layer]:
                if n == name:
                    return w_sb[layer][:, at:at + w]
                at += w
            raise KeyError(name)

        def value_buffer(a, job):
            return (values if a.heads == 16 else values_l2)[job % 2]

        def mask_of(a, s):
            return {"causal": causal, "self3": self3, "cross3": cross3}.get(a.mask, target[s])

        def two(t3):
            return t3[:, :, :].rearrange("p t f -> p (t f)")

        block = ctx.enter_context(nc.Block())

        @block.sync
        def _(sp):
            sp.dma_start(x_all[:, :, :], t["x"]).then_inc(loaded["tokens"], 16)
            sp.dma_start(c_all[:, :, :], t["ctx"]).then_inc(loaded["tokens"], 16)
            for name, dst in (("ident", ident), ("head_rows", head_rows), ("quadrants", quadrants), ("iota", iota)):
                sp.dma_start(dst[:, :], t[name]).then_inc(loaded["consts"], 16)
            sp.dma_start(causal_in, t["causal"]).then_inc(loaded["consts"], 16)
            sp.dma_start(w_sb["l0"][:, :], t["w_l0"]).then_inc(loaded["l0"], 16)
            sp.dma_start(cols[:, :], t["cols"]).then_inc(loaded["vectors"], 16)
            sp.dma_start(rows[:, :, :], t["rows"].partition_broadcast(P)).then_inc(loaded["vectors"], 16)
            sp.dma_start(target_mask[:, :, :], t["target_mask"]).then_inc(loaded["masks"], 16)
            sp.dma_start(mask3_in[:, :], t["mask3"].partition_broadcast(P)).then_inc(loaded["masks"], 16)
            sp.dma_start(w_sb["l1"][:, :], t["w_l1"]).then_inc(loaded["l1"], 16)
            for i in range(2):
                for qt in range(QT):
                    sp.dma_start(pair_bias[i][:, qt], t[f"bias{i}"][:, qt]).then_inc(loaded["bias"], 16)
            sp.dma_start(w_sb["l2"][:, :], t["w_l2"]).then_inc(loaded["l2"], 16)
            sp.dma_start(w64[:, :], t["w64"]).then_inc(loaded["l2"], 16)
            sp.dma_start(probs_all[:, :, :], t["probs"]).then_inc(loaded["l3"], 16)
            sp.dma_start(w_sb["l3"][:, :], t["w_l3"]).then_inc(loaded["l3"], 16)
            with sp.Fori(0, TURNS) as it:
                for s in range(STREAMS):
                    last = [x[1].k for x in PLAN3.order
                            if x[0] == "step" and x[1].args == ["ff2"] and x[1].s == s][-1]
                    sp.wait_ge(signals[3]["step_done"], PRIMED + it * PLAN3.counts["step"] + last)
                    sp.dma_start(t["out"][:, bass.ds(it * (STREAMS * S) + s * S, S)], two(tok["O"][s]))\
                      .then_inc(out_stored, 16)
            sp.wait_ge(out_stored, 16 * (PRIMED + B))

        @block.gpsimd
        def _(pool):
            pool.memset(ones[:, :], 1.0).then_inc(consts_made, 1)
            pool.memset(minus_half[:, :], -0.5).then_inc(consts_made, 1)
            for e, tile in eps_tile.items():
                pool.memset(tile[:, :], e).then_inc(consts_made, 1)
            for i in range(2):
                pool.memset(length_mask[i][:, :], 0.0).then_inc(consts_made, 1)
                pool.memset(values[i][:, :, :], 1.0).then_inc(consts_made, 1)
                pool.memset(values_l2[i][:, :, :], 1.0).then_inc(consts_made, 1)
            pool.memset(u_all[:, 0:B], 0.0).then_inc(consts_made, 1)
            pool.memset(h_ring[:, 0:B], 0.0).then_inc(consts_made, 1)
            for n, primed in enumerate((signals[1]["step_done"], signals[3]["step_done"], h_saved, z_ready)):
                pool.memset(unused[:, n:n + 1], 0.0).then_inc(primed, PRIMED)
            pool.memset(unused[:, 4:5], 0.0).then_inc(out_stored, 16 * PRIMED)
            pool.wait_ge(consts_made, 12)
            for ph, plan in ((1, PLAN1), (3, PLAN3)):
                sig = signals[ph]
                with pool.Fori(0, TURNS) as it:
                    for kind, step, _ in plan.order:
                        if kind != "step" or step.what not in NORMS:
                            continue
                        eps = 1e-6 if ph == 3 and step.what == "ff2" else 1e-5
                        at = it * plan.counts["norm"] + step.norm
                        pool.wait_ge(sig["variance_ready"], at)
                        pool.tensor_tensor(variance[:, :], moments[:, :, 1], eps_tile[eps][:, :], ALU.add)\
                            .then_inc(sig["eps_added"], 1)
                        pool.wait_ge(sig["eps_added"], at)
                        pool.tensor_tensor(rstd[:, :], variance[:, :], minus_half[:, :], ALU.pow)\
                            .then_inc(sig["step_done"], 1)

        def tensor_turn(pe, ph, plan, sig, it):
            def steps_done(k):
                pe.wait_ge(sig["step_done"], PRIMED + it * plan.counts["step"] + k)

            def core_scores(n, g):
                a, s = plan.jobs[n]
                gi = plan.base[n] + g
                qt, m, heads = a.group(g)
                if g == 0:
                    steps_done(plan.operands[n])
                if gi >= 2:
                    pe.wait_ge(sig["probs_ready"], it * plan.groups + gi - 1)
                bank = 2 * (gi % 2)
                masked = a.mask is not None
                if masked:
                    for u in range(2):
                        pe.matmul(scores[:, bank + u, :], ident16[:, :], mask_of(a, s)[:, qt, :],
                                  start=True, stop=False, skip_group_check=True)
                if a.lengths:
                    for u, v, i, j in heads:
                        pe.matmul(scores[:, bank + u, v * S:(v + 1) * S], head_select[:, 4 * i + j, :],
                                  length_mask[n % 2][:, :], start=(not masked and v == 0), stop=False,
                                  skip_group_check=True)
                for v in range(2):
                    for u, vv, i, j in heads:
                        if vv != v:
                            continue
                        last = pe.matmul(scores[:, bank + u, v * S:(v + 1) * S],
                                         q_heads[n % 2][32 * i:32 * i + 32, j, qt * P:(qt + 1) * P],
                                         keys[n % 2][32 * i:32 * i + 32, :],
                                         start=not (masked or a.lengths), stop=True, skip_group_check=True)
                last.then_inc(sig["scores_ready"], 1)

            def core_turn(n, g):
                gi = plan.base[n] + g
                pe.wait_ge(sig["probs_ready"], it * plan.groups + gi + 1)
                for half in range(2):
                    if gi >= 1:
                        pe.wait_ge(sig[f"kept{half}"], it * plan.groups + gi)
                    for q in range(2):
                        for c in range(QT):
                            last = pe.transpose(turned[:, half, q * S + c * P:q * S + (c + 1) * P],
                                                probs[gi % 2][:, 2 * half + q, c * P:(c + 1) * P], ident[:, :])
                    last.then_inc(sig["turned_ready"], 1)

            def core_values(n, g):
                a, s = plan.jobs[n]
                gi = plan.base[n] + g
                qt, m, heads = a.group(g)
                w1 = a.width + 1
                if g == 0 and n > 0:
                    steps_done(plan.normalized[n - 1])
                for pos in range(4):
                    h = 4 * m + pos
                    if pos % 2 == 0:
                        pe.wait_ge(sig[f"kept{pos // 2}"], it * plan.groups + gi + 1)
                    at = qt * a.heads * w1 + h * w1
                    for c in range(QT):
                        last = pe.matmul(mixed[:, at:at + STREAMED],
                                         probs_t[gi % 2][:, pos * S + c * P:pos * S + (c + 1) * P],
                                         value_buffer(a, n)[:, c, h * w1:h * w1 + STREAMED],
                                         start=(c == 0), stop=(c == QT - 1), skip_group_check=True)
                last.then_inc(sig["mixed_ready"], 1)

            def chain_step(st):
                if not st.on_pe:
                    return
                steps_done(st.k - 1)
                s, a, w = st.s, st.a, st.what
                if w == "turn":
                    src = tok[st.args[0]][s]
                    for c in range(QT):
                        last = pe.transpose(chain_ps[:, c * P:(c + 1) * P], src[:, c, :], ident[:, :])
                elif w == "project_q":
                    last = pe.matmul(chain_ps[:, 0:S], weight(a.layer, f"q{a.n}"), feat["XT"][s][:, :],
                                     start=True, stop=True)
                elif w == "project_k":
                    last = pe.matmul(chain_ps[:, 0:S], weight(a.layer, f"k{a.n}"), feat[a.keys][s][:, :],
                                     start=True, stop=True)
                elif w == "project_v":
                    for c in range(QT):
                        last = pe.matmul(chain_ps[:, c * P:(c + 1) * P], feat[a.keys][s][:, c * P:(c + 1) * P],
                                         weight(a.layer, f"v{a.n}"), start=True, stop=True)
                elif w == "energies0":
                    for c in range(QT):
                        last = pe.matmul(chain_ps[:, c * 16:(c + 1) * 16], keys[st.job % 2][:, c * P:(c + 1) * P],
                                         q_row0[:, :], start=True, stop=True)
                elif w == "lengths":
                    for c in range(QT):
                        last = pe.matmul(chain_ps[0:16, 0:1], nonzero[:, c, :], ones[:, 0:1],
                                         start=(c == 0), stop=(c == QT - 1))
                elif w == "out_projection":
                    for c in range(QT):
                        last = pe.matmul(chain_ps[:, c * P:(c + 1) * P], feat["ZT"][s][:, c * P:(c + 1) * P],
                                         weight(a.layer, f"o{a.n}"), start=True, stop=True)
                elif w == "l0_fc1":
                    last = pe.matmul(chain_ps[:, 0:S], weight("l0", "fc1"), feat["ZT"][s][:, :],
                                     start=True, stop=True)
                elif w == "l0_fc2":
                    for c in range(QT):
                        last = pe.matmul(chain_ps[:, c * P:(c + 1) * P], hidden[:, 0, c * P:(c + 1) * P],
                                         weight("l0", "fc2"), start=True, stop=True)
                elif w == "ff1":
                    pair = int(st.args[0])
                    for q in range(2):
                        f = 2 * pair + q
                        last = pe.matmul(chain_ps[:, q * S:(q + 1) * S],
                                         weight(a.layer, "ff1")[:, f * P:(f + 1) * P], feat["ZT"][s][:, :],
                                         start=True, stop=True)
                elif w == "ff2":
                    for c in range(QT):
                        for f in range(FC):
                            last = pe.matmul(chain_ps[:, c * P:(c + 1) * P], hidden[:, f, c * P:(c + 1) * P],
                                             weight(a.layer, "ff2")[:, f * P:(f + 1) * P],
                                             start=(f == 0), stop=(f == FC - 1))
                elif w == "l2_in":
                    last = pe.matmul(chain_ps[:, 0:S], weight("l2", "in"), feat["XT"][s][:, :],
                                     start=True, stop=True)
                elif w == "l2_u":
                    last = pe.matmul(chain_ps[0:NS, 0:S], weight("l2", "bmat"), hidden[:, 0, :],
                                     start=True, stop=True)
                elif w == "mod":
                    for c in range(QT):
                        last = pe.matmul(chain_ps[0:NS, 0:P], probs_b[s][:, c, :], ones[:, :],
                                         start=(c == 0), stop=(c == QT - 1))
                elif w == "target":
                    for c in range(QT):
                        pe.matmul(chain_ps[:, c * P:(c + 1) * P], states_b[s][:, c * P:(c + 1) * P],
                                  w64[:, P:2 * P], start=True, stop=False)
                        last = pe.matmul(chain_ps[:, c * P:(c + 1) * P], mod_b[s][:, :], w64[:, 2 * P:3 * P],
                                         start=False, stop=True)
                last.then_inc(sig["product_ready"], 1)

            if ph == 1:
                pe.wait_ge(loaded["tokens"], 2 * 16)
            for kind, n, g in plan.order:
                if kind == "scores":
                    core_scores(n, g)
                elif kind == "turn":
                    core_turn(n, g)
                elif kind == "values":
                    core_values(n, g)
                else:
                    if n.what == "project_q" and n.a in (L1S, L2A):
                        pe.wait_ge(loaded["l1" if n.a is L1S else "l2"], 16 if n.a is L1S else 2 * 16)
                    chain_step(n)

        def tensor_scan(pe):
            with pe.Fori(0, S // BLOCK) as blk:
                pe.wait_ge(u_ready, blk + 1)
                pe.matmul(chain_ps[:, 0:BLOCK * B], w64[:, 0:P], u_block[0][:, :], start=True, stop=False,
                          skip_group_check=True).then_inc(z_ready, 1)
                for j in range(BLOCK):
                    if j == 0:
                        pe.wait_ge(h_saved, PRIMED + blk)
                    else:
                        pe.wait_ge(h_ready, blk * BLOCK + j)
                    pe.matmul(chain_ps[:, j * B:(j + 1) * B], w64[:, 0:P], h_ring[:, j * B:(j + 1) * B],
                              start=False, stop=(j == BLOCK - 1), skip_group_check=True).then_inc(drive_ready, 1)

        @block.tensor
        def _(pe):
            pe.wait_ge(loaded["consts"], 5 * 16)
            pe.wait_ge(loaded["l0"], 16)
            pe.wait_ge(consts_made, 12)
            pe.wait_ge(consts_cast, 3)
            for ph, plan in ((1, PLAN1), (3, PLAN3)):
                sig = signals[ph]
                if ph == 3:
                    tensor_scan(pe)
                    pe.wait_ge(loaded["l3"], 2 * 16)
                    pe.wait_ge(states_ready, 1)
                with pe.Fori(0, TURNS) as it:
                    tensor_turn(pe, ph, plan, sig, it)

        def scalar_turn(act, ph, plan, sig, it):
            act.wait_ge(sig["step_done"], PRIMED + it * plan.counts["step"])

            def core_exp(n, g):
                a, s = plan.jobs[n]
                gi = plan.base[n] + g
                act.wait_ge(sig["max_ready"], it * plan.groups + gi + 1)
                if gi >= 2:
                    act.wait_ge(sig["turned_ready"], it * (2 * plan.groups) + 2 * (gi - 1))
                for pos in range(4):
                    if a.bias is None:
                        src = scores[:, 2 * (gi % 2) + pos // 2, (pos % 2) * S:(pos % 2 + 1) * S]
                    else:
                        src = biased[gi % 2][:, pos, :]
                    last = act.activation(probs[gi % 2][:, pos, :], src, ACT.Exp,
                                          bias=minus_max[:, gi % 2, pos:pos + 1])
                last.then_inc(sig["probs_ready"], 1)

            def core_keep(n, g, half):
                gi = plan.base[n] + g
                act.wait_ge(sig["turned_ready"], it * (2 * plan.groups) + 2 * gi + half + 1)
                if gi >= 2:
                    act.wait_ge(sig["mixed_ready"], it * plan.groups + gi - 1)
                act.activation(probs_t[gi % 2][:, half * 512:(half + 1) * 512], turned[:, half, :], ACT.Copy)\
                    .then_inc(sig[f"kept{half}"], 1)

            def chain_step(st):
                s, a, w = st.s, st.a, st.what
                if w not in ("turn", "project_k", "l0_fc1", "ff1", "l2_in", "mod"):
                    return
                act.wait_ge(sig["product_ready"], it * plan.counts["product"] + st.product)
                if w == "turn":
                    last = act.activation(feat[st.args[1]][s][:, :], chain_ps[:, 0:S], ACT.Copy)
                elif w == "project_k":
                    last = act.activation(keys[st.job % 2][:, :], chain_ps[:, 0:S], ACT.Identity, bias=col(a.bk))
                elif w == "l0_fc1":
                    last = act.activation(hidden[:, 0, :], chain_ps[:, 0:S], ACT.Relu, bias=col("l0_fc1b"))
                elif w == "ff1":
                    pair = int(st.args[0])
                    for q in range(2):
                        f = 2 * pair + q
                        last = act.activation(hidden[:, f, :], chain_ps[:, q * S:(q + 1) * S],
                                              ACT.Relu if ph == 1 else ACT.Gelu, bias=col(f"{a.layer}_ff1b{f}"))
                elif w == "l2_in":
                    last = act.activation(hidden[:, 0, :], chain_ps[:, 0:S], ACT.Identity, bias=col("l2_bin"))
                elif w == "mod":
                    last = act.activation(mod_b[s][:, :], chain_ps[0:NS, 0:P], ACT.Copy, scale=1.0 / S)
                last.then_inc(sig["step_done"], 1)

            for kind, n, g in plan.order:
                if kind == "scores":
                    core_exp(n, g)
                elif kind == "turn":
                    core_keep(n, g, 0)
                    if plan.jobs[n][0].bias is not None:
                        core_keep(n, g, 1)
                elif kind == "step":
                    chain_step(n)

        def scalar_scan(act):
            with act.Fori(0, S // BLOCK) as blk:
                act.wait_ge(h_saved, PRIMED + blk)
                for j in range(BLOCK):
                    act.wait_ge(drive_ready, blk * BLOCK + j + 1)
                    act.activation(h_ring[:, (j + 1) * B:(j + 2) * B], chain_ps[0:NS, j * B:(j + 1) * B], ACT.Silu)\
                        .then_inc(h_ready, 1)

        @block.scalar
        def _(act):
            act.wait_ge(loaded["vectors"], 2 * 16)
            act.wait_ge(consts_made, 12)
            for ph, plan in ((1, PLAN1), (3, PLAN3)):
                if ph == 3:
                    scalar_scan(act)
                with act.Fori(0, TURNS) as it:
                    scalar_turn(act, ph, plan, signals[ph], it)

        def vector_turn(dve, ph, plan, sig, it, link_sem):
            dve.wait_ge(sig["step_done"], PRIMED + it * plan.counts["step"])
            done = [0]

            def link(ins):
                done[0] += 1
                ins.then_inc(link_sem, 1)
                dve.wait_ge(link_sem, it * tallies.get(ph, 1000) + done[0])

            def core_max(n, g):
                a, s = plan.jobs[n]
                gi = plan.base[n] + g
                qt, m, heads = a.group(g)
                par = gi % 2
                dve.wait_ge(sig["scores_ready"], it * plan.groups + gi + 1)
                src = scores[:, 2 * par:2 * par + 2, :].rearrange("p u (v k) -> p (u v) k", v=2)
                if a.bias is not None:
                    if g == 0:
                        dve.wait_ge(loaded["bias"], 4 * 16)
                    link(dve.tensor_tensor(biased[par][:, :, :], src,
                                           pair_bias[a.bias][:, qt, m, :].rearrange("p (h k) -> p h k", h=4),
                                           ALU.add))
                    src = biased[par][:, :, :]
                out = minus_max_raw if a.guard else minus_max
                last = dve.tensor_reduce(out[:, par, :], src, axis=AX.X, op=ALU.max, negate=True)
                if a.guard:
                    link(last)
                    last = dve.scalar_tensor_tensor(minus_max[:, par, :], minus_max_raw[:, par, :], UNMASKED_MIN,
                                                    minus_max_raw[:, par, :], op0=ALU.is_lt, op1=ALU.mult)
                last.then_inc(sig["max_ready"], 1)

            def core_keep(n, g):
                gi = plan.base[n] + g
                dve.wait_ge(sig["turned_ready"], it * (2 * plan.groups) + 2 * gi + 2)
                if gi >= 2:
                    dve.wait_ge(sig["mixed_ready"], it * plan.groups + gi - 1)
                dve.tensor_copy(probs_t[gi % 2][:, 512:1024], turned[:, 1, :]).then_inc(sig["kept1"], 1)

            def moments_of(src):
                for c in range(QT):
                    last = dve.bn_stats(stats[:, c, :], src[:, c, :])
                link(last)
                dve.memset(spacer[:, :], 0.0)
                for c in range(QT):
                    last = dve.bn_aggr(moments[:, c, :], stats[:, c, :])
                last.then_inc(sig["variance_ready"], 1)

            def layer_norm(src, dst, gain, shift):
                for c in range(QT):
                    last = dve.tensor_scalar(centred[:, c, :], src[:, c, :], moments[:, c, 0:1], rstd[:, c:c + 1],
                                             ALU.subtract, ALU.mult)
                link(last)
                link(dve.tensor_tensor(centred[:, :, :], centred[:, :, :], row(gain), ALU.mult))
                return dve.tensor_tensor(dst[:, :, :], centred[:, :, :], row(shift), ALU.add)

            def keep_rows(dst, src, which):
                for c in range(QT):
                    last = dve.tensor_scalar(dst[:, c, :], src[:, c, :], row_keep_s[:, which, c:c + 1], None,
                                             ALU.mult)
                return last

            def find_rows(src, which, s):
                link(dve.tensor_reduce(row_max[s][:, which, :], src[:, :, :], axis=AX.X, op=ALU.max,
                                       apply_absolute_value=True))
                return dve.tensor_scalar(row_keep[s][:, which, :], row_max[s][:, which, :], 0.0, None,
                                         ALU.not_equal)

            for kind, n, g in plan.order:
                if kind == "scores":
                    core_max(n, g)
                    continue
                if kind == "turn":
                    if plan.jobs[n][0].bias is None:
                        core_keep(n, g)
                    continue
                if kind == "values":
                    continue
                st, s, a, w = n, n.s, n.a, n.what
                row_keep_s = row_keep[s]
                X, X1, X2, Z, C, CM, O = (tok[i][s] for i in ("X", "X1", "X2", "Z", "C", "CM", "O"))
                if w in ("turn", "project_k", "l0_fc1", "ff1", "l2_in", "mod"):
                    continue
                if st.on_pe:
                    dve.wait_ge(sig["product_ready"], it * plan.counts["product"] + st.product)
                elif st.k > 1:
                    dve.wait_ge(sig["step_done"], PRIMED + it * plan.counts["step"] + st.k - 1)
                product = chain_ps[:, 0:S].rearrange("p (t f) -> p t f", t=QT)
                if w == "load":
                    at = it * (STREAMS * S) + s * S
                    flat = x_all[:, :, :].rearrange("p b f -> p (b f)")
                    link(dve.tensor_scalar(two(X), flat[:, bass.ds(at, S)], 1.0, None, ALU.mult))
                    flat = c_all[:, :, :].rearrange("p b f -> p (b f)")
                    dve.tensor_scalar(two(C), flat[:, bass.ds(at, S)], 1.0, None, ALU.mult)
                    flat = target_mask[:, :, :].rearrange("p b f -> p (b f)")
                    at = it * (STREAMS * QT * S) + s * QT * S
                    for c in range(QT):
                        for r in range(2):
                            dve.tensor_scalar(target[s][:, c, r * S:(r + 1) * S],
                                              flat[:, bass.ds(at + c * S, S)], MASKED, None, ALU.mult)
                    last = find_rows(X, 0, s)
                elif w == "project_q":
                    k = a.per_quadrant
                    at = 0 if k == 4 else 4
                    last = dve.tensor_tensor(
                        q_heads[st.job % 2][:, 0:k, :], chain_ps[:, 0:S].unsqueeze(1).to_broadcast([P, k, S]),
                        head_rows[:, at:at + k].unsqueeze(2).to_broadcast([P, k, S]), ALU.mult) \
                        if a.bq == "zero" else dve.scalar_tensor_tensor(
                        q_heads[st.job % 2][:, 0:k, :], chain_ps[:, 0:S].unsqueeze(1).to_broadcast([P, k, S]),
                        col(a.bq), head_rows[:, at:at + k].unsqueeze(2).to_broadcast([P, k, S]),
                        op0=ALU.add, op1=ALU.mult)
                    link(last)
                    flat = q_heads[st.job % 2][:, 0:k, :]
                    last = dve.tensor_scalar(flat, flat, a.scale, None, ALU.mult)
                    if a.lengths:
                        link(last)
                        last = dve.tensor_tensor(
                            q_row0[:, :].rearrange("p (i j) -> p i j", i=4),
                            q_heads[st.job % 2][:, :, 0].unsqueeze(1).to_broadcast([P, 4, 4]),
                            quadrants[:, :].unsqueeze(2).to_broadcast([P, 4, 4]), ALU.mult)
                elif w == "project_v":
                    vb = value_buffer(a, st.job)[:, :, 0:a.heads * (a.width + 1)]\
                        .rearrange("p t (h d) -> p t h d", h=a.heads)
                    for c in range(QT):
                        last = dve.tensor_tensor(
                            vb[:, c, :, 0:a.width], product[:, c, :].rearrange("p (h d) -> p h d", h=a.heads),
                            rows[:, ROWS.index(a.bv), :].rearrange("p (h d) -> p h d", h=a.heads), ALU.add)
                elif w == "energies0":
                    last = dve.tensor_scalar(nonzero[:, :, :].rearrange("p t h -> p (t h)"), chain_ps[:, 0:32],
                                             0.0, None, ALU.not_equal)
                elif w == "lengths":
                    last = dve.tensor_scalar(length_mask[st.job % 2][0:16, :], iota[:, :], chain_ps[0:16, 0:1],
                                             MASKED, ALU.is_ge, ALU.mult)
                elif w == "normalize":
                    dve.wait_ge(sig["mixed_ready"], it * plan.groups + plan.base[st.job + 1])
                    w1 = a.width + 1
                    mx = mixed[:, 0:QT * a.heads * w1].rearrange("p (th d) -> p th d", d=w1)
                    inv = inverse[:, :, :].rearrange("p t h -> p (t h)")[:, 0:QT * a.heads]
                    link(dve.reciprocal(inv, mx[:, :, a.width]))
                    last = dve.tensor_tensor(
                        two(Z).rearrange("p (th d) -> p th d", d=a.width), mx[:, :, 0:a.width],
                        inv.unsqueeze(2).to_broadcast([P, QT * a.heads, a.width]), ALU.mult)
                elif w == "l0_ln1":
                    link(keep_rows(Z, Z, 0))
                    link(dve.tensor_tensor(Z[:, :, :], Z[:, :, :], X[:, :, :], ALU.add))
                    moments_of(Z)
                    continue
                elif w == "l0_ln2":
                    link(keep_rows(Z, Z, 1))
                    link(dve.tensor_tensor(Z[:, :, :], Z[:, :, :], X1[:, :, :], ALU.add))
                    moments_of(Z)
                    continue
                elif w == "l0_fc2":
                    link(dve.tensor_tensor(Z[:, :, :], product, row("l0_fc2b"), ALU.add))
                    link(keep_rows(Z, Z, 0))
                    link(dve.tensor_tensor(Z[:, :, :], Z[:, :, :], X2[:, :, :], ALU.add))
                    moments_of(Z)
                    continue
                elif w == "out_projection":
                    link(dve.tensor_tensor(Z[:, :, :], product, row(f"{a.layer}_bo{a.n}"), ALU.add))
                    old = X if a.n == 1 else X1
                    link(dve.tensor_tensor(Z[:, :, :], Z[:, :, :], old[:, :, :], ALU.add))
                    if a is L2A:
                        flat = residual[:, :, :].rearrange("p b f -> p (b f)")
                        dve.tensor_scalar(flat[:, bass.ds(it * (STREAMS * S) + s * S, S)], two(Z), 1.0, None,
                                          ALU.mult)
                    moments_of(Z)
                    continue
                elif w == "ff2":
                    link(dve.tensor_tensor(Z[:, :, :], product, row(f"{a.layer}_ff2b"), ALU.add))
                    if ph == 1:
                        link(dve.scalar_tensor_tensor(two(Z), two(Z), 0.0, two(X2), op0=ALU.max, op1=ALU.add))
                    else:
                        link(dve.tensor_tensor(Z[:, :, :], Z[:, :, :], X2[:, :, :], ALU.add))
                    moments_of(Z)
                    continue
                elif w == "l2_ln_x":
                    moments_of(X)
                    continue
                elif w == "l2_ln_base":
                    moments_of(C)
                    continue
                elif w == "apply":
                    what = st.args[0]
                    if what == "l0_ln1":
                        link(layer_norm(Z, X1, "l0_g1", "l0_b1"))
                        link(find_rows(X1, 1, s))
                        last = keep_rows(CM, C, 1)
                    elif what == "l0_ln2":
                        last = layer_norm(Z, X2, "l0_g2", "l0_b2")
                    elif what == "l0_fc2":
                        last = layer_norm(Z, X, "l0_g3", "l0_b3")
                    elif what == "out_projection":
                        if a is L2A:
                            last = layer_norm(Z, X1, "l2_g2", "l2_b2")
                        else:
                            last = layer_norm(Z, X1 if a.n == 1 else X2, f"{a.layer}_g{a.n}", f"{a.layer}_b{a.n}")
                    elif what == "ff2" and ph == 1:
                        last = layer_norm(Z, X, "l1_g3", "l1_b3")
                    elif what == "ff2":
                        dve.wait_ge(out_stored, 16 * PRIMED + it * (16 * STREAMS))
                        last = layer_norm(Z, O, "l3_g3", "l3_b3")
                    elif what == "l2_ln_x":
                        last = layer_norm(X, X1, "l2_g1", "l2_b1")
                    else:
                        last = layer_norm(C, Z, "l2_g1", "l2_b1")
                elif w == "l2_u":
                    dst = u_all[:, B:B + S * B].rearrange("p (t b) -> p t b", b=B)
                    last = dve.tensor_scalar(dst[:, :, bass.ds(it * STREAMS + s, 1)],
                                           chain_ps[0:NS, 0:S].unsqueeze(2), 1.0, None, ALU.mult)
                elif w == "load3":
                    b = it * STREAMS + s
                    hv = h_all.rearrange("p (t b) -> p t b", b=B)
                    dve.tensor_scalar(states_b[s][:, :].unsqueeze(2), hv[:, :, bass.ds(b, 1)], 1.0, None, ALU.mult)
                    flat = c_all[:, :, :].rearrange("p b f -> p (b f)")
                    dve.tensor_scalar(two(C), flat[:, bass.ds(b * S, S)], 1.0, None, ALU.mult)
                    flat = probs_all[:, :, :].rearrange("p b f -> p (b f)")
                    last = dve.tensor_scalar(probs_b[s][:, :, :].rearrange("p t f -> p (t f)"),
                                           flat[:, bass.ds(b * (QT * NS), QT * NS)], 1.0, None, ALU.mult)
                elif w == "target":
                    link(dve.tensor_tensor(Z[:, :, :], product, row("l2_bprog"), ALU.add))
                    flat = residual[:, :, :].rearrange("p b f -> p (b f)")
                    last = dve.tensor_tensor(two(X), two(Z), flat[:, bass.ds(it * (STREAMS * S) + s * S, S)],
                                             ALU.add)
                last.then_inc(sig["step_done"], 1)
            tallies[ph] = done[0]

        def vector_scan(dve, link):
            dve.wait_ge(signals[1]["step_done"], PRIMED + TURNS * PLAN1.counts["step"])
            with dve.Fori(0, S // BLOCK) as blk:
                dve.wait_ge(z_ready, PRIMED + blk)
                dve.tensor_scalar(u_block[0][:, :], u_all[:, bass.ds(blk * (BLOCK * B), BLOCK * B)], 1.0, None, ALU.mult)\
                    .then_inc(u_ready, 1)
                dve.wait_ge(h_ready, blk * BLOCK + BLOCK)
                dve.tensor_scalar(h_all[:, bass.ds(blk * (BLOCK * B), BLOCK * B)], h_ring[:, B:(BLOCK + 1) * B], 1.0, None, ALU.mult)
                dve.tensor_copy(h_ring[:, 0:B], h_ring[:, BLOCK * B:(BLOCK + 1) * B]).then_inc(h_saved, 1)
            dve.wait_ge(h_saved, PRIMED + S // BLOCK)
            dve.wait_ge(loaded["l3"], 2 * 16)
            dve.tensor_tensor(h_all, h_all, u_all[:, B:B + S * B], ALU.add).then_inc(states_ready, 1)
            dve.wait_ge(states_ready, 1)

        @block.vector
        def _(dve):
            dve.wait_ge(loaded["tokens"], 2 * 16)
            dve.wait_ge(loaded["consts"], 5 * 16)
            dve.wait_ge(loaded["vectors"], 2 * 16)
            dve.wait_ge(loaded["masks"], 2 * 16)
            dve.wait_ge(consts_made, 12)
            done = [0]

            def link(ins):
                done[0] += 1
                ins.then_inc(vector_link, 1)
                dve.wait_ge(vector_link, done[0])

            dve.tensor_copy(ident16[:, :], ident[:, :]).then_inc(consts_cast, 1)
            dve.tensor_copy(head_select[:, :, :], ident[:, 0:16].unsqueeze(2).to_broadcast([P, 16, P]))\
                .then_inc(consts_cast, 1)
            dve.tensor_copy(causal[:, :, :].rearrange("p t (r k) -> p t r k", r=2),
                            causal_in.unsqueeze(2).to_broadcast([P, QT, 2, S])).then_inc(consts_cast, 1)
            dve.wait_ge(consts_cast, 3)
            link(dve.tensor_copy(key_keep[:, :], mask3_in[:, :]))
            link(dve.tensor_scalar(keep2[:, :, :], causal[:, :, :], 0.0, None, ALU.is_equal))
            link(dve.tensor_tensor(
                keep2[:, :, :].rearrange("p t (r k) -> p (t r) k", r=2),
                keep2[:, :, :].rearrange("p t (r k) -> p (t r) k", r=2),
                key_keep[:, :].unsqueeze(1).to_broadcast([P, 4, S]), ALU.mult))
            link(dve.tensor_scalar(self3[:, :, :], keep2[:, :, :], -MASKED, MASKED, ALU.mult, ALU.add))
            link(dve.tensor_scalar(cross3[:, :, :].rearrange("p t (r k) -> p (t r) k", r=2),
                                   key_keep[:, :].unsqueeze(1).to_broadcast([P, 4, S]),
                                   -MASKED, MASKED, ALU.mult, ALU.add))
            for ph, plan, lk in ((1, PLAN1, vector_link1), (3, PLAN3, vector_link3)):
                if ph == 3:
                    vector_scan(dve, link)
                with dve.Fori(0, TURNS) as it:
                    vector_turn(dve, ph, plan, signals[ph], it, lk)


def _host_arrays(i):
    c = np.ascontiguousarray

    def tokens(v):
        v = v.reshape(B, QT, P, v.shape[-1]).transpose(2, 0, 1, 3)
        return c(v.reshape(P, B, -1))

    def heads(w):
        return w.transpose(1, 0, 2).reshape(P, P)

    def placed(w):
        v = w.reshape(-1, 2, 2, 2, 2, 8).transpose(0, 2, 3, 1, 4, 5)
        return v.reshape(w.shape)

    def chunks(w):
        return w.reshape(FC, P, P).transpose(1, 0, 2).reshape(P, FF)

    def pair(v):
        return c(v.reshape(16, QT, P, S).transpose(2, 1, 0, 3).reshape(P, QT, 4, 4 * S))

    L0, L1, L2, L3 = ({k[len(p):]: v for k, v in i.items() if k.startswith(p)}
                      for p in ("L0_xattn_", "L1_xattn_", "L2_xattn_", "L3_xattn_"))
    out = {
        "x": tokens(i["x"]), "ctx": tokens(i["ctx_1024"]), "probs": tokens(i["ctxb_2048x64"]),
        "target_mask": tokens(i["mask_BxSxS2_bk1"]), "mask3": c(i["mask_1xS2_if1"].reshape(S)),
        "bias0": pair(i["fside_1x16xSxS2_0"]), "bias1": pair(L1["attn_2d_bias"]),
        "w_l0": np.concatenate([placed(heads(L0["Wq1"])), placed(heads(L0["Wk1"])), heads(L0["Wv1"]), placed(heads(L0["Wq2"])),
                                placed(heads(L0["Wk2"])), heads(L0["Wv2"]), L0["fc1_w"].T, L0["fc2_w"].T], 1),
        "w_l1": np.concatenate([placed(L1["sa_wq"]), placed(L1["sa_wk"]), L1["sa_wv"], L1["sa_wo"], placed(L1["ca_wq"]), placed(L1["ca_wk"]),
                                L1["ca_wv"], L1["ca_wo"], L1["ff_w1"], chunks(L1["ff_w2"])], 1),
        "w_l2": np.concatenate([L2["W_qkv"].T, L2["W_o"].T, L2["W_in"].T, L2["Bmat"]], 1),
        "w64": np.concatenate([L2["A"].T, np.zeros((NS, P - NS), np.float32), L2["Cmat"], L2["W_prog"].T], 1),
        "w_l3": np.concatenate([placed(L3["Wqkv"][:, 0:P]), placed(L3["Wqkv"][:, P:2 * P]), L3["Wqkv"][:, 2 * P:],
                                L3["Wo1"], placed(L3["Wq"]), placed(L3["Wk"]), L3["Wv"], L3["Wo2"], L3["W1"],
                                chunks(L3["W2"])], 1),
    }
    zero = np.zeros(P, np.float32)
    by_row = {"l0_g1": L0["ln1_g"], "l0_b1": L0["ln1_b"], "l0_g2": L0["ln2_g"], "l0_b2": L0["ln2_b"],
              "l0_g3": L0["ln3_g"], "l0_b3": L0["ln3_b"], "l0_fc2b": L0["fc2_b"],
              "l1_bv1": L1["sa_bv"], "l1_bo1": L1["sa_bo"], "l1_g1": L1["sa_g"], "l1_b1": L1["sa_b"],
              "l1_bv2": L1["ca_bv"], "l1_bo2": L1["ca_bo"], "l1_g2": L1["ca_g"], "l1_b2": L1["ca_b"],
              "l1_ff2b": L1["ff_b2"], "l1_g3": L1["ff_g"], "l1_b3": L1["ff_b"],
              "l2_bv1": L2["b_qkv"][2 * P:], "l2_bo1": L2["b_o"], "l2_g1": L2["g1"], "l2_b1": L2["beta1"],
              "l2_g2": L2["g2"], "l2_b2": L2["beta2"], "l2_bprog": L2["b_prog"],
              "l3_bo1": L3["bo1"], "l3_g1": L3["g1"], "l3_b1": L3["b1"], "l3_bo2": L3["bo2"], "l3_g2": L3["g2"],
              "l3_b2": L3["b2"], "l3_ff2b": L3["bf2"], "l3_g3": L3["g3"], "l3_b3": L3["b3"], "zero": zero}
    by_col = {"l0_fc1b": L0["fc1_b"], "l1_bq1": placed(L1["sa_bq"]), "l1_bk1": placed(L1["sa_bk"]), "l1_bq2": placed(L1["ca_bq"]),
              "l1_bk2": placed(L1["ca_bk"]), "l2_bq1": L2["b_qkv"][0:P], "l2_bk1": L2["b_qkv"][P:2 * P],
              "l2_bin": L2["b_in"], "zero": zero}
    for f in range(FC):
        by_col[f"l1_ff1b{f}"] = L1["ff_b1"][f * P:(f + 1) * P]
        by_col[f"l3_ff1b{f}"] = L3["bf1"][f * P:(f + 1) * P]
    out["rows"] = np.concatenate([by_row[n] for n in ROWS])
    out["cols"] = np.stack([by_col[n] for n in COLS], 1)
    p, k = np.arange(P), np.arange(S)
    out["ident"] = np.eye(P, dtype=np.float32)
    out["head_rows"] = np.concatenate([((p % 32) // 8)[:, None] == np.arange(4)[None, :],
                                       ((p % 32) // 16)[:, None] == np.arange(2)[None, :]], 1).astype(np.float32)
    out["quadrants"] = ((p // 32)[:, None] == np.arange(4)[None, :]).astype(np.float32)
    out["iota"] = np.tile(k.astype(np.float32), (16, 1))
    q = (np.arange(QT)[None, :] * P + p[:, None])[:, :, None]
    out["causal"] = np.where(k[None, None, :] > q, np.float32(MASKED), np.float32(0))
    return {n: c(v) for n, v in out.items()}


_INPUTS = ["x", "ctx", "probs", "target_mask", "mask3", "bias0", "bias1", "w_l0", "w_l1", "w_l2", "w64", "w_l3",
           "rows", "cols", "ident", "head_rows", "quadrants", "iota", "causal"]


def kernel(**inputs):
    import concourse.bacc as bacc
    from concourse.bass_utils import run_bass_kernel_spmd

    arrays = _host_arrays({k: np.asarray(v) for k, v in inputs.items()})

    def program(tallies):
        nc = bacc.Bacc("TRN2", target_bir_lowering=False, num_devices=1)
        t = {n: nc.dram_tensor(f"in_{n}", arrays[n].shape, mybir.dt.from_np(arrays[n].dtype),
                               kind="ExternalInput").ap() for n in _INPUTS}
        t["out"] = nc.dram_tensor("out_x", (P, B * S), F32, kind="ExternalOutput").ap()
        build(nc, t, tallies)
        return nc

    tallies = {}
    program(tallies)
    nc = program(tallies)
    r = run_bass_kernel_spmd(nc, [{f"in_{n}": arrays[n] for n in _INPUTS}], core_ids=[0])
    out = r.results[0]["out_x"]
    return np.ascontiguousarray(out.reshape(P, B, QT, P).transpose(1, 2, 0, 3).reshape(B, S, P))
```

```python
from contextlib import ExitStack

import numpy as np
import concourse.bass as bass
from concourse import mybir

F32 = mybir.dt.float32
F32R = mybir.dt.float32r
I32 = mybir.dt.int32
BF16 = mybir.dt.bfloat16
ACT = mybir.ActivationFunctionType
ALU = mybir.AluOpType
AX = mybir.AxisListType

P = 128
B = 4
S = 256
QT = S // P
STREAMS = B
NS = 64
FF = 512
FC = FF // P
BLOCK = 16
LANES = 2
SLACK = 0.3
STREAMED = 64
PIECES = 4
UPPER_BITS = -4096
PRIMED = 1
MASKED = -1e30
UNMASKED_MIN = 1e29

WEIGHTS = {
    "l0": [("q1", 128), ("k1", 128), ("v1", 128), ("q2", 128), ("k2", 128), ("v2", 128), ("fc1", 128), ("fc2", 128)],
    "l1": [("q1", 128), ("k1", 128), ("v1", 128), ("o1", 128), ("q2", 128), ("k2", 128), ("v2", 128), ("o2", 128),
           ("ff1", FF), ("ff2", FF)],
    "l2": [("q1", 128), ("k1", 128), ("v1", 128), ("o1", 128), ("in", 128), ("bmat", NS)],
    "l3": [("q1", 128), ("k1", 128), ("v1", 128), ("o1", 128), ("q2", 128), ("k2", 128), ("v2", 128), ("o2", 128),
           ("ff1", FF), ("ff2", FF)],
}
ROWS = ["l0_g1", "l0_b1", "l0_g2", "l0_b2", "l0_g3", "l0_b3", "l0_fc2b",
        "l1_bv1", "l1_bo1", "l1_g1", "l1_b1", "l1_bv2", "l1_bo2", "l1_g2", "l1_b2", "l1_ff2b", "l1_g3", "l1_b3",
        "l2_bv1", "l2_bo1", "l2_g1", "l2_b1", "l2_g2", "l2_b2", "l2_bprog",
        "l3_bo1", "l3_g1", "l3_b1", "l3_bo2", "l3_g2", "l3_b2", "l3_ff2b", "l3_g3", "l3_b3", "zero"]
COLS = ["l0_fc1b", "l1_bq1", "l1_bk1", "l1_bq2", "l1_bk2", "l1_ff1b0", "l1_ff1b1", "l1_ff1b2", "l1_ff1b3",
        "l2_bq1", "l2_bk1", "l2_bin", "l3_ff1b0", "l3_ff1b1", "l3_ff1b2", "l3_ff1b3", "zero"]


class Attention:

    def __init__(self, name, layer, n, heads, scale, mask=None, lengths=False, bias=None, biased_qkv=False,
                 keys="CT"):
        self.name, self.layer, self.n, self.heads, self.scale = name, layer, n, heads, scale
        self.mask, self.lengths, self.bias, self.keys = mask, lengths, bias, keys
        self.width = P // heads
        self.tall = PIECES * self.width
        self.tile_groups = heads // 4
        self.groups = QT * self.tile_groups
        self.guard = lengths or bias == 0
        self.bq = f"{layer}_bq{n}" if biased_qkv else "zero"
        self.bk = f"{layer}_bk{n}" if biased_qkv else "zero"
        self.bv = f"{layer}_bv{n}" if biased_qkv else "zero"

    def group(self, g):
        qt, m = divmod(g, self.tile_groups)
        places = P // self.tall
        out = []
        for u in range(2):
            for v in range(2):
                if places == 4:
                    out.append((u, v, 2 * (m % 2) + u, 2 * (m // 2) + v))
                else:
                    out.append((u, v, u, 2 * m + v))
        return qt, m, out

    def seen(self, qt):
        return P * (qt + 1) if self is L0S else S


L0S = Attention("l0s", "l0", 1, 16, 8.0 ** -0.5, mask="causal", lengths=True, keys="XT")
L0C = Attention("l0c", "l0", 2, 16, 8.0 ** -0.5, lengths=True)
L1S = Attention("l1s", "l1", 1, 16, 128.0 ** -0.5, mask="target", bias=0, biased_qkv=True, keys="XT")
L1C = Attention("l1c", "l1", 2, 16, 128.0 ** -0.5, bias=1, biased_qkv=True)
L2A = Attention("l2a", "l2", 1, 8, 0.25, biased_qkv=True)
L3S = Attention("l3s", "l3", 1, 16, 8.0 ** -0.5, mask="self3", keys="XT")
L3C = Attention("l3c", "l3", 2, 16, 8.0 ** -0.5, mask="cross3")


def prepare(a):
    return (["project_k", "project_q", "project_v"] + (["energies0", "lengths"] if a.lengths else [])
            + (["l2_ln_base", "apply l2_ln_base", "turn CM CT"] if a is L1C else []))


def finish(a):
    if a is L0S:
        return ["normalize", "l0_ln1", "apply l0_ln1", "turn X1 XT", "turn CM CT"]
    if a is L0C:
        return ["normalize", "l0_ln2", "apply l0_ln2", "turn X2 ZT", "l0_fc1", "l0_fc2", "apply l0_fc2", "turn X XT"]
    if a is L1S:
        return ["normalize", "turn Z ZT", "out_projection", "apply out_projection", "turn C CT"]
    if a is L1C:
        return ["normalize", "turn Z ZT", "out_projection", "apply out_projection", "turn X2 ZT", "ff1 0", "ff1 1", "ff1 2", "ff1 3",
                "ff2", "apply ff2", "l2_ln_x", "apply l2_ln_x", "turn X1 XT"]
    if a is L2A:
        return ["normalize", "turn Z ZT", "out_projection", "apply out_projection", "turn X1 XT", "l2_in", "l2_u"]
    if a is L3S:
        return ["normalize", "turn Z ZT", "out_projection", "apply out_projection", "turn X1 XT"]
    return ["normalize", "turn Z ZT", "out_projection", "apply out_projection", "turn X2 ZT", "ff1 0", "ff1 1", "ff1 2", "ff1 3",
            "ff2", "apply ff2"]


ON_PE = {"project_q", "project_k", "project_v", "energies0", "lengths", "turn", "l0_fc1", "l0_fc2",
         "out_projection", "ff1", "ff2", "l2_in", "l2_u", "mod", "target"}
OPERANDS = {"project_q", "project_k", "project_v", "energies0", "lengths"}
READS_EARLY = {"out_projection", "l0_fc2", "ff2", "project_q", "project_k"}
NORMS = {"l0_ln1", "l0_ln2", "l0_fc2", "out_projection", "ff2", "l2_ln_x", "l2_ln_base"}


class Step:

    def __init__(self, what, stream, attention, job, counts, product_before):
        self.what, *self.args = what.split()
        self.s, self.a, self.job = stream, attention, job
        self.lane = stream % LANES
        count = counts[self.lane]
        count["step"] += 1
        self.k = count["step"]
        self.on_pe = self.what in ON_PE
        if self.on_pe:
            count["product"] += 1
        self.product = count["product"]
        self.product_before = product_before
        self.early = 0
        if self.what in READS_EARLY:
            counts[0]["early"] += 1
            self.early = counts[0]["early"]
        if self.what in NORMS:
            count["norm"] += 1
        self.norm = count["norm"]


PE_STEP = {"project_k": 0.5, "project_q": 0.5, "project_v": 0.5, "energies0": 0.5, "lengths": 0.1, "turn": 0.25,
           "l0_fc1": 0.5, "l0_fc2": 0.5, "out_projection": 0.5, "ff1": 0.5, "ff2": 1.8, "l2_in": 0.5, "l2_u": 0.5,
           "mod": 0.5, "target": 0.9}
ACT_STEP = {"turn": 0.35, "l0_fc1": 0.4, "ff1": 0.4, "l2_in": 0.4, "mod": 0.3}
DVE_STEP = {"project_k": 1.3, "project_q": 1.3, "project_v": 0.8, "energies0": 0.2, "lengths": 0.4,
            "normalize": 0.8, "l0_ln1": 2.0, "l0_ln2": 2.0, "l0_fc2": 2.3, "out_projection": 2.0, "ff2": 2.0,
            "l2_ln_x": 1.2, "l2_ln_base": 1.2, "apply": 1.7, "l2_u": 0.4, "target": 0.8, "load": 3.0}
SIGNAL = 0.1
POOL_NORM = 1.0
STACK_PAIR = 5.0
URGENCY = 0.03
CROWDED = 3.0


class Clock:

    def __init__(self):
        self.pe = self.act = self.dve = self.dma = 0.0
        self.lane = [0.0] * LANES
        self.bank = 0.0
        self.exp, self.kept, self.stacked = {}, {}, {}

    def core(self, part, plan, n, g):
        a, _ = plan.jobs[n]
        gi = plan.base[n] + g
        qt = a.group(g)[0]
        share = a.seen(qt) / S
        if part == "scores":
            stacked = self.stacked.get(n, 0.0)
            self.pe = max(self.pe, self.exp.get(gi - 2, 0.0) + SIGNAL, stacked) + 0.43 * share
            self.pe += 0.43 * (a.mask is not None) + 0.43 * a.lengths * share
            self.dve = max(self.dve, self.pe + SIGNAL) + 1.15 * share + 0.2 * a.guard + 1.2 * (a.bias is not None)
            self.act = max(self.act, self.dve + SIGNAL) + 1.5 * share
            self.exp[gi] = self.act
        elif part == "turn":
            self.pe = max(self.pe, self.exp[gi] + SIGNAL) + 0.9 * share
            self.act = max(self.act, self.pe) + 0.5 * share
            if a.bias is None:
                self.dve = max(self.dve, self.pe + SIGNAL) + 0.6 * share
            else:
                self.act += 0.5
            self.kept[gi] = max(self.act, self.dve if a.bias is None else 0.0)
        else:
            self.pe = max(self.pe, self.kept[gi] + SIGNAL) + 1.7 * share

    def fits(self, what, lane, queued):
        what = what.split()[0]
        if self.dve > self.pe + CROWDED and what in DVE_STEP:
            return False
        free = self.pe if what in ON_PE else self.dve
        slack = SLACK + URGENCY * queued
        ready = max(self.lane[lane], self.bank if what in ON_PE else 0.0)
        return ready + SIGNAL <= free + slack

    def step(self, st):
        w, t = st.what, self.lane[st.lane] + SIGNAL
        if st.on_pe:
            self.pe = t = max(self.pe, t, self.bank + SIGNAL) + PE_STEP[w]
            t += SIGNAL
        if w == "normalize":
            t = max(t, self.pe + SIGNAL)
        if w in ACT_STEP:
            self.act = t = max(self.act, t) + ACT_STEP[w]
        else:
            start = max(self.dve, t)
            self.dve = t = start + DVE_STEP[w]
            if st.early:
                self.bank = start + 0.4
        if st.on_pe and not st.early:
            self.bank = t
        if w in NORMS:
            t += POOL_NORM
        self.lane[st.lane] = t
        if w in ("project_q", "project_k"):
            self.dma = max(self.dma, t) + STACK_PAIR
            if w == "project_q":
                self.stacked[st.job] = self.dma + 2.0
                self.dma += 2 * STACK_PAIR


class Plan:

    def __init__(self, attentions, load):
        self.jobs = [(a, s) for a in attentions for s in range(STREAMS)]
        self.base = [sum(a.groups for a, _ in self.jobs[:n]) for n in range(len(self.jobs) + 1)]
        self.groups = self.base[-1]
        self.order = []
        self.counts = [{"step": 0, "product": 0, "norm": 0, "early": 0} for _ in range(LANES)]
        self.operands = {}
        self.normalized = {}
        self.queue = [[] for _ in range(LANES)]
        self.clock = Clock()
        self.product_before = None
        groups = [(n, g) for n, (a, _) in enumerate(self.jobs) for g in range(a.groups)]
        last = len(self.jobs) - 1

        def enter(n, steps):
            self.queue[n % LANES] += [(w, n) for w in steps]

        enter(0, load + prepare(self.jobs[0][0]))
        self.flush(0, "all")
        enter(1, load + prepare(self.jobs[1][0])[:2])
        self.part("scores", *groups[0])
        self.part("scores", *groups[1])
        for n, (a, s) in enumerate(self.jobs):
            for g in range(a.groups):
                gi = self.base[n] + g
                self.part("turn", n, g)
                self.fill()
                if gi + 2 < self.groups:
                    m, h = groups[gi + 2]
                    if h == 0:
                        self.flush(m, "prepare")
                    self.part("scores", m, h)
                    self.fill()
                if g == a.groups - 2 and n + 2 <= last:
                    enter(n + 2, (load if n + 2 < STREAMS else []) + prepare(self.jobs[n + 2][0])[:2])
                if g == 0 and n > 0:
                    self.flush(n - 1, "normalize")
                self.part("values", n, g)
                if g == a.groups - 1:
                    self.queue[n % LANES].insert(0, ("normalize", n))
                    if n + 2 <= last:
                        enter(n + 2, prepare(self.jobs[n + 2][0])[2:])
                    enter(n, finish(a)[1:])
                if gi == 0:
                    enter(1, prepare(self.jobs[1][0])[2:])
                self.fill()
        while any(self.queue):
            lane = min((i for i in range(LANES) if self.queue[i]), key=lambda i: self.clock.lane[i])
            self.pop(lane)

    def part(self, part, n, g):
        self.order.append((part, n, g))
        self.clock.core(part, self, n, g)

    def fill(self):
        for _ in range(2):
            lanes = [i for i in range(LANES) if self.queue[i] and self.clock.fits(self.queue[i][0][0], i, len(self.queue[i]))]
            if not lanes:
                return
            self.pop(max(lanes, key=lambda i: len(self.queue[i])))

    def flush(self, job, until):
        lane = job % LANES
        kinds = {"prepare": OPERANDS, "normalize": {"normalize"}}
        while any(until == "all" or (j == job and w.split()[0] in kinds[until]) for w, j in self.queue[lane]):
            self.pop(lane)

    def pop(self, lane):
        what, job = self.queue[lane].pop(0)
        a, s = self.jobs[job]
        step = Step(what, s, a, job, self.counts, self.product_before)
        if step.on_pe:
            self.product_before = step
        if step.what in ("project_v", "lengths"):
            self.operands[job] = step.k
        if step.what == "normalize":
            self.normalized[job] = step.k
        self.order.append(("step", step, None))
        self.clock.step(step)


PLAN1 = Plan([L0S, L0C, L1S, L1C, L2A], ["load", "turn X XT"])
PLAN3 = Plan([L3S, L3C], ["mod", "target", "turn X XT", "turn C CT"])


def build(nc, t):
    ctx = ExitStack()
    with ctx:
        def sb(name, shape, dt=F32):
            return ctx.enter_context(nc.sbuf_tensor(name, shape, dt))

        def pb(name, shape, dt=F32):
            return ctx.enter_context(nc.psum_tensor(name, shape, dt))

        def sem(name):
            return ctx.enter_context(nc.semaphore(name))

        x_all = sb("x_all", [P, B, S])
        c_all = sb("c_all", [P, B, S])
        target_mask = sb("target_mask", [P, B, QT * S], mybir.dt.uint8)
        width = {k: sum(n for _, n in v) for k, v in WEIGHTS.items()}
        w_sb = {k: sb(f"w_{k}", [P, width[k]]) for k in ("l0", "l1", "l2")}
        w64 = sb("w64", [NS, 3 * P])
        rows = sb("rows", [P, len(ROWS), P])
        cols = sb("cols", [P, len(COLS)])
        pair_bias = [sb(f"pair_bias{i}", [P, QT, 4, 4 * S]) for i in range(2)]
        w_sb["l3"] = pair_bias[1][:, 0, :, :].rearrange("p m k -> p (m k)")[:, 0:width["l3"]]
        probs_all = pair_bias[1][:, 1, 0, 0:B * QT * NS].rearrange("p (b n) -> p b n", b=B)
        mask3_in = pair_bias[1][:, 1, 1, 0:S].bitcast(I32)
        ident = sb("ident", [P, P])
        head_blocks = sb("head_blocks", [P, 16])
        iota = sb("iota", [16, S])
        ident16 = sb("ident16", [P, P], BF16)
        causal = sb("causal", [P, QT, S], BF16)
        ones = sb("ones", [P, P])
        minus_half = sb("minus_half", [P, QT])
        tok = {n: [sb(f"{n}{s}", [P, QT, P]) for s in range(STREAMS)] for n in ("X1",)}
        tok["X"] = [x_all[:, s, :].rearrange("p (t f) -> p t f", t=QT) for s in range(STREAMS)]
        tok["C"] = [c_all[:, s, :].rearrange("p (t f) -> p t f", t=QT) for s in range(STREAMS)]
        tok["O"] = tok["X1"]
        tok["Z"] = [sb(f"Z{s}", [P, QT, P]) for s in range(STREAMS)]
        for n in ("X2", "CM"):
            tok[n] = [sb(f"{n}{i}", [P, QT, P]) for i in range(LANES)] * 2
        feat = {n: [sb(f"{n}{s}", [P, S]) for s in range(STREAMS)] for n in ("XT", "CT")}
        feat["ZT"] = [sb(f"ZT{i}", [P, S]) for i in range(LANES)] * 2
        hidden = [sb(f"hidden{i}", [P, FC, S]) for i in range(LANES)]
        row_max = [sb(f"row_max{s}", [P, 2, QT]) for s in range(STREAMS)]
        row_keep = [sb(f"row_keep{s}", [P, 2, QT]) for s in range(STREAMS)]
        target = [sb(f"target{s}", [P, QT, S], BF16) for s in range(STREAMS)]
        self3, cross3 = target[0:2]
        mod_b = [pair_bias[0][0:NS, 1, 0, s * P:(s + 1) * P] for s in range(STREAMS)]
        split = [sb(f"split{i}", [P, 2, 2, S]) for i in range(LANES)]
        stacked_q = [sb(f"stacked_q{i}", [P, 4, S]) for i in range(2)]
        stacked_k = [sb(f"stacked_k{i}", [P, 4, S]) for i in range(2)]
        values = [sb(f"values{i}", [P, QT, 16 * 9 + STREAMED]) for i in range(2)]
        values_l2 = [sb(f"values_l2{i}", [P, QT, 8 * 17 + STREAMED]) for i in range(2)]
        q_row0 = [sb(f"q_row0{i}", [P, 16]) for i in range(LANES)]
        nonzero = [sb(f"nonzero{i}", [P, QT, 16]) for i in range(LANES)]
        length_mask = [sb(f"length_mask{i}", [P, S], BF16) for i in range(2)]
        biased = [sb(f"biased{i}", [P, 4, S]) for i in range(2)]
        keep2 = biased[0][:, 0:2, :]
        key_keep = biased[0][:, 2, :]
        causal_in = biased[1][:, 0:2, :]
        minus_max = sb("minus_max", [P, 2, 4])
        minus_max_raw = sb("minus_max_raw", [P, 2, 4])
        probs = [sb(f"probs{i}", [P, 4, S]) for i in range(2)]
        probs_t = [sb(f"probs_t{i}", [P, 4 * S]) for i in range(2)]
        inverse = [sb(f"inverse{i}", [P, QT, 16]) for i in range(LANES)]
        stats = [sb(f"stats{i}", [P, QT, 6]) for i in range(LANES)]
        moments = [sb(f"moments{i}", [P, QT, 2]) for i in range(LANES)]
        variance = [sb(f"variance{i}", [P, QT]) for i in range(LANES)]
        rstd = [sb(f"rstd{i}", [P, QT]) for i in range(LANES)]
        unused = sb("unused", [P, 5])
        spacer = sb("spacer", [P, 1])
        eps_tile = {e: sb(f"eps{n}", [P, QT]) for n, e in enumerate((1e-5, 1e-6))}
        centred = [sb(f"centred{i}", [P, QT, P]) for i in range(LANES)]
        h_all = pair_bias[0][0:NS, 0, 0, :]
        u_all = pair_bias[0][0:NS, 0, 1:3, :].rearrange("p m k -> p (m k)")[:, 0:B + S * B]
        u_block = [sb(f"u_block{i}", [NS, BLOCK * B]) for i in range(1)]
        h_ring = sb("h_ring", [NS, (BLOCK + 1) * B])

        scores = pb("scores", [P, 4, 512])
        turned = pb("turned", [P, 2, 512])
        mixed = pb("mixed", [P, 512])
        chain_ps = pb("chain_ps", [P, 512])

        loaded = {k: sem(f"loaded_{k}") for k in ("tokens", "consts", "vectors", "l0", "masks", "mask3", "l1", "bias", "l2", "l3")}
        consts_made = sem("consts_made")
        consts_cast = sem("consts_cast")
        out_stored = sem("out_stored")
        signals = {}
        for ph in (1, 3):
            signals[ph] = {n: sem(f"{n}_p{ph}") for n in (
                "step_done0", "step_done1", "product_ready0", "product_ready1", "variance_ready0",
                "variance_ready1", "product_read", "eps_added", "scores_ready",
                "max_ready", "probs_ready", "turned_ready", "kept0", "kept1", "mixed_ready",
                "stacked0_pair0", "stacked0_pair1", "stacked1_pair0", "stacked1_pair1")}
        vector_link = sem("vector_link")
        vector_link1, vector_link3 = sem("vector_link1"), sem("vector_link3")
        drive_ready, h_ready, u_ready, h_saved = sem("drive_ready"), sem("h_ready"), sem("u_ready"), sem("h_saved")
        z_ready, states_ready = sem("z_ready"), sem("states_ready")

        def row(name):
            return rows[:, ROWS.index(name), :].unsqueeze(1).to_broadcast([P, QT, P])

        def col(name):
            i = COLS.index(name)
            return cols[:, i:i + 1]

        def weight(layer, name):
            at = 0
            for n, w in WEIGHTS[layer]:
                if n == name:
                    return w_sb[layer][:, at:at + w]
                at += w
            raise KeyError(name)

        def value_buffer(a, job):
            return (values if a.heads == 16 else values_l2)[job % 2]

        def mask_of(a, s):
            return {"causal": causal, "self3": self3, "cross3": cross3}.get(a.mask, target[s])

        def kept_part(half, a, g):
            return half.rearrange("p (h k) -> p h k", h=2)[:, :, 0:a.seen(a.group(g)[0])]

        def stacked_by(n):
            return 16 * 2 * PIECES * 2 * (n // 2 + 1)

        def two(t3):
            return t3[:, :, :].rearrange("p t f -> p (t f)")

        block = ctx.enter_context(nc.Block())

        def stack_operands(sp, plan, sig, ph):
            set_done = {}
            for kind, st, _ in plan.order:
                if kind == "step" and st.what in ("project_q", "project_k"):
                    set_done[st.job, st.what] = st
            for n in range(len(plan.jobs)):
                a, lane = plan.jobs[n][0], set_done[n, "project_k"].lane
                if ph == 1 and a is L2A and n == 4 * STREAMS + 2:
                    sp.wait_ge(sig["max_ready"], plan.base[4 * STREAMS])
                    sp.dma_start(mask3_in, t["mask3"].partition_broadcast(P)).then_inc(loaded["mask3"], 16)
                    sp.dma_start(probs_all, t["probs"]).then_inc(loaded["l3"], 16)
                    sp.dma_start(w_sb["l3"], t["w_l3"]).then_inc(loaded["l3"], 16)
                if n >= 2:
                    sp.wait_ge(sig["scores_ready"], plan.base[n - 1])
                for pair in range(2):
                    for queries in (0, 1):
                        if pair == 0:
                            sp.wait_ge(sig[f"step_done{lane}"], set_done[n, "project_q" if queries else "project_k"].k)
                        dst = (stacked_q if queries else stacked_k)[n % 2]
                        for piece in range(PIECES):
                            part = piece // 2 if queries else piece % 2
                            for j in (2 * pair, 2 * pair + 1):
                                sp.dma_start(dst[piece:P:PIECES, j, :],
                                             split[lane][32 * j:32 * (j + 1), 1 - queries, part, :])\
                                    .then_inc(sig[f"stacked{n % 2}_pair{pair}"], 16)

        @block.sync
        def _(sp):
            sp.dma_start(x_all[:, :, :], t["x"]).then_inc(loaded["tokens"], 16)
            sp.dma_start(c_all[:, :, :], t["ctx"]).then_inc(loaded["tokens"], 16)
            for name, dst in (("ident", ident), ("head_blocks", head_blocks), ("iota", iota)):
                sp.dma_start(dst[:, :], t[name]).then_inc(loaded["consts"], 16)
            sp.dma_start(causal_in, t["causal"]).then_inc(loaded["consts"], 16)
            sp.dma_start(w_sb["l0"][:, :], t["w_l0"]).then_inc(loaded["l0"], 16)
            sp.dma_start(cols[:, :], t["cols"]).then_inc(loaded["vectors"], 16)
            sp.dma_start(rows[:, :, :], t["rows"].partition_broadcast(P)).then_inc(loaded["vectors"], 16)
            sp.dma_start(target_mask[:, :, :], t["target_mask"]).then_inc(loaded["masks"], 16)
            sp.dma_start(w_sb["l1"][:, :], t["w_l1"]).then_inc(loaded["l1"], 16)
            for i in range(2):
                for qt in range(QT):
                    sp.dma_start(pair_bias[i][:, qt], t[f"bias{i}"][:, qt]).then_inc(loaded["bias"], 16)
            sp.dma_start(w_sb["l2"][:, :], t["w_l2"]).then_inc(loaded["l2"], 16)
            sp.dma_start(w64[:, :], t["w64"]).then_inc(loaded["l2"], 16)
            for ph, plan in ((1, PLAN1), (3, PLAN3)):
                stack_operands(sp, plan, signals[ph], ph)
            for s in range(STREAMS):
                last = [x[1].k for x in PLAN3.order
                        if x[0] == "step" and x[1].args == ["ff2"] and x[1].s == s][-1]
                sp.wait_ge(signals[3][f"step_done{s % LANES}"], last)
                sp.dma_start(t["out"][:, s * S:(s + 1) * S], two(tok["O"][s])).then_inc(out_stored, 16)
            sp.wait_ge(out_stored, 16 * B)

        @block.gpsimd
        def _(pool):
            pool.memset(ones[:, :], 1.0).then_inc(consts_made, 1)
            pool.memset(minus_half[:, :], -0.5).then_inc(consts_made, 1)
            for e, tile in eps_tile.items():
                pool.memset(tile[:, :], e).then_inc(consts_made, 1)
            for i in range(2):
                pool.memset(length_mask[i][:, :], 0.0).then_inc(consts_made, 1)
                pool.memset(values[i][:, :, :], 1.0).then_inc(consts_made, 1)
                pool.memset(values_l2[i][:, :, :], 1.0).then_inc(consts_made, 1)
            pool.memset(h_ring[:, 0:B], 0.0).then_inc(consts_made, 1)
            for n, primed in enumerate((h_saved, z_ready)):
                pool.memset(unused[:, n:n + 1], 0.0).then_inc(primed, PRIMED)
            pool.wait_ge(consts_made, 11)
            for ph, plan in ((1, PLAN1), (3, PLAN3)):
                sig = signals[ph]
                norms = 0
                for kind, step, _ in plan.order:
                    if kind != "step" or step.what not in NORMS:
                        continue
                    eps = 1e-6 if ph == 3 and step.what == "ff2" else 1e-5
                    lane = step.lane
                    norms += 1
                    pool.wait_ge(sig[f"variance_ready{lane}"], step.norm)
                    pool.tensor_tensor(variance[lane][:, :], moments[lane][:, :, 1], eps_tile[eps][:, :], ALU.add)\
                        .then_inc(sig["eps_added"], 1)
                    pool.wait_ge(sig["eps_added"], norms)
                    pool.tensor_tensor(rstd[lane][:, :], variance[lane][:, :], minus_half[:, :], ALU.pow)\
                        .then_inc(sig[f"step_done{lane}"], 1)

        def tensor_phase(pe, ph, plan, sig):
            def steps_done(lane, k):
                if k > 0:
                    pe.wait_ge(sig[f"step_done{lane}"], k)

            def core_scores(n, g):
                a, s = plan.jobs[n]
                gi = plan.base[n] + g
                qt, m, heads = a.group(g)
                if g == 0:
                    steps_done(n % LANES, plan.operands[n])
                    pe.wait_ge(sig[f"stacked{n % 2}_pair0"], stacked_by(n))
                if g == a.tile_groups // 2:
                    pe.wait_ge(sig[f"stacked{n % 2}_pair1"], stacked_by(n))
                if gi >= 2:
                    pe.wait_ge(sig["probs_ready"], gi - 1)
                bank = 2 * (gi % 2)
                seen = a.seen(qt)
                masked = a.mask is not None
                if a.lengths:
                    for u, v, i, j in heads:
                        h = 4 * j + i
                        pe.matmul(scores[:, bank + u, v * S:v * S + seen], ident16[:, h:h + 1].to_broadcast([P, P]),
                                  length_mask[n % 2][:, 0:seen], start=(v == 0), stop=False,
                                  skip_group_check=True)
                    if masked:
                        for u in range(2):
                            pe.matmul(scores[:, bank + u, :].rearrange("p (v k) -> p v k", v=2)[:, :, seen - P:seen],
                                      ident16[:, :],
                                      causal[:, qt, seen - P:seen].unsqueeze(1).to_broadcast([P, 2, P]),
                                      start=False, stop=False, skip_group_check=True)
                elif masked:
                    for u in range(2):
                        pe.matmul(scores[:, bank + u, :].rearrange("p (v k) -> p v k", v=2), ident16[:, :],
                                  mask_of(a, s)[:, qt, :].unsqueeze(1).to_broadcast([P, 2, S]),
                                  start=True, stop=False, skip_group_check=True)
                for v in range(2):
                    for u, vv, i, j in heads:
                        if vv != v:
                            continue
                        at = a.tall * i
                        last = pe.matmul(scores[:, bank + u, v * S:v * S + seen],
                                         stacked_q[n % 2][at:at + a.tall, j, qt * P:(qt + 1) * P].bitcast(F32R),
                                         stacked_k[n % 2][at:at + a.tall, j, 0:seen].bitcast(F32R),
                                         start=not (masked or a.lengths), stop=True, skip_group_check=True)
                last.then_inc(sig["scores_ready"], 1)

            def core_turn(n, g):
                gi = plan.base[n] + g
                a = plan.jobs[n][0]
                seen = a.seen(a.group(g)[0])
                pe.wait_ge(sig["probs_ready"], gi + 1)
                for half in range(2):
                    if gi >= 1:
                        pe.wait_ge(sig[f"kept{half}"], gi)
                    for q in range(2):
                        for c in range(seen // P):
                            last = pe.transpose(turned[:, half, q * S + c * P:q * S + (c + 1) * P],
                                                probs[gi % 2][:, 2 * half + q, c * P:(c + 1) * P], ident[:, :])
                    last.then_inc(sig["turned_ready"], 1)

            def core_values(n, g):
                a, s = plan.jobs[n]
                gi = plan.base[n] + g
                qt, m, heads = a.group(g)
                tiles = a.seen(qt) // P
                w1 = a.width + 1
                if g == 0 and n > 0:
                    steps_done((n - 1) % LANES, plan.normalized[n - 1])
                for pos in range(4):
                    h = 4 * m + pos
                    if pos % 2 == 0:
                        pe.wait_ge(sig[f"kept{pos // 2}"], gi + 1)
                    at = qt * a.heads * w1 + h * w1
                    for c in range(tiles):
                        last = pe.matmul(mixed[:, at:at + STREAMED],
                                         probs_t[gi % 2][:, pos * S + c * P:pos * S + (c + 1) * P],
                                         value_buffer(a, n)[:, c, h * w1:h * w1 + STREAMED],
                                         start=(c == 0), stop=(c == tiles - 1), skip_group_check=True)
                last.then_inc(sig["mixed_ready"], 1)

            def chain_step(st):
                if not st.on_pe:
                    return
                steps_done(st.lane, st.k - 1)
                before = st.product_before
                if before is not None and before.early:
                    pe.wait_ge(sig["product_read"], before.early)
                elif before is not None and before.lane != st.lane:
                    steps_done(before.lane, before.k)
                s, a, w = st.s, st.a, st.what
                if w == "turn":
                    src = tok[st.args[0]][s]
                    for c in range(QT):
                        last = pe.transpose(chain_ps[:, c * P:(c + 1) * P], src[:, c, :], ident[:, :])
                elif w == "project_q":
                    last = pe.matmul(chain_ps[:, 0:S], weight(a.layer, f"q{a.n}"), feat["XT"][s][:, :],
                                     start=True, stop=True)
                elif w == "project_k":
                    last = pe.matmul(chain_ps[:, 0:S], weight(a.layer, f"k{a.n}"), feat[a.keys][s][:, :],
                                     start=True, stop=True)
                elif w == "project_v":
                    for c in range(QT):
                        last = pe.matmul(chain_ps[:, c * P:(c + 1) * P], feat[a.keys][s][:, c * P:(c + 1) * P],
                                         weight(a.layer, f"v{a.n}"), start=True, stop=True)
                elif w == "energies0":
                    for c in range(QT):
                        for part in range(2):
                            last = pe.matmul(chain_ps[:, c * 16:(c + 1) * 16],
                                             split[st.lane][:, 1, part, c * P:(c + 1) * P], q_row0[st.lane][:, :],
                                             start=(part == 0), stop=(part == 1))
                elif w == "lengths":
                    for c in range(QT):
                        last = pe.matmul(chain_ps[0:16, 0:1], nonzero[st.lane][:, c, :], ones[:, 0:1],
                                         start=(c == 0), stop=(c == QT - 1))
                elif w == "out_projection":
                    for c in range(QT):
                        last = pe.matmul(chain_ps[:, c * P:(c + 1) * P], feat["ZT"][s][:, c * P:(c + 1) * P],
                                         weight(a.layer, f"o{a.n}"), start=True, stop=True)
                elif w == "l0_fc1":
                    last = pe.matmul(chain_ps[:, 0:S], weight("l0", "fc1"), feat["ZT"][s][:, :],
                                     start=True, stop=True)
                elif w == "l0_fc2":
                    for c in range(QT):
                        last = pe.matmul(chain_ps[:, c * P:(c + 1) * P], hidden[st.lane][:, 0, c * P:(c + 1) * P],
                                         weight("l0", "fc2"), start=True, stop=True)
                elif w == "ff1":
                    f = int(st.args[0])
                    last = pe.matmul(chain_ps[:, 0:S], weight(a.layer, "ff1")[:, f * P:(f + 1) * P],
                                     feat["ZT"][s][:, :], start=True, stop=True)
                elif w == "ff2":
                    for c in range(QT):
                        for f in range(FC):
                            last = pe.matmul(chain_ps[:, c * P:(c + 1) * P], hidden[st.lane][:, f, c * P:(c + 1) * P],
                                             weight(a.layer, "ff2")[:, f * P:(f + 1) * P],
                                             start=(f == 0), stop=(f == FC - 1))
                elif w == "l2_in":
                    last = pe.matmul(chain_ps[:, 0:S], weight("l2", "in"), feat["XT"][s][:, :],
                                     start=True, stop=True)
                elif w == "l2_u":
                    last = pe.matmul(chain_ps[0:NS, 0:S], weight("l2", "bmat"), hidden[st.lane][:, 0, :],
                                     start=True, stop=True)
                elif w == "mod":
                    for c in range(QT):
                        last = pe.matmul(chain_ps[0:NS, 0:P], probs_all[:, s, c * NS:(c + 1) * NS], ones[:, :],
                                         start=(c == 0), stop=(c == QT - 1))
                elif w == "target":
                    for c in range(QT):
                        pe.matmul(chain_ps[:, c * P:(c + 1) * P], h_all.rearrange("p (t b) -> p t b", b=B)[:, c * P:(c + 1) * P, s],
                                  w64[:, P:2 * P], start=True, stop=False)
                        last = pe.matmul(chain_ps[:, c * P:(c + 1) * P], mod_b[s], w64[:, 2 * P:3 * P],
                                         start=False, stop=True)
                last.then_inc(sig[f"product_ready{st.lane}"], 1)

            if ph == 1:
                pe.wait_ge(loaded["tokens"], 2 * 16)
            for kind, n, g in plan.order:
                if kind == "scores":
                    core_scores(n, g)
                elif kind == "turn":
                    core_turn(n, g)
                elif kind == "values":
                    core_values(n, g)
                else:
                    if n.what == "project_q" and n.a in (L1S, L2A):
                        pe.wait_ge(loaded["l1" if n.a is L1S else "l2"], 16 if n.a is L1S else 2 * 16)
                    chain_step(n)

        def tensor_scan(pe):
            with pe.Fori(0, S // BLOCK) as blk:
                pe.wait_ge(u_ready, blk + 1)
                pe.matmul(chain_ps[:, 0:BLOCK * B], w64[:, 0:P], u_block[0][:, :], start=True, stop=False,
                          skip_group_check=True).then_inc(z_ready, 1)
                for j in range(BLOCK):
                    if j == 0:
                        pe.wait_ge(h_saved, PRIMED + blk)
                    else:
                        pe.wait_ge(h_ready, blk * BLOCK + j)
                    pe.matmul(chain_ps[:, j * B:(j + 1) * B], w64[:, 0:P], h_ring[:, j * B:(j + 1) * B],
                              start=False, stop=(j == BLOCK - 1), skip_group_check=True).then_inc(drive_ready, 1)

        @block.tensor
        def _(pe):
            pe.wait_ge(loaded["consts"], 4 * 16)
            pe.wait_ge(loaded["l0"], 16)
            pe.wait_ge(consts_made, 11)
            pe.wait_ge(consts_cast, 2)
            for ph, plan in ((1, PLAN1), (3, PLAN3)):
                sig = signals[ph]
                if ph == 3:
                    tensor_scan(pe)
                    pe.wait_ge(loaded["l3"], 2 * 16)
                    pe.wait_ge(states_ready, 1)
                tensor_phase(pe, ph, plan, sig)

        def scalar_phase(act, ph, plan, sig):
            def core_exp(n, g):
                a, s = plan.jobs[n]
                gi = plan.base[n] + g
                act.wait_ge(sig["max_ready"], gi + 1)
                if gi >= 2:
                    act.wait_ge(sig["turned_ready"], 2 * (gi - 1))
                seen = a.seen(a.group(g)[0])
                for pos in range(4):
                    if a.bias is None:
                        src = scores[:, 2 * (gi % 2) + pos // 2, (pos % 2) * S:(pos % 2) * S + seen]
                    else:
                        src = biased[gi % 2][:, pos, :]
                    last = act.activation(probs[gi % 2][:, pos, 0:seen], src, ACT.Exp,
                                          bias=minus_max[:, gi % 2, pos:pos + 1])
                last.then_inc(sig["probs_ready"], 1)

            def core_keep(n, g, half):
                gi = plan.base[n] + g
                act.wait_ge(sig["turned_ready"], 2 * gi + half + 1)
                if gi >= 2:
                    act.wait_ge(sig["mixed_ready"], gi - 1)
                a = plan.jobs[n][0]
                act.activation(kept_part(probs_t[gi % 2][:, half * 512:(half + 1) * 512], a, g),
                               kept_part(turned[:, half, :], a, g), ACT.Copy)\
                    .then_inc(sig[f"kept{half}"], 1)

            def chain_step(st):
                s, a, w = st.s, st.a, st.what
                if w not in ("turn", "l0_fc1", "ff1", "l2_in", "mod"):
                    return
                act.wait_ge(sig[f"product_ready{st.lane}"], st.product)
                if w == "turn":
                    last = act.activation(feat[st.args[1]][s][:, :], chain_ps[:, 0:S], ACT.Copy)
                elif w == "l0_fc1":
                    last = act.activation(hidden[st.lane][:, 0, :], chain_ps[:, 0:S], ACT.Relu, bias=col("l0_fc1b"))
                elif w == "ff1":
                    f = int(st.args[0])
                    last = act.activation(hidden[st.lane][:, f, :], chain_ps[:, 0:S],
                                          ACT.Relu if ph == 1 else ACT.Gelu, bias=col(f"{a.layer}_ff1b{f}"))
                elif w == "l2_in":
                    last = act.activation(hidden[st.lane][:, 0, :], chain_ps[:, 0:S], ACT.Identity, bias=col("l2_bin"))
                elif w == "mod":
                    last = act.activation(mod_b[s], chain_ps[0:NS, 0:P], ACT.Copy, scale=1.0 / S)
                last.then_inc(sig[f"step_done{st.lane}"], 1)

            for kind, n, g in plan.order:
                if kind == "scores":
                    core_exp(n, g)
                elif kind == "turn":
                    core_keep(n, g, 0)
                    if plan.jobs[n][0].bias is not None:
                        core_keep(n, g, 1)
                elif kind == "step":
                    chain_step(n)

        def scalar_scan(act):
            with act.Fori(0, S // BLOCK) as blk:
                act.wait_ge(h_saved, PRIMED + blk)
                for j in range(BLOCK):
                    act.wait_ge(drive_ready, blk * BLOCK + j + 1)
                    act.activation(h_ring[:, (j + 1) * B:(j + 2) * B], chain_ps[0:NS, j * B:(j + 1) * B], ACT.Silu)\
                        .then_inc(h_ready, 1)

        @block.scalar
        def _(act):
            act.wait_ge(loaded["vectors"], 2 * 16)
            act.wait_ge(consts_made, 11)
            for ph, plan in ((1, PLAN1), (3, PLAN3)):
                if ph == 3:
                    scalar_scan(act)
                scalar_phase(act, ph, plan, signals[ph])

        def vector_phase(dve, ph, plan, sig, link_sem):
            done = [0]

            def link(ins):
                done[0] += 1
                ins.then_inc(link_sem, 1)
                dve.wait_ge(link_sem, done[0])

            def product_read(ins, st):
                ins.then_inc(sig["product_read"], 1)
                dve.wait_ge(sig["product_read"], st.early)

            def core_max(n, g):
                a, s = plan.jobs[n]
                gi = plan.base[n] + g
                qt, m, heads = a.group(g)
                par = gi % 2
                dve.wait_ge(sig["scores_ready"], gi + 1)
                src = scores[:, 2 * par:2 * par + 2, :].rearrange("p u (v k) -> p (u v) k", v=2)[:, :, 0:a.seen(qt)]
                if a.bias is not None:
                    if g == 0:
                        dve.wait_ge(loaded["bias"], 4 * 16)
                    link(dve.tensor_tensor(biased[par][:, :, :], src,
                                           pair_bias[a.bias][:, qt, m, :].rearrange("p (h k) -> p h k", h=4),
                                           ALU.add))
                    src = biased[par][:, :, :]
                out = minus_max_raw if a.guard else minus_max
                last = dve.tensor_reduce(out[:, par, :], src, axis=AX.X, op=ALU.max, negate=True)
                if a.guard:
                    link(last)
                    last = dve.scalar_tensor_tensor(minus_max[:, par, :], minus_max_raw[:, par, :], UNMASKED_MIN,
                                                    minus_max_raw[:, par, :], op0=ALU.is_lt, op1=ALU.mult)
                last.then_inc(sig["max_ready"], 1)

            def core_keep(n, g):
                gi = plan.base[n] + g
                dve.wait_ge(sig["turned_ready"], 2 * gi + 2)
                if gi >= 2:
                    dve.wait_ge(sig["mixed_ready"], gi - 1)
                a = plan.jobs[n][0]
                dve.tensor_copy(kept_part(probs_t[gi % 2][:, 512:1024], a, g), kept_part(turned[:, 1, :], a, g))\
                    .then_inc(sig["kept1"], 1)

            def moments_of(src, st):
                for c in range(QT):
                    last = dve.bn_stats(stats[st.lane][:, c, :], src[:, c, :])
                link(last)
                dve.memset(spacer[:, :], 0.0)
                for c in range(QT):
                    last = dve.bn_aggr(moments[st.lane][:, c, :], stats[st.lane][:, c, :])
                last.then_inc(sig[f"variance_ready{st.lane}"], 1)

            def layer_norm(src, dst, gain, shift, st):
                for c in range(QT):
                    last = dve.tensor_scalar(centred[st.lane][:, c, :], src[:, c, :], moments[st.lane][:, c, 0:1], rstd[st.lane][:, c:c + 1],
                                             ALU.subtract, ALU.mult)
                link(last)
                link(dve.tensor_tensor(centred[st.lane][:, :, :], centred[st.lane][:, :, :], row(gain), ALU.mult))
                return dve.tensor_tensor(dst[:, :, :], centred[st.lane][:, :, :], row(shift), ALU.add)

            def keep_rows(dst, src, which):
                for c in range(QT):
                    last = dve.tensor_scalar(dst[:, c, :], src[:, c, :], row_keep_s[:, which, c:c + 1], None,
                                             ALU.mult)
                return last

            def find_rows(src, which, s):
                link(dve.tensor_reduce(row_max[s][:, which, :], src[:, :, :], axis=AX.X, op=ALU.max,
                                       apply_absolute_value=True))
                return dve.tensor_scalar(row_keep[s][:, which, :], row_max[s][:, which, :], 0.0, None,
                                         ALU.not_equal)

            for kind, n, g in plan.order:
                if kind == "scores":
                    if ph == 1 and (plan.jobs[n], g) == ((L2A, 3), 0):
                        dve.wait_ge(sig["scores_ready"], plan.base[n])
                        vector_masks3(dve, link)
                    core_max(n, g)
                    continue
                if kind == "turn":
                    if plan.jobs[n][0].bias is None:
                        core_keep(n, g)
                    continue
                if kind == "values":
                    continue
                st, s, a, w = n, n.s, n.a, n.what
                row_keep_s = row_keep[s]
                X, X1, X2, Z, C, CM, O = (tok[i][s] for i in ("X", "X1", "X2", "Z", "C", "CM", "O"))
                if w in ("turn", "l0_fc1", "ff1", "l2_in", "mod"):
                    continue
                if st.on_pe:
                    dve.wait_ge(sig[f"product_ready{st.lane}"], st.product)
                elif st.k > 1:
                    dve.wait_ge(sig[f"step_done{st.lane}"], st.k - 1)
                product = chain_ps[:, 0:S].rearrange("p (t f) -> p t f", t=QT)
                if w == "load":
                    dve.tensor_scalar(
                        target[s][:, :, :], target_mask[:, s, :].rearrange("p (t k) -> p t k", t=QT), MASKED, None,
                        ALU.mult)
                    last = find_rows(X, 0, s)
                elif w in ("project_q", "project_k"):
                    queries = w == "project_q"
                    if st.job > 1:
                        for pair in range(2):
                            dve.wait_ge(sig[f"stacked{st.job % 2}_pair{pair}"], stacked_by(st.job - 2))
                    upper, lower = split[st.lane][:, 1 - queries, 0, :], split[st.lane][:, 1 - queries, 1, :]
                    whole = two(centred[st.lane])
                    product_read(dve.tensor_scalar(whole, chain_ps[:, 0:S], col(a.bq if queries else a.bk),
                                                   a.scale if queries else 1.0, ALU.add, ALU.mult), st)
                    link(dve.tensor_scalar(upper.bitcast(I32), whole.bitcast(I32), UPPER_BITS, None,
                                           ALU.bitwise_and))
                    last = dve.tensor_tensor(lower, whole, upper, ALU.subtract)
                    if a.lengths and queries:
                        last = dve.tensor_tensor(q_row0[st.lane][:, :], whole[:, 0:1].to_broadcast([P, 16]), head_blocks[:, :],
                                          ALU.mult)
                elif w == "project_v":
                    vb = value_buffer(a, st.job)[:, :, 0:a.heads * (a.width + 1)]\
                        .rearrange("p t (h d) -> p t h d", h=a.heads)
                    for c in range(QT):
                        last = dve.tensor_tensor(
                            vb[:, c, :, 0:a.width], product[:, c, :].rearrange("p (h d) -> p h d", h=a.heads),
                            rows[:, ROWS.index(a.bv), :].rearrange("p (h d) -> p h d", h=a.heads), ALU.add)
                elif w == "energies0":
                    last = dve.tensor_scalar(nonzero[st.lane][:, :, :].rearrange("p t h -> p (t h)"), chain_ps[:, 0:32],
                                             0.0, None, ALU.not_equal)
                elif w == "lengths":
                    last = dve.tensor_scalar(length_mask[st.job % 2][0:16, :], iota[:, :], chain_ps[0:16, 0:1],
                                             MASKED, ALU.is_ge, ALU.mult)
                elif w == "normalize":
                    dve.wait_ge(sig["mixed_ready"], plan.base[st.job + 1])
                    w1 = a.width + 1
                    mx = mixed[:, 0:QT * a.heads * w1].rearrange("p (th d) -> p th d", d=w1)
                    inv = inverse[st.lane][:, :, :].rearrange("p t h -> p (t h)")[:, 0:QT * a.heads]
                    link(dve.reciprocal(inv, mx[:, :, a.width]))
                    last = dve.tensor_tensor(
                        two(Z).rearrange("p (th d) -> p th d", d=a.width), mx[:, :, 0:a.width],
                        inv.unsqueeze(2).to_broadcast([P, QT * a.heads, a.width]), ALU.mult)
                elif w == "l0_ln1":
                    link(keep_rows(Z, Z, 0))
                    link(dve.tensor_tensor(Z[:, :, :], Z[:, :, :], X[:, :, :], ALU.add))
                    moments_of(Z, st)
                    continue
                elif w == "l0_ln2":
                    link(keep_rows(Z, Z, 1))
                    link(dve.tensor_tensor(Z[:, :, :], Z[:, :, :], X1[:, :, :], ALU.add))
                    moments_of(Z, st)
                    continue
                elif w == "l0_fc2":
                    product_read(dve.tensor_tensor(Z[:, :, :], product, row("l0_fc2b"), ALU.add), st)
                    link(keep_rows(Z, Z, 0))
                    link(dve.tensor_tensor(Z[:, :, :], Z[:, :, :], X2[:, :, :], ALU.add))
                    moments_of(Z, st)
                    continue
                elif w == "out_projection":
                    product_read(dve.tensor_tensor(Z[:, :, :], product, row(f"{a.layer}_bo{a.n}"), ALU.add), st)
                    old = X if a.n == 1 else X1
                    link(dve.tensor_tensor(Z[:, :, :], Z[:, :, :], old[:, :, :], ALU.add))
                    if a is L2A:
                        dve.tensor_copy(X[:, :, :], Z[:, :, :])
                    moments_of(Z, st)
                    continue
                elif w == "ff2":
                    product_read(dve.tensor_tensor(Z[:, :, :], product, row(f"{a.layer}_ff2b"), ALU.add), st)
                    if ph == 1:
                        link(dve.scalar_tensor_tensor(two(Z), two(Z), 0.0, two(X2), op0=ALU.max, op1=ALU.add))
                    else:
                        link(dve.tensor_tensor(Z[:, :, :], Z[:, :, :], X2[:, :, :], ALU.add))
                    moments_of(Z, st)
                    continue
                elif w == "l2_ln_x":
                    moments_of(X, st)
                    continue
                elif w == "l2_ln_base":
                    moments_of(C, st)
                    continue
                elif w == "apply":
                    what = st.args[0]
                    if what == "l0_ln1":
                        link(layer_norm(Z, X1, "l0_g1", "l0_b1", st))
                        link(find_rows(X1, 1, s))
                        last = keep_rows(CM, C, 1)
                    elif what == "l0_ln2":
                        last = layer_norm(Z, X2, "l0_g2", "l0_b2", st)
                    elif what == "l0_fc2":
                        last = layer_norm(Z, X, "l0_g3", "l0_b3", st)
                    elif what == "out_projection":
                        if a is L2A:
                            last = layer_norm(Z, X1, "l2_g2", "l2_b2", st)
                        else:
                            last = layer_norm(Z, X1 if a.n == 1 else X2, f"{a.layer}_g{a.n}", f"{a.layer}_b{a.n}", st)
                    elif what == "ff2" and ph == 1:
                        last = layer_norm(Z, X, "l1_g3", "l1_b3", st)
                    elif what == "ff2":
                        last = layer_norm(Z, O, "l3_g3", "l3_b3", st)
                    elif what == "l2_ln_x":
                        last = layer_norm(X, X1, "l2_g1", "l2_b1", st)
                    else:
                        last = layer_norm(C, CM, "l2_g1", "l2_b1", st)
                elif w == "l2_u":
                    if s == 0:
                        link(dve.memset(u_all[:, 0:B], 0.0))
                    dst = u_all[:, B:B + S * B].rearrange("p (t b) -> p t b", b=B)
                    last = dve.tensor_copy(dst[:, :, s], chain_ps[0:NS, 0:S])
                elif w == "target":
                    link(dve.tensor_tensor(X[:, :, :], X[:, :, :], row("l2_bprog"), ALU.add))
                    last = dve.tensor_tensor(X[:, :, :], product, X[:, :, :], ALU.add)
                last.then_inc(sig[f"step_done{st.lane}"], 1)

        def vector_masks3(dve, link):
            dve.wait_ge(loaded["mask3"], 16)
            link(dve.tensor_copy(key_keep, mask3_in))
            link(dve.tensor_scalar(keep2, causal[:, :, :], 0.0, None, ALU.is_equal))
            link(dve.tensor_tensor(keep2, keep2, key_keep.unsqueeze(1).to_broadcast([P, QT, S]), ALU.mult))
            link(dve.tensor_scalar(self3[:, :, :], keep2, -MASKED, MASKED, ALU.mult, ALU.add))
            link(dve.tensor_scalar(cross3[:, :, :], key_keep.unsqueeze(1).to_broadcast([P, QT, S]),
                                   -MASKED, MASKED, ALU.mult, ALU.add))

        def vector_scan(dve, link):
            with dve.Fori(0, S // BLOCK) as blk:
                dve.wait_ge(z_ready, PRIMED + blk)
                dve.tensor_scalar(u_block[0][:, :], u_all[:, bass.ds(blk * (BLOCK * B), BLOCK * B)], 1.0, None, ALU.mult)\
                    .then_inc(u_ready, 1)
                dve.wait_ge(h_ready, blk * BLOCK + BLOCK)
                dve.tensor_scalar(h_all[:, bass.ds(blk * (BLOCK * B), BLOCK * B)], h_ring[:, B:(BLOCK + 1) * B], 1.0, None, ALU.mult)
                dve.tensor_copy(h_ring[:, 0:B], h_ring[:, BLOCK * B:(BLOCK + 1) * B]).then_inc(h_saved, 1)
            dve.wait_ge(h_saved, PRIMED + S // BLOCK)
            dve.wait_ge(loaded["l3"], 2 * 16)
            dve.tensor_tensor(h_all, h_all, u_all[:, B:B + S * B], ALU.add).then_inc(states_ready, 1)
            dve.wait_ge(states_ready, 1)

        @block.vector
        def _(dve):
            dve.wait_ge(loaded["tokens"], 2 * 16)
            dve.wait_ge(loaded["consts"], 4 * 16)
            dve.wait_ge(loaded["vectors"], 2 * 16)
            dve.wait_ge(loaded["masks"], 16)
            dve.wait_ge(consts_made, 11)
            done = [0]

            def link(ins):
                done[0] += 1
                ins.then_inc(vector_link, 1)
                dve.wait_ge(vector_link, done[0])

            dve.tensor_copy(ident16[:, :], ident[:, :]).then_inc(consts_cast, 1)
            dve.tensor_copy(causal[:, :, :], causal_in).then_inc(consts_cast, 1)
            dve.wait_ge(consts_cast, 2)
            for ph, plan, lk in ((1, PLAN1, vector_link1), (3, PLAN3, vector_link3)):
                if ph == 3:
                    for lane in range(LANES):
                        dve.wait_ge(signals[1][f"step_done{lane}"], PLAN1.counts[lane]["step"])
                    vector_scan(dve, link)
                vector_phase(dve, ph, plan, signals[ph], lk)


def _host_arrays(i):
    c = np.ascontiguousarray

    def tokens(v):
        v = v.reshape(B, QT, P, v.shape[-1]).transpose(2, 0, 1, 3)
        return c(v.reshape(P, B, -1))

    def heads(w):
        return w.transpose(1, 0, 2).reshape(P, P)

    def placed(w):
        v = w.reshape(-1, 2, 2, 2, 2, 8).transpose(0, 1, 4, 2, 3, 5)
        return v.reshape(w.shape)

    def placed8(w):
        v = w.reshape(-1, 2, 2, 2, 16).transpose(0, 1, 3, 2, 4)
        return v.reshape(w.shape)

    def chunks(w):
        return w.reshape(FC, P, P).transpose(1, 0, 2).reshape(P, FF)

    def pair(v):
        return c(v.reshape(16, QT, P, S).transpose(2, 1, 0, 3).reshape(P, QT, 4, 4 * S))

    L0, L1, L2, L3 = ({k[len(p):]: v for k, v in i.items() if k.startswith(p)}
                      for p in ("L0_xattn_", "L1_xattn_", "L2_xattn_", "L3_xattn_"))
    out = {
        "x": tokens(i["x"]), "ctx": tokens(i["ctx_1024"]), "probs": tokens(i["ctxb_2048x64"]),
        "target_mask": tokens(i["mask_BxSxS2_bk1"]), "mask3": c(i["mask_1xS2_if1"].reshape(S)),
        "bias0": pair(i["fside_1x16xSxS2_0"]), "bias1": pair(L1["attn_2d_bias"]),
        "w_l0": np.concatenate([placed(heads(L0["Wq1"])), placed(heads(L0["Wk1"])), heads(L0["Wv1"]), placed(heads(L0["Wq2"])),
                                placed(heads(L0["Wk2"])), heads(L0["Wv2"]), L0["fc1_w"].T, L0["fc2_w"].T], 1),
        "w_l1": np.concatenate([placed(L1["sa_wq"]), placed(L1["sa_wk"]), L1["sa_wv"], L1["sa_wo"], placed(L1["ca_wq"]), placed(L1["ca_wk"]),
                                L1["ca_wv"], L1["ca_wo"], L1["ff_w1"], chunks(L1["ff_w2"])], 1),
        "w_l2": np.concatenate([placed8(L2["W_qkv"][0:P].T), placed8(L2["W_qkv"][P:2 * P].T), L2["W_qkv"][2 * P:].T,
                                L2["W_o"].T, L2["W_in"].T, L2["Bmat"]], 1),
        "w64": np.concatenate([L2["A"].T, np.zeros((NS, P - NS), np.float32), L2["Cmat"], L2["W_prog"].T], 1),
        "w_l3": np.concatenate([placed(L3["Wqkv"][:, 0:P]), placed(L3["Wqkv"][:, P:2 * P]), L3["Wqkv"][:, 2 * P:],
                                L3["Wo1"], placed(L3["Wq"]), placed(L3["Wk"]), L3["Wv"], L3["Wo2"], L3["W1"],
                                chunks(L3["W2"])], 1),
    }
    zero = np.zeros(P, np.float32)
    by_row = {"l0_g1": L0["ln1_g"], "l0_b1": L0["ln1_b"], "l0_g2": L0["ln2_g"], "l0_b2": L0["ln2_b"],
              "l0_g3": L0["ln3_g"], "l0_b3": L0["ln3_b"], "l0_fc2b": L0["fc2_b"],
              "l1_bv1": L1["sa_bv"], "l1_bo1": L1["sa_bo"], "l1_g1": L1["sa_g"], "l1_b1": L1["sa_b"],
              "l1_bv2": L1["ca_bv"], "l1_bo2": L1["ca_bo"], "l1_g2": L1["ca_g"], "l1_b2": L1["ca_b"],
              "l1_ff2b": L1["ff_b2"], "l1_g3": L1["ff_g"], "l1_b3": L1["ff_b"],
              "l2_bv1": L2["b_qkv"][2 * P:], "l2_bo1": L2["b_o"], "l2_g1": L2["g1"], "l2_b1": L2["beta1"],
              "l2_g2": L2["g2"], "l2_b2": L2["beta2"], "l2_bprog": L2["b_prog"],
              "l3_bo1": L3["bo1"], "l3_g1": L3["g1"], "l3_b1": L3["b1"], "l3_bo2": L3["bo2"], "l3_g2": L3["g2"],
              "l3_b2": L3["b2"], "l3_ff2b": L3["bf2"], "l3_g3": L3["g3"], "l3_b3": L3["b3"], "zero": zero}
    by_col = {"l0_fc1b": L0["fc1_b"], "l1_bq1": placed(L1["sa_bq"]), "l1_bk1": placed(L1["sa_bk"]), "l1_bq2": placed(L1["ca_bq"]),
              "l1_bk2": placed(L1["ca_bk"]), "l2_bq1": placed8(L2["b_qkv"][0:P]), "l2_bk1": placed8(L2["b_qkv"][P:2 * P]),
              "l2_bin": L2["b_in"], "zero": zero}
    for f in range(FC):
        by_col[f"l1_ff1b{f}"] = L1["ff_b1"][f * P:(f + 1) * P]
        by_col[f"l3_ff1b{f}"] = L3["bf1"][f * P:(f + 1) * P]
    out["rows"] = np.concatenate([by_row[n] for n in ROWS])
    out["cols"] = np.stack([by_col[n] for n in COLS], 1)
    p, k = np.arange(P), np.arange(S)
    out["ident"] = np.eye(P, dtype=np.float32)
    out["head_blocks"] = ((p // 8)[:, None] == np.arange(16)[None, :]).astype(np.float32)
    out["iota"] = np.tile(k.astype(np.float32), (16, 1))
    q = (np.arange(QT)[None, :] * P + p[:, None])[:, :, None]
    out["causal"] = np.where(k[None, None, :] > q, np.float32(MASKED), np.float32(0))
    return {n: c(v) for n, v in out.items()}


_INPUTS = ["x", "ctx", "probs", "target_mask", "mask3", "bias0", "bias1", "w_l0", "w_l1", "w_l2", "w64", "w_l3",
           "rows", "cols", "ident", "head_blocks", "iota", "causal"]


def kernel(**inputs):
    import concourse.bacc as bacc
    from concourse.bass_utils import run_bass_kernel_spmd

    arrays = _host_arrays({k: np.asarray(v) for k, v in inputs.items()})

    nc = bacc.Bacc("TRN2", target_bir_lowering=False, num_devices=1)
    t = {n: nc.dram_tensor(f"in_{n}", arrays[n].shape, mybir.dt.from_np(arrays[n].dtype),
                           kind="ExternalInput").ap() for n in _INPUTS}
    t["out"] = nc.dram_tensor("out_x", (P, B * S), F32, kind="ExternalOutput").ap()
    build(nc, t)
    r = run_bass_kernel_spmd(nc, [{f"in_{n}": arrays[n] for n in _INPUTS}], core_ids=[0])
    out = r.results[0]["out_x"]
    return np.ascontiguousarray(out.reshape(P, B, QT, P).transpose(1, 2, 0, 3).reshape(B, S, P))
```

```python
from contextlib import ExitStack

import numpy as np
import concourse.bass as bass
from concourse import mybir

F32 = mybir.dt.float32
F32R = mybir.dt.float32r
I32 = mybir.dt.int32
BF16 = mybir.dt.bfloat16
ACT = mybir.ActivationFunctionType
ALU = mybir.AluOpType
AX = mybir.AxisListType

P = 128
B = 4
S = 256
QT = S // P
STREAMS = B
NS = 64
FF = 512
FC = FF // P
BLOCK = 32
BLOCKS = S // BLOCK
WARMING = (512, 384)
RINGS = 2
LANES = 2
SLACK = 0.36
STREAMED = 64
PIECES = 4
UPPER_BITS = -4096
MASKED = -1e30
LOWEST = -3.4e38
UNMASKED_MIN = 1e29

WEIGHTS = {
    "l0": [("q1", 128), ("k1", 128), ("v1", 128), ("q2", 128), ("k2", 128), ("v2", 128), ("fc1", 128), ("fc2", 128)],
    "l1": [("q1", 128), ("k1", 128), ("v1", 128), ("o1", 128), ("q2", 128), ("k2", 128), ("v2", 128), ("o2", 128),
           ("ff1", FF), ("ff2", FF)],
    "l2": [("q1", 128), ("k1", 128), ("v1", 128), ("o1", 128), ("in", 128), ("bmat", NS)],
    "l3": [("q1", 128), ("k1", 128), ("v1", 128), ("o1", 128), ("q2", 128), ("k2", 128), ("v2", 128), ("o2", 128),
           ("ff1", FF), ("ff2", FF)],
}
ROWS = ["l0_g1", "l0_b1", "l0_g2", "l0_b2", "l0_g3", "l0_b3", "l0_fc2b", "zero",
        "l1_bv1", "l1_bo1", "l1_g1", "l1_b1", "l1_bv2", "l1_bo2", "l1_g2", "l1_b2", "l1_ff2b", "l1_g3", "l1_b3",
        "l2_bv1", "l2_bo1", "l2_g1", "l2_b1", "l2_g2", "l2_b2", "l2_bprog",
        "l3_bo1", "l3_g1", "l3_b1", "l3_bo2", "l3_g2", "l3_b2", "l3_ff2b", "l3_g3", "l3_b3"]
L0_ROWS = 8
COLS = ["l0_fc1b", "l1_bq1", "l1_bk1", "l1_bq2", "l1_bk2", "l1_ff1b0", "l1_ff1b1", "l1_ff1b2", "l1_ff1b3",
        "l2_bq1", "l2_bk1", "l2_bin", "l3_ff1b0", "l3_ff1b1", "l3_ff1b2", "l3_ff1b3", "zero"]


class Attention:

    def __init__(self, name, layer, n, heads, scale, mask=None, lengths=False, bias=None, biased_qkv=False,
                 keys="CT"):
        self.name, self.layer, self.n, self.heads, self.scale = name, layer, n, heads, scale
        self.mask, self.lengths, self.bias, self.keys = mask, lengths, bias, keys
        self.width = P // heads
        self.tall = PIECES * self.width
        self.tile_groups = heads // 4
        self.groups = QT * self.tile_groups
        self.guard = lengths or bias == 0
        self.bq = f"{layer}_bq{n}" if biased_qkv else "zero"
        self.bk = f"{layer}_bk{n}" if biased_qkv else "zero"
        self.bv = f"{layer}_bv{n}" if biased_qkv else "zero"

    def group(self, g):
        qt, m = divmod(g, self.tile_groups)
        places = P // self.tall
        out = []
        for u in range(2):
            for v in range(2):
                if places == 4:
                    out.append((u, v, 2 * (m % 2) + u, 2 * (m // 2) + v))
                else:
                    out.append((u, v, u, 2 * m + v))
        return qt, m, out

    def seen(self, qt):
        return P * (qt + 1) if self is L0S else S


L0S = Attention("l0s", "l0", 1, 16, 8.0 ** -0.5, mask="causal", lengths=True, keys="XT")
L0C = Attention("l0c", "l0", 2, 16, 8.0 ** -0.5, lengths=True)
L1S = Attention("l1s", "l1", 1, 16, 128.0 ** -0.5, mask="target", bias=0, biased_qkv=True, keys="XT")
L1C = Attention("l1c", "l1", 2, 16, 128.0 ** -0.5, bias=1, biased_qkv=True)
L2A = Attention("l2a", "l2", 1, 8, 0.25, biased_qkv=True)
L3S = Attention("l3s", "l3", 1, 16, 8.0 ** -0.5, mask="self3", keys="XT")
L3C = Attention("l3c", "l3", 2, 16, 8.0 ** -0.5, mask="cross3")


def prepare(a):
    return (["project_k", "project_q", "project_v"] + (["energies0", "lengths"] if a.lengths else [])
            + (["l2_ln_base", "apply l2_ln_base", "turn CM CT"] if a is L1C else []))


def finish(a):
    if a is L0S:
        return ["normalize", "l0_ln1", "apply l0_ln1", "turn X1 XT", "turn CM CT"]
    if a is L0C:
        return ["normalize", "l0_ln2", "apply l0_ln2", "turn X2 ZT", "l0_fc1", "l0_fc2", "apply l0_fc2", "turn X XT"]
    if a is L1S:
        return ["normalize", "turn Z ZT", "out_projection", "apply out_projection", "turn C CT"]
    if a is L1C:
        return ["normalize", "turn Z ZT", "out_projection", "apply out_projection", "turn X2 ZT", "ff1 0", "ff1 1",
                "ff2", "apply ff2", "l2_ln_x", "apply l2_ln_x", "turn X1 XT"]
    if a is L2A:
        return ["normalize", "turn Z ZT", "out_projection", "apply out_projection", "turn X1 XT", "l2_in", "l2_u"]
    if a is L3S:
        return ["normalize", "turn C CT", "turn Z ZT", "out_projection", "apply out_projection", "turn X1 XT"]
    return ["normalize", "turn Z ZT", "out_projection", "apply out_projection", "turn X2 ZT", "ff1 0", "ff1 1",
            "ff2", "apply ff2"]


ON_PE = {"project_q", "project_k", "project_v", "energies0", "lengths", "turn", "l0_fc1", "l0_fc2",
         "out_projection", "ff1", "ff2", "l2_in", "l2_u", "mod", "target"}
OPERANDS = {"project_q", "project_k", "project_v", "energies0", "lengths"}
READS_EARLY = {"out_projection", "l0_fc2", "ff2", "project_q", "project_k"}
NORMS = {"l0_ln1", "l0_ln2", "l0_fc2", "out_projection", "ff2", "l2_ln_x", "l2_ln_base"}


class Step:

    def __init__(self, what, stream, attention, job, counts, product_before):
        self.what, *self.args = what.split()
        self.s, self.a, self.job = stream, attention, job
        self.lane = stream % LANES
        count = counts[self.lane]
        count["step"] += 1
        self.k = count["step"]
        self.on_pe = self.what in ON_PE
        if self.on_pe:
            count["product"] += 1
        self.product = count["product"]
        self.product_before = product_before
        self.early = 0
        if self.what in READS_EARLY:
            counts[0]["early"] += 1
            self.early = counts[0]["early"]
        if self.what in NORMS:
            count["norm"] += 1
        self.norm = count["norm"]


PE_STEP = {"project_k": 0.5, "project_q": 0.5, "project_v": 0.5, "energies0": 0.5, "lengths": 0.1, "turn": 0.25,
           "l0_fc1": 0.5, "l0_fc2": 0.5, "out_projection": 0.5, "ff1": 0.9, "ff2": 1.8, "l2_in": 0.5, "l2_u": 0.5,
           "mod": 0.5, "target": 0.9}
ACT_STEP = {"turn": 0.35, "l0_fc1": 0.4, "ff1": 0.8, "l2_in": 0.4, "mod": 0.3}
DVE_STEP = {"project_k": 1.3, "project_q": 1.3, "project_v": 0.8, "energies0": 0.2, "lengths": 0.4,
            "normalize": 0.8, "l0_ln1": 2.0, "l0_ln2": 2.0, "l0_fc2": 2.3, "out_projection": 2.0, "ff2": 2.0,
            "l2_ln_x": 1.2, "l2_ln_base": 1.2, "apply": 1.7, "l2_u": 0.4, "target": 0.8, "load": 3.0}
SIGNAL = 0.1
POOL_NORM = 1.0
TABLE = 1.3
STACK_PAIR = 5.0
CROWDED = 5.0


class Clock:

    def __init__(self):
        self.pe = self.act = self.dve = self.dma = 0.0
        self.lane = [0.0] * LANES
        self.bank = 0.0
        self.exp, self.kept, self.stacked = {}, {}, {}

    def core(self, part, plan, n, g):
        a, _ = plan.jobs[n]
        gi = plan.base[n] + g
        qt = a.group(g)[0]
        share = a.seen(qt) / S
        if part == "scores":
            stacked = self.stacked.get(n, 0.0)
            self.pe = max(self.pe, self.exp.get(gi - 2, 0.0) + SIGNAL, stacked) + 0.43 * share
            self.pe += 0.43 * (a.mask is not None) + 0.43 * a.lengths * share
            self.dve = max(self.dve, self.pe + SIGNAL) + (1.15 if a.bias is None else 1.7) * share + 0.2 * a.guard
            self.act = max(self.act, self.dve + SIGNAL) + 1.5 * share
            self.exp[gi] = self.act
        elif part == "turn":
            self.pe = max(self.pe, self.exp[gi] + SIGNAL) + 0.9 * share
            self.act = max(self.act, self.pe) + 0.5 * share
            if a.bias is None:
                self.dve = max(self.dve, self.pe + SIGNAL) + 0.6 * share
            else:
                self.act += 0.5
            self.kept[gi] = max(self.act, self.dve if a.bias is None else 0.0)
        else:
            self.pe = max(self.pe, self.kept[gi] + SIGNAL) + 1.7 * share

    def fits(self, what, lane):
        what = what.split()[0]
        if self.dve > self.pe + CROWDED and what in DVE_STEP:
            return False
        free = self.pe if what in ON_PE else self.dve
        ready = max(self.lane[lane], self.bank if what in ON_PE else 0.0)
        return ready + SIGNAL <= free + SLACK

    def step(self, st):
        w, t = st.what, self.lane[st.lane] + SIGNAL
        if st.on_pe:
            self.pe = t = max(self.pe, t, self.bank + SIGNAL) + PE_STEP[w]
            t += SIGNAL
        if w == "normalize":
            t = max(t, self.pe + SIGNAL)
        if w in ACT_STEP:
            gelu = w == "ff1" and st.a is L3C
            self.act = t = max(self.act, t) + ACT_STEP[w] + TABLE * (gelu and st.args == ["0"])
            if gelu and st.args == ["1"]:
                self.act += TABLE
        else:
            start = max(self.dve, t)
            self.dve = t = start + DVE_STEP[w]
            if st.early:
                self.bank = start + 0.4
        if st.on_pe and not st.early:
            self.bank = t
        if w in NORMS:
            t += POOL_NORM
        self.lane[st.lane] = t
        if w in ("project_q", "project_k"):
            self.dma = max(self.dma, t) + STACK_PAIR
            if w == "project_q":
                self.stacked[st.job] = self.dma + 2.0
                self.dma += 2 * STACK_PAIR


class Plan:

    def __init__(self, jobs, load):
        self.jobs = jobs
        self.lanes = [s % LANES for _, s in jobs]
        self.base = [sum(a.groups for a, _ in self.jobs[:n]) for n in range(len(self.jobs) + 1)]
        self.groups = self.base[-1]
        self.order = []
        self.counts = [{"step": 0, "product": 0, "norm": 0, "early": 0} for _ in range(LANES)]
        self.operands = {}
        self.normalized = {}
        self.queue = [[] for _ in range(LANES)]
        self.clock = Clock()
        self.product_before = None
        groups = [(n, g) for n, (a, _) in enumerate(self.jobs) for g in range(a.groups)]
        last = len(self.jobs) - 1

        def enter(n, steps):
            self.queue[self.lanes[n]] += [(w, n) for w in steps]

        enter(0, load + prepare(self.jobs[0][0]))
        self.flush(0, "all")
        enter(1, load + prepare(self.jobs[1][0])[:2])
        self.part("scores", *groups[0])
        self.part("scores", *groups[1])
        for n, (a, s) in enumerate(self.jobs):
            for g in range(a.groups):
                gi = self.base[n] + g
                self.part("turn", n, g)
                self.fill()
                if gi + 2 < self.groups:
                    m, h = groups[gi + 2]
                    if h == 0:
                        self.flush(m, "prepare")
                    self.part("scores", m, h)
                    self.fill()
                at_once = n + 2 <= last and self.jobs[n + 2][1] != s
                if g == a.groups - 2 and at_once:
                    first = load if self.jobs[n + 2][0] is self.jobs[0][0] else []
                    enter(n + 2, first + prepare(self.jobs[n + 2][0])[:2])
                if g == 0 and n > 0:
                    self.flush(n - 1, "normalize")
                self.part("values", n, g)
                if g == a.groups - 1:
                    self.queue[self.lanes[n]].insert(0, ("normalize", n))
                    if at_once:
                        enter(n + 2, prepare(self.jobs[n + 2][0])[2:])
                    enter(n, finish(a)[1:])
                    if n + 2 <= last and not at_once:
                        enter(n + 2, prepare(self.jobs[n + 2][0]))
                if gi == 0:
                    enter(1, prepare(self.jobs[1][0])[2:])
                self.fill()
        while any(self.queue):
            lane = min((i for i in range(LANES) if self.queue[i]), key=lambda i: self.clock.lane[i])
            self.pop(lane)

    def part(self, part, n, g):
        self.order.append((part, n, g))
        self.clock.core(part, self, n, g)

    def fill(self):
        for _ in range(2):
            lanes = [i for i in range(LANES) if self.queue[i] and self.clock.fits(self.queue[i][0][0], i)]
            if not lanes:
                return
            self.pop(max(lanes, key=lambda i: len(self.queue[i])))

    def flush(self, job, until):
        lane = self.lanes[job]
        kinds = {"prepare": OPERANDS, "normalize": {"normalize"}}
        while any(until == "all" or (j == job and w.split()[0] in kinds[until]) for w, j in self.queue[lane]):
            self.pop(lane)

    def pop(self, lane):
        what, job = self.queue[lane].pop(0)
        a, s = self.jobs[job]
        step = Step(what, s, a, job, self.counts, self.product_before)
        if step.on_pe:
            self.product_before = step
        if step.what in ("project_v", "lengths"):
            self.operands[job] = step.k
        if step.what == "normalize":
            self.normalized[job] = step.k
        self.order.append(("step", step, None))
        self.clock.step(step)
        if what == "ff1 0" and a is L3C:
            self.pop(lane)


def streams(*attentions):
    return [(a, s) for a in attentions for s in range(STREAMS)]


PLAN1 = Plan(streams(L0S, L0C, L1S, L1C, L2A), ["load", "turn X XT"])
PLAN3 = Plan(streams(L3S, L3C), ["mod", "target", "turn X XT"])


def build(nc, t):
    ctx = ExitStack()
    with ctx:
        def sb(name, shape, dt=F32):
            return ctx.enter_context(nc.sbuf_tensor(name, shape, dt))

        def pb(name, shape, dt=F32):
            return ctx.enter_context(nc.psum_tensor(name, shape, dt))

        def sem(name):
            return ctx.enter_context(nc.semaphore(name))

        x_all = sb("x_all", [P, B, S])
        c_all = sb("c_all", [P, B, S])
        target_mask = sb("target_mask", [P, B, QT * S], mybir.dt.uint8)
        width = {k: sum(n for _, n in v) for k, v in WEIGHTS.items()}
        w_sb = {k: sb(f"w_{k}", [P, width[k]]) for k in ("l0", "l1", "l2")}
        w64 = sb("w64", [NS, 3 * P])
        rows = sb("rows", [P, len(ROWS), P])
        cols = sb("cols", [P, len(COLS)])
        pair_bias = [sb(f"pair_bias{i}", [P, QT, 4, 4 * S]) for i in range(2)]
        w_sb["l3"] = pair_bias[1][:, 0, :, :].rearrange("p m k -> p (m k)")[:, 0:width["l3"]]
        probs_all = pair_bias[1][:, 1, 0, 0:B * QT * NS].rearrange("p (b n) -> p b n", b=B)
        mask3_in = pair_bias[1][:, 1, 1, 0:S].bitcast(I32)
        ident = sb("ident", [P, P])
        head_blocks = sb("head_blocks", [P, 16])
        iota = sb("iota", [16, S])
        ident16 = sb("ident16", [P, P], BF16)
        causal = sb("causal", [P, QT, S], BF16)
        ones = sb("ones", [P, P])
        minus_half = sb("minus_half", [P, QT])
        tok = {n: [sb(f"{n}{s}", [P, QT, P]) for s in range(STREAMS)] for n in ("X1",)}
        tok["X"] = [x_all[:, s, :].rearrange("p (t f) -> p t f", t=QT) for s in range(STREAMS)]
        tok["C"] = [c_all[:, s, :].rearrange("p (t f) -> p t f", t=QT) for s in range(STREAMS)]
        tok["O"] = tok["X1"]
        tok["Z"] = [sb(f"Z{s}", [P, QT, P]) for s in range(STREAMS)]
        for n in ("X2", "CM"):
            tok[n] = [sb(f"{n}{i}", [P, QT, P]) for i in range(LANES)] * 2
        feat = {n: [sb(f"{n}{s}", [P, S]) for s in range(STREAMS)] for n in ("XT", "CT")}
        feat["ZT"] = [sb(f"ZT{i}", [P, S]) for i in range(LANES)] * 2
        hidden = [sb(f"hidden{i}", [P, FC, S]) for i in range(LANES)]
        row_max = [sb(f"row_max{s}", [P, 2, QT]) for s in range(STREAMS)]
        row_keep = [sb(f"row_keep{s}", [P, 2, QT]) for s in range(STREAMS)]
        target = [sb(f"target{s}", [P, QT, S], BF16) for s in range(STREAMS)]
        self3, cross3 = target[0:2]
        mod_b = [pair_bias[0][0:NS, 1, 0, s * P:(s + 1) * P] for s in range(STREAMS)]
        split = [sb(f"split{i}", [P, 2, 2, S]) for i in range(LANES)]
        stacked_q = [sb(f"stacked_q{i}", [P, 4, S]) for i in range(2)]
        stacked_k = [sb(f"stacked_k{i}", [P, 4, S]) for i in range(2)]
        values = [sb(f"values{i}", [P, QT, 16 * 9 + STREAMED]) for i in range(2)]
        values_l2 = [sb(f"values_l2{i}", [P, QT, 8 * 17 + STREAMED]) for i in range(2)]
        q_row0 = [sb(f"q_row0{i}", [P, 16]) for i in range(LANES)]
        nonzero = [sb(f"nonzero{i}", [P, QT, 16]) for i in range(LANES)]
        length_mask = [sb(f"length_mask{i}", [P, S], BF16) for i in range(2)]
        biased = [sb(f"biased{i}", [P, 4, S]) for i in range(2)]
        keep2 = biased[0][:, 0:2, :]
        key_keep = biased[0][:, 2, :]
        causal_in = biased[1][:, 0:2, :]
        minus_max = sb("minus_max", [P, 2, 4])
        row_maxima = sb("row_maxima", [P, 2, 4])
        minus_max_raw = sb("minus_max_raw", [P, 2, 4])
        probs = [sb(f"probs{i}", [P, 4, S]) for i in range(2)]
        probs_t = [sb(f"probs_t{i}", [P, 4 * S]) for i in range(2)]
        inverse = [sb(f"inverse{i}", [P, QT, 16]) for i in range(LANES)]
        stats = [sb(f"stats{i}", [P, QT, 6]) for i in range(LANES)]
        moments = [sb(f"moments{i}", [P, QT, 2]) for i in range(LANES)]
        variance = [sb(f"variance{i}", [P, QT]) for i in range(LANES)]
        rstd = [sb(f"rstd{i}", [P, QT]) for i in range(LANES)]
        unused = sb("unused", [P, 1])
        spacer = sb("spacer", [P, 1])
        eps_tile = {e: sb(f"eps{n}", [P, QT]) for n, e in enumerate((1e-5, 1e-6))}
        centred = [sb(f"centred{i}", [P, QT, P]) for i in range(LANES)]
        h_all = pair_bias[0][0:NS, 0, 0, :]
        u_all = pair_bias[0][0:NS, 0, 1:3, :].rearrange("p m k -> p (m k)")[:, 0:B + S * B]
        u_block = [sb(f"u_block{i}", [NS, BLOCK * B]) for i in range(RINGS)]
        h_ring = [sb(f"h_ring{i}", [NS, BLOCK * B]) for i in range(RINGS)]

        scores = pb("scores", [P, 4, 512])
        turned = pb("turned", [P, 2, 512])
        mixed = pb("mixed", [P, 512])
        chain_ps = pb("chain_ps", [P, 512])
        warm_rows = causal[:, :, :].rearrange("p t k -> p (t k)")
        z_bank = [chain_ps, mixed]

        loaded = {k: sem(f"loaded_{k}") for k in ("tokens", "context", "ident", "rows", "consts", "vectors", "l0", "masks", "mask3", "l1", "bias", "l2", "l3")}
        consts_made = sem("consts_made")
        consts_cast = sem("consts_cast")
        out_stored = sem("out_stored")
        signals = {}
        for ph in (1, 3):
            signals[ph] = {n: sem(f"{n}_p{ph}") for n in (
                "step_done0", "step_done1", "product_ready0", "product_ready1", "variance_ready0",
                "variance_ready1", "product_read", "eps_added", "scores_ready",
                "max_ready", "probs_ready", "turned_ready", "kept0", "kept1", "mixed_ready",
                "stacked0_pair0", "stacked0_pair1", "stacked1_pair0", "stacked1_pair1")}
        vector_link = sem("vector_link")
        vector_link1, vector_link3 = sem("vector_link1"), sem("vector_link3")
        drive_ready, h_ready, u_ready, h_saved = sem("drive_ready"), sem("h_ready"), sem("u_ready"), sem("h_saved")
        z_ready = sem("z_ready")

        def row(name):
            return rows[:, ROWS.index(name), :].unsqueeze(1).to_broadcast([P, QT, P])

        def col(name):
            i = COLS.index(name)
            return cols[:, i:i + 1]

        def weight(layer, name):
            at = 0
            for n, w in WEIGHTS[layer]:
                if n == name:
                    return w_sb[layer][:, at:at + w]
                at += w
            raise KeyError(name)

        def value_buffer(a, job):
            return (values if a.heads == 16 else values_l2)[job % 2]

        def mask_of(a, s):
            return {"causal": causal, "self3": self3, "cross3": cross3}.get(a.mask, target[s])

        def kept_part(half, a, g):
            return half.rearrange("p (h k) -> p h k", h=2)[:, :, 0:a.seen(a.group(g)[0])]

        def stacked_by(n):
            return 16 * 2 * PIECES * 2 * (n // 2 + 1)

        def two(t3):
            return t3[:, :, :].rearrange("p t f -> p (t f)")

        block = ctx.enter_context(nc.Block())

        def stack_operands(sp, plan, sig, ph):
            set_done = {}
            for kind, st, _ in plan.order:
                if kind == "step" and st.what in ("project_q", "project_k"):
                    set_done[st.job, st.what] = st
            for n in range(len(plan.jobs)):
                a, lane = plan.jobs[n][0], set_done[n, "project_k"].lane
                if ph == 1 and n == len(plan.jobs) - 1:
                    sp.wait_ge(sig["max_ready"], plan.base[plan.jobs.index((L1C, STREAMS - 1)) + 1])
                    sp.dma_start(mask3_in, t["mask3"].partition_broadcast(P)).then_inc(loaded["mask3"], 16)
                    sp.dma_start(probs_all, t["probs"]).then_inc(loaded["l3"], 16)
                    sp.dma_start(w_sb["l3"], t["w_l3"]).then_inc(loaded["l3"], 16)
                if ph == 1 and n == 1:
                    sp.dma_start(rows[:, L0_ROWS:, :], t["rows"][L0_ROWS * P:].partition_broadcast(P))\
                        .then_inc(loaded["rows"], 16)
                if ph == 1 and n == 2:
                    sp.dma_start(w_sb["l1"][:, :], t["w_l1"]).then_inc(loaded["l1"], 16)
                    sp.dma_start(w_sb["l2"][:, :], t["w_l2"]).then_inc(loaded["l2"], 16)
                    sp.dma_start(w64[:, :], t["w64"]).then_inc(loaded["l2"], 16)
                if ph == 1 and 2 < n < 3 + 2 * QT:
                    i, qt = divmod(n - 3, QT)
                    sp.dma_start(pair_bias[i][:, qt], t[f"bias{i}"][:, qt]).then_inc(loaded["bias"], 16)
                if n >= 2:
                    sp.wait_ge(sig["scores_ready"], plan.base[n - 1])
                for pair in range(2):
                    for queries in (0, 1):
                        if pair == 0:
                            sp.wait_ge(sig[f"step_done{lane}"], set_done[n, "project_q" if queries else "project_k"].k)
                        dst = (stacked_q if queries else stacked_k)[n % 2]
                        for piece in range(PIECES):
                            part = piece // 2 if queries else piece % 2
                            for j in (2 * pair, 2 * pair + 1):
                                sp.dma_start(dst[piece:P:PIECES, j, :],
                                             split[lane][32 * j:32 * (j + 1), 1 - queries, part, :])\
                                    .then_inc(sig[f"stacked{n % 2}_pair{pair}"], 16)

        @block.sync
        def _(sp):
            sp.dma_start(x_all[:, :, :], t["x"]).then_inc(loaded["tokens"], 16)
            sp.dma_start(ident[:, :], t["ident"]).then_inc(loaded["ident"], 16)
            sp.dma_start(w_sb["l0"][:, :], t["w_l0"]).then_inc(loaded["l0"], 16)
            sp.dma_start(cols[:, :], t["cols"]).then_inc(loaded["vectors"], 16)
            sp.dma_start(target_mask[:, :, :], t["target_mask"]).then_inc(loaded["masks"], 16)
            for name, dst in (("head_blocks", head_blocks), ("iota", iota)):
                sp.dma_start(dst[:, :], t[name]).then_inc(loaded["consts"], 16)
            sp.dma_start(causal_in, t["causal"]).then_inc(loaded["consts"], 16)
            sp.dma_start(rows[:, 0:L0_ROWS, :], t["rows"][0:L0_ROWS * P].partition_broadcast(P))\
                .then_inc(loaded["vectors"], 16)
            sp.dma_start(c_all[:, :, :], t["ctx"]).then_inc(loaded["context"], 16)
            for ph, plan in ((1, PLAN1), (3, PLAN3)):
                stack_operands(sp, plan, signals[ph], ph)
            for s in range(STREAMS):
                last = [x[1].k for x in PLAN3.order
                        if x[0] == "step" and x[1].args == ["ff2"] and x[1].s == s][-1]
                sp.wait_ge(signals[3][f"step_done{s % LANES}"], last)
                sp.dma_start(t["out"][:, s * S:(s + 1) * S], two(tok["O"][s])).then_inc(out_stored, 16)
            sp.wait_ge(out_stored, 16 * B)

        @block.gpsimd
        def _(pool):
            pool.memset(ones[:, :], 1.0).then_inc(consts_made, 1)
            pool.memset(minus_half[:, :], -0.5).then_inc(consts_made, 1)
            for e, tile in eps_tile.items():
                pool.memset(tile[:, :], e).then_inc(consts_made, 1)
            for i in range(2):
                pool.memset(length_mask[i][:, :], 0.0).then_inc(consts_made, 1)
                pool.memset(values[i][:, :, :], 1.0).then_inc(consts_made, 1)
                pool.memset(values_l2[i][:, :, :], 1.0).then_inc(consts_made, 1)
            pool.memset(h_ring[RINGS - 1][:, :], 0.0).then_inc(h_ready, 1)
            pool.memset(unused[:, 0:1], 0.0).then_inc(h_saved, RINGS)
            pool.wait_ge(consts_made, 10)
            for ph, plan in ((1, PLAN1), (3, PLAN3)):
                sig = signals[ph]
                norms = 0
                for kind, step, _ in plan.order:
                    if kind != "step" or step.what not in NORMS:
                        continue
                    eps = 1e-6 if ph == 3 and step.what == "ff2" else 1e-5
                    lane = step.lane
                    norms += 1
                    pool.wait_ge(sig[f"variance_ready{lane}"], step.norm)
                    pool.tensor_tensor(variance[lane][:, :], moments[lane][:, :, 1], eps_tile[eps][:, :], ALU.add)\
                        .then_inc(sig["eps_added"], 1)
                    pool.wait_ge(sig["eps_added"], norms)
                    pool.tensor_tensor(rstd[lane][:, :], variance[lane][:, :], minus_half[:, :], ALU.pow)\
                        .then_inc(sig[f"step_done{lane}"], 1)

        def tensor_phase(pe, ph, plan, sig):
            def steps_done(lane, k):
                if k > 0:
                    pe.wait_ge(sig[f"step_done{lane}"], k)

            def core_scores(n, g):
                a, s = plan.jobs[n]
                gi = plan.base[n] + g
                qt, m, heads = a.group(g)
                if g == 0:
                    steps_done(plan.lanes[n], plan.operands[n])
                    pe.wait_ge(sig[f"stacked{n % 2}_pair0"], stacked_by(n))
                if g == a.tile_groups // 2:
                    pe.wait_ge(sig[f"stacked{n % 2}_pair1"], stacked_by(n))
                if gi >= 2:
                    pe.wait_ge(sig["probs_ready"], gi - 1)
                bank = 2 * (gi % 2)
                seen = a.seen(qt)
                masked = a.mask is not None
                if a.lengths:
                    for u, v, i, j in heads:
                        h = 4 * j + i
                        pe.matmul(scores[:, bank + u, v * S:v * S + seen], ident16[:, h:h + 1].to_broadcast([P, P]),
                                  length_mask[n % 2][:, 0:seen], start=(v == 0), stop=False,
                                  skip_group_check=True)
                    if masked:
                        for u in range(2):
                            pe.matmul(scores[:, bank + u, :].rearrange("p (v k) -> p v k", v=2)[:, :, seen - P:seen],
                                      ident16[:, :],
                                      causal[:, qt, seen - P:seen].unsqueeze(1).to_broadcast([P, 2, P]),
                                      start=False, stop=False, skip_group_check=True)
                elif masked:
                    for u in range(2):
                        pe.matmul(scores[:, bank + u, :].rearrange("p (v k) -> p v k", v=2), ident16[:, :],
                                  mask_of(a, s)[:, qt, :].unsqueeze(1).to_broadcast([P, 2, S]),
                                  start=True, stop=False, skip_group_check=True)
                for v in range(2):
                    for u, vv, i, j in heads:
                        if vv != v:
                            continue
                        at = a.tall * i
                        last = pe.matmul(scores[:, bank + u, v * S:v * S + seen],
                                         stacked_q[n % 2][at:at + a.tall, j, qt * P:(qt + 1) * P].bitcast(F32R),
                                         stacked_k[n % 2][at:at + a.tall, j, 0:seen].bitcast(F32R),
                                         start=not (masked or a.lengths), stop=True, skip_group_check=True)
                last.then_inc(sig["scores_ready"], 1)

            def core_turn(n, g):
                gi = plan.base[n] + g
                a = plan.jobs[n][0]
                seen = a.seen(a.group(g)[0])
                pe.wait_ge(sig["probs_ready"], gi + 1)
                for half in range(2):
                    if gi >= 1:
                        pe.wait_ge(sig[f"kept{half}"], gi)
                    for q in range(2):
                        for c in range(seen // P):
                            last = pe.transpose(turned[:, half, q * S + c * P:q * S + (c + 1) * P],
                                                probs[gi % 2][:, 2 * half + q, c * P:(c + 1) * P], ident[:, :])
                    last.then_inc(sig["turned_ready"], 1)

            def core_values(n, g):
                a, s = plan.jobs[n]
                gi = plan.base[n] + g
                qt, m, heads = a.group(g)
                tiles = a.seen(qt) // P
                w1 = a.width + 1
                if g == 0 and n > 0:
                    steps_done(plan.lanes[n - 1], plan.normalized[n - 1])
                for pos in range(4):
                    h = 4 * m + pos
                    if pos % 2 == 0:
                        pe.wait_ge(sig[f"kept{pos // 2}"], gi + 1)
                    at = qt * a.heads * w1 + h * w1
                    for c in range(tiles):
                        last = pe.matmul(mixed[:, at:at + STREAMED],
                                         probs_t[gi % 2][:, pos * S + c * P:pos * S + (c + 1) * P],
                                         value_buffer(a, n)[:, c, h * w1:h * w1 + STREAMED],
                                         start=(c == 0), stop=(c == tiles - 1), skip_group_check=True)
                last.then_inc(sig["mixed_ready"], 1)

            def chain_step(st):
                if not st.on_pe:
                    return
                steps_done(st.lane, st.k - 1)
                before = st.product_before
                if before is not None and before.early:
                    pe.wait_ge(sig["product_read"], before.early)
                elif before is not None and before.lane != st.lane:
                    steps_done(before.lane, before.k)
                s, a, w = st.s, st.a, st.what
                if w == "turn":
                    src = tok[st.args[0]][s]
                    for c in range(QT):
                        last = pe.transpose(chain_ps[:, c * P:(c + 1) * P], src[:, c, :], ident[:, :])
                elif w == "project_q":
                    last = pe.matmul(chain_ps[:, 0:S], weight(a.layer, f"q{a.n}"), feat["XT"][s][:, :],
                                     start=True, stop=True)
                elif w == "project_k":
                    last = pe.matmul(chain_ps[:, 0:S], weight(a.layer, f"k{a.n}"), feat[a.keys][s][:, :],
                                     start=True, stop=True)
                elif w == "project_v":
                    for c in range(QT):
                        last = pe.matmul(chain_ps[:, c * P:(c + 1) * P], feat[a.keys][s][:, c * P:(c + 1) * P],
                                         weight(a.layer, f"v{a.n}"), start=True, stop=True)
                elif w == "energies0":
                    for c in range(QT):
                        for part in range(2):
                            last = pe.matmul(chain_ps[:, c * 16:(c + 1) * 16],
                                             split[st.lane][:, 1, part, c * P:(c + 1) * P], q_row0[st.lane][:, :],
                                             start=(part == 0), stop=(part == 1))
                elif w == "lengths":
                    for c in range(QT):
                        last = pe.matmul(chain_ps[0:16, 0:1], nonzero[st.lane][:, c, :], ones[:, 0:1],
                                         start=(c == 0), stop=(c == QT - 1))
                elif w == "out_projection":
                    for c in range(QT):
                        last = pe.matmul(chain_ps[:, c * P:(c + 1) * P], feat["ZT"][s][:, c * P:(c + 1) * P],
                                         weight(a.layer, f"o{a.n}"), start=True, stop=True)
                elif w == "l0_fc1":
                    last = pe.matmul(chain_ps[:, 0:S], weight("l0", "fc1"), feat["ZT"][s][:, :],
                                     start=True, stop=True)
                elif w == "l0_fc2":
                    for c in range(QT):
                        last = pe.matmul(chain_ps[:, c * P:(c + 1) * P], hidden[st.lane][:, 0, c * P:(c + 1) * P],
                                         weight("l0", "fc2"), start=True, stop=True)
                elif w == "ff1":
                    for q in range(2):
                        f = 2 * int(st.args[0]) + q
                        last = pe.matmul(chain_ps[:, q * S:(q + 1) * S], weight(a.layer, "ff1")[:, f * P:(f + 1) * P],
                                         feat["ZT"][s][:, :], start=True, stop=True)
                elif w == "ff2":
                    for c in range(QT):
                        for f in range(FC):
                            last = pe.matmul(chain_ps[:, c * P:(c + 1) * P], hidden[st.lane][:, f, c * P:(c + 1) * P],
                                             weight(a.layer, "ff2")[:, f * P:(f + 1) * P],
                                             start=(f == 0), stop=(f == FC - 1))
                elif w == "l2_in":
                    last = pe.matmul(chain_ps[:, 0:S], weight("l2", "in"), feat["XT"][s][:, :],
                                     start=True, stop=True)
                elif w == "l2_u":
                    last = pe.matmul(chain_ps[0:NS, 0:S], weight("l2", "bmat"), hidden[st.lane][:, 0, :],
                                     start=True, stop=True)
                elif w == "mod":
                    for c in range(QT):
                        last = pe.matmul(chain_ps[0:NS, 0:P], probs_all[:, s, c * NS:(c + 1) * NS], ones[:, :],
                                         start=(c == 0), stop=(c == QT - 1))
                elif w == "target":
                    for c in range(QT):
                        pe.matmul(chain_ps[:, c * P:(c + 1) * P], h_all.rearrange("p (t b) -> p t b", b=B)[:, c * P:(c + 1) * P, s],
                                  w64[:, P:2 * P], start=True, stop=False)
                        last = pe.matmul(chain_ps[:, c * P:(c + 1) * P], mod_b[s], w64[:, 2 * P:3 * P],
                                         start=False, stop=True)
                last.then_inc(sig[f"product_ready{st.lane}"], 1)

            if ph == 1:
                pe.wait_ge(loaded["tokens"], 16)
            for kind, n, g in plan.order:
                if kind == "scores":
                    core_scores(n, g)
                elif kind == "turn":
                    core_turn(n, g)
                elif kind == "values":
                    core_values(n, g)
                else:
                    if n.what == "project_k" and n.a is L1S:
                        pe.wait_ge(loaded["l1"], 16)
                    if n.what == "project_k" and n.a is L2A:
                        pe.wait_ge(loaded["l2"], 2 * 16)
                    chain_step(n)

        def tensor_scan(pe):
            def inputs(ring, done):
                pe.wait_ge(u_ready, done)
                pe.matmul(z_bank[ring][:, 0:BLOCK * B], w64[:, 0:P], u_block[ring][:, :], start=True, stop=False,
                          skip_group_check=True).then_inc(z_ready, 1)

            def turn(at, last):
                for ring in range(RINGS):
                    for j in range(BLOCK):
                        if j == BLOCK // 2 and not (last and ring == RINGS - 1):
                            inputs((ring + 1) % RINGS, at + ring + 2)
                        pe.wait_ge(h_ready, at * BLOCK + (ring * BLOCK + j + 1))
                        h = h_ring[ring][:, (j - 1) * B:j * B] if j else h_ring[ring - 1][:, (BLOCK - 1) * B:]
                        pe.matmul(z_bank[ring][:, j * B:(j + 1) * B], w64[:, 0:P], h, start=False,
                                  stop=(j == BLOCK - 1), skip_group_check=True).then_inc(drive_ready, 1)
                        for width in WARMING:
                            pe.matmul(scores[:, 0, 0:width], ident16[:, :], warm_rows[:, 0:width], start=True,
                                      stop=True, skip_group_check=True)

            inputs(0, 1)
            with pe.Fori(0, BLOCKS // RINGS - 1) as i:
                turn(i * RINGS, False)
            turn(BLOCKS - RINGS, True)

        @block.tensor
        def _(pe):
            pe.wait_ge(loaded["ident"], 16)
            pe.wait_ge(loaded["l0"], 16)
            pe.wait_ge(consts_made, 10)
            pe.wait_ge(consts_cast, 2)
            for ph, plan in ((1, PLAN1), (3, PLAN3)):
                sig = signals[ph]
                if ph == 3:
                    tensor_scan(pe)
                    pe.wait_ge(loaded["l3"], 2 * 16)
                    pe.wait_ge(h_saved, RINGS + BLOCKS)
                tensor_phase(pe, ph, plan, sig)

        def scalar_phase(act, ph, plan, sig):
            def core_exp(n, g):
                a, s = plan.jobs[n]
                gi = plan.base[n] + g
                act.wait_ge(sig["max_ready"], gi + 1)
                if gi >= 2:
                    act.wait_ge(sig["turned_ready"], 2 * (gi - 1))
                seen = a.seen(a.group(g)[0])
                for pos in range(4):
                    if a.bias is None:
                        src = scores[:, 2 * (gi % 2) + pos // 2, (pos % 2) * S:(pos % 2) * S + seen]
                    else:
                        src = biased[gi % 2][:, pos, :]
                    last = act.activation(probs[gi % 2][:, pos, 0:seen], src, ACT.Exp,
                                          bias=minus_max[:, gi % 2, pos:pos + 1])
                last.then_inc(sig["probs_ready"], 1)

            def core_keep(n, g, half):
                gi = plan.base[n] + g
                act.wait_ge(sig["turned_ready"], 2 * gi + half + 1)
                if gi >= 2:
                    act.wait_ge(sig["mixed_ready"], gi - 1)
                a = plan.jobs[n][0]
                act.activation(kept_part(probs_t[gi % 2][:, half * 512:(half + 1) * 512], a, g),
                               kept_part(turned[:, half, :], a, g), ACT.Copy)\
                    .then_inc(sig[f"kept{half}"], 1)

            def chain_step(st):
                s, a, w = st.s, st.a, st.what
                if w not in ("turn", "l0_fc1", "ff1", "l2_in", "mod"):
                    return
                act.wait_ge(sig[f"product_ready{st.lane}"], st.product)
                if w == "turn":
                    last = act.activation(feat[st.args[1]][s][:, :], chain_ps[:, 0:S], ACT.Copy)
                elif w == "l0_fc1":
                    last = act.activation(hidden[st.lane][:, 0, :], chain_ps[:, 0:S], ACT.Relu, bias=col("l0_fc1b"))
                elif w == "ff1":
                    for q in range(2):
                        f = 2 * int(st.args[0]) + q
                        last = act.activation(hidden[st.lane][:, f, :], chain_ps[:, q * S:(q + 1) * S],
                                              ACT.Relu if ph == 1 else ACT.Gelu, bias=col(f"{a.layer}_ff1b{f}"))
                elif w == "l2_in":
                    last = act.activation(hidden[st.lane][:, 0, :], chain_ps[:, 0:S], ACT.Identity, bias=col("l2_bin"))
                elif w == "mod":
                    last = act.activation(mod_b[s], chain_ps[0:NS, 0:P], ACT.Copy, scale=1.0 / S)
                last.then_inc(sig[f"step_done{st.lane}"], 1)

            for kind, n, g in plan.order:
                if kind == "scores":
                    core_exp(n, g)
                elif kind == "turn":
                    core_keep(n, g, 0)
                    if plan.jobs[n][0].bias is not None:
                        core_keep(n, g, 1)
                elif kind == "step":
                    chain_step(n)

        def scalar_scan(act):
            def turn(at):
                for ring in range(RINGS):
                    act.wait_ge(h_saved, at + ring + 1)
                    for j in range(BLOCK):
                        act.wait_ge(drive_ready, at * BLOCK + (ring * BLOCK + j + 1))
                        act.activation(h_ring[ring][:, j * B:(j + 1) * B], z_bank[ring][0:NS, j * B:(j + 1) * B],
                                       ACT.Silu).then_inc(h_ready, 1)

            with act.Fori(0, BLOCKS // RINGS - 1) as i:
                turn(i * RINGS)
            turn(BLOCKS - RINGS)

        @block.scalar
        def _(act):
            act.wait_ge(loaded["vectors"], 2 * 16)
            act.wait_ge(consts_made, 10)
            for ph, plan in ((1, PLAN1), (3, PLAN3)):
                if ph == 3:
                    scalar_scan(act)
                scalar_phase(act, ph, plan, signals[ph])

        def vector_phase(dve, ph, plan, sig, link_sem):
            done = [0]

            def link(ins):
                done[0] += 1
                ins.then_inc(link_sem, 1)
                dve.wait_ge(link_sem, done[0])

            def product_read(ins, st):
                ins.then_inc(sig["product_read"], 1)
                dve.wait_ge(sig["product_read"], st.early)

            def core_max(n, g):
                a, s = plan.jobs[n]
                gi = plan.base[n] + g
                qt, m, heads = a.group(g)
                par = gi % 2
                dve.wait_ge(sig["scores_ready"], gi + 1)
                src = scores[:, 2 * par:2 * par + 2, :].rearrange("p u (v k) -> p (u v) k", v=2)[:, :, 0:a.seen(qt)]
                if a.bias is not None:
                    if g == 0:
                        dve.wait_ge(loaded["bias"], 4 * 16)
                    for pos in range(4):
                        last = dve.tensor_tensor_reduce(
                            biased[par][:, pos, :], src[:, pos, :],
                            pair_bias[a.bias][:, qt, m, pos * S:(pos + 1) * S], 1.0, LOWEST, ALU.add, ALU.max,
                            accum_out=row_maxima[:, par, pos:pos + 1])
                    link(last)
                    out = minus_max_raw if a.guard else minus_max
                    last = dve.tensor_scalar(out[:, par, :], row_maxima[:, par, :], -1.0, None, ALU.mult)
                else:
                    out = minus_max_raw if a.guard else minus_max
                    last = dve.tensor_reduce(out[:, par, :], src, axis=AX.X, op=ALU.max, negate=True)
                if a.guard:
                    link(last)
                    last = dve.scalar_tensor_tensor(minus_max[:, par, :], minus_max_raw[:, par, :], UNMASKED_MIN,
                                                    minus_max_raw[:, par, :], op0=ALU.is_lt, op1=ALU.mult)
                last.then_inc(sig["max_ready"], 1)

            def core_keep(n, g):
                gi = plan.base[n] + g
                dve.wait_ge(sig["turned_ready"], 2 * gi + 2)
                if gi >= 2:
                    dve.wait_ge(sig["mixed_ready"], gi - 1)
                a = plan.jobs[n][0]
                dve.tensor_copy(kept_part(probs_t[gi % 2][:, 512:1024], a, g), kept_part(turned[:, 1, :], a, g))\
                    .then_inc(sig["kept1"], 1)

            def moments_of(src, st):
                for c in range(QT):
                    last = dve.bn_stats(stats[st.lane][:, c, :], src[:, c, :])
                link(last)
                dve.memset(spacer[:, :], 0.0)
                for c in range(QT):
                    last = dve.bn_aggr(moments[st.lane][:, c, :], stats[st.lane][:, c, :])
                last.then_inc(sig[f"variance_ready{st.lane}"], 1)

            def layer_norm(src, dst, gain, shift, st):
                for c in range(QT):
                    last = dve.tensor_scalar(centred[st.lane][:, c, :], src[:, c, :], moments[st.lane][:, c, 0:1], rstd[st.lane][:, c:c + 1],
                                             ALU.subtract, ALU.mult)
                link(last)
                link(dve.tensor_tensor(centred[st.lane][:, :, :], centred[st.lane][:, :, :], row(gain), ALU.mult))
                return dve.tensor_tensor(dst[:, :, :], centred[st.lane][:, :, :], row(shift), ALU.add)

            def keep_rows(dst, src, which):
                for c in range(QT):
                    last = dve.tensor_scalar(dst[:, c, :], src[:, c, :], row_keep_s[:, which, c:c + 1], None,
                                             ALU.mult)
                return last

            def find_rows(src, which, s):
                link(dve.tensor_reduce(row_max[s][:, which, :], src[:, :, :], axis=AX.X, op=ALU.max,
                                       apply_absolute_value=True))
                return dve.tensor_scalar(row_keep[s][:, which, :], row_max[s][:, which, :], 0.0, None,
                                         ALU.not_equal)

            for kind, n, g in plan.order:
                if kind == "scores":
                    if ph == 1 and (plan.jobs[n], g) == ((L2A, 3), 0):
                        dve.wait_ge(sig["scores_ready"], plan.base[n])
                        vector_masks3(dve, link)
                    core_max(n, g)
                    continue
                if kind == "turn":
                    if plan.jobs[n][0].bias is None:
                        core_keep(n, g)
                    continue
                if kind == "values":
                    continue
                st, s, a, w = n, n.s, n.a, n.what
                row_keep_s = row_keep[s]
                X, X1, X2, Z, C, CM, O = (tok[i][s] for i in ("X", "X1", "X2", "Z", "C", "CM", "O"))
                if w in ("turn", "l0_fc1", "ff1", "l2_in", "mod"):
                    continue
                if st.on_pe:
                    dve.wait_ge(sig[f"product_ready{st.lane}"], st.product)
                elif st.k > 1:
                    dve.wait_ge(sig[f"step_done{st.lane}"], st.k - 1)
                if w == "project_k" and a is L1S:
                    dve.wait_ge(loaded["rows"], 16)
                if w == "apply" and st.args[0] == "l0_ln1":
                    dve.wait_ge(loaded["context"], 16)
                product = chain_ps[:, 0:S].rearrange("p (t f) -> p t f", t=QT)
                if w == "load":
                    dve.tensor_scalar(
                        target[s][:, :, :], target_mask[:, s, :].rearrange("p (t k) -> p t k", t=QT), MASKED, None,
                        ALU.mult)
                    last = find_rows(X, 0, s)
                elif w in ("project_q", "project_k"):
                    queries = w == "project_q"
                    earlier = [n for n in range(st.job) if plan.lanes[n] == st.lane]
                    if earlier:
                        for pair in range(2):
                            dve.wait_ge(sig[f"stacked{earlier[-1] % 2}_pair{pair}"], stacked_by(earlier[-1]))
                    upper, lower = split[st.lane][:, 1 - queries, 0, :], split[st.lane][:, 1 - queries, 1, :]
                    whole = two(centred[st.lane])
                    product_read(dve.tensor_scalar(whole, chain_ps[:, 0:S], col(a.bq if queries else a.bk),
                                                   a.scale if queries else 1.0, ALU.add, ALU.mult), st)
                    link(dve.tensor_scalar(upper.bitcast(I32), whole.bitcast(I32), UPPER_BITS, None,
                                           ALU.bitwise_and))
                    last = dve.tensor_tensor(lower, whole, upper, ALU.subtract)
                    if a.lengths and queries:
                        last = dve.tensor_tensor(q_row0[st.lane][:, :], whole[:, 0:1].to_broadcast([P, 16]), head_blocks[:, :],
                                          ALU.mult)
                elif w == "project_v":
                    if st.job >= 2:
                        dve.wait_ge(sig["mixed_ready"], plan.base[st.job - 1])
                    vb = value_buffer(a, st.job)[:, :, 0:a.heads * (a.width + 1)]\
                        .rearrange("p t (h d) -> p t h d", h=a.heads)
                    for c in range(QT):
                        last = dve.tensor_tensor(
                            vb[:, c, :, 0:a.width], product[:, c, :].rearrange("p (h d) -> p h d", h=a.heads),
                            rows[:, ROWS.index(a.bv), :].rearrange("p (h d) -> p h d", h=a.heads), ALU.add)
                elif w == "energies0":
                    last = dve.tensor_scalar(nonzero[st.lane][:, :, :].rearrange("p t h -> p (t h)"), chain_ps[:, 0:32],
                                             0.0, None, ALU.not_equal)
                elif w == "lengths":
                    last = dve.tensor_scalar(length_mask[st.job % 2][0:16, :], iota[:, :], chain_ps[0:16, 0:1],
                                             MASKED, ALU.is_ge, ALU.mult)
                elif w == "normalize":
                    dve.wait_ge(sig["mixed_ready"], plan.base[st.job + 1])
                    w1 = a.width + 1
                    mx = mixed[:, 0:QT * a.heads * w1].rearrange("p (th d) -> p th d", d=w1)
                    inv = inverse[st.lane][:, :, :].rearrange("p t h -> p (t h)")[:, 0:QT * a.heads]
                    link(dve.reciprocal(inv, mx[:, :, a.width]))
                    last = dve.tensor_tensor(
                        two(Z).rearrange("p (th d) -> p th d", d=a.width), mx[:, :, 0:a.width],
                        inv.unsqueeze(2).to_broadcast([P, QT * a.heads, a.width]), ALU.mult)
                elif w == "l0_ln1":
                    link(keep_rows(Z, Z, 0))
                    link(dve.tensor_tensor(Z[:, :, :], Z[:, :, :], X[:, :, :], ALU.add))
                    moments_of(Z, st)
                    continue
                elif w == "l0_ln2":
                    link(keep_rows(Z, Z, 1))
                    link(dve.tensor_tensor(Z[:, :, :], Z[:, :, :], X1[:, :, :], ALU.add))
                    moments_of(Z, st)
                    continue
                elif w == "l0_fc2":
                    product_read(dve.tensor_tensor(Z[:, :, :], product, row("l0_fc2b"), ALU.add), st)
                    link(keep_rows(Z, Z, 0))
                    link(dve.tensor_tensor(Z[:, :, :], Z[:, :, :], X2[:, :, :], ALU.add))
                    moments_of(Z, st)
                    continue
                elif w == "out_projection":
                    product_read(dve.tensor_tensor(Z[:, :, :], product, row(f"{a.layer}_bo{a.n}"), ALU.add), st)
                    old = X if a.n == 1 else X1
                    link(dve.tensor_tensor(Z[:, :, :], Z[:, :, :], old[:, :, :], ALU.add))
                    if a is L2A:
                        dve.tensor_copy(X[:, :, :], Z[:, :, :])
                    moments_of(Z, st)
                    continue
                elif w == "ff2":
                    product_read(dve.tensor_tensor(Z[:, :, :], product, row(f"{a.layer}_ff2b"), ALU.add), st)
                    if ph == 1:
                        link(dve.scalar_tensor_tensor(two(Z), two(Z), 0.0, two(X2), op0=ALU.max, op1=ALU.add))
                    else:
                        link(dve.tensor_tensor(Z[:, :, :], Z[:, :, :], X2[:, :, :], ALU.add))
                    moments_of(Z, st)
                    continue
                elif w == "l2_ln_x":
                    moments_of(X, st)
                    continue
                elif w == "l2_ln_base":
                    moments_of(C, st)
                    continue
                elif w == "apply":
                    what = st.args[0]
                    if what == "l0_ln1":
                        link(layer_norm(Z, X1, "l0_g1", "l0_b1", st))
                        link(find_rows(X1, 1, s))
                        last = keep_rows(CM, C, 1)
                    elif what == "l0_ln2":
                        last = layer_norm(Z, X2, "l0_g2", "l0_b2", st)
                    elif what == "l0_fc2":
                        last = layer_norm(Z, X, "l0_g3", "l0_b3", st)
                    elif what == "out_projection":
                        if a is L2A:
                            last = layer_norm(Z, X1, "l2_g2", "l2_b2", st)
                        else:
                            last = layer_norm(Z, X1 if a.n == 1 else X2, f"{a.layer}_g{a.n}", f"{a.layer}_b{a.n}", st)
                    elif what == "ff2" and ph == 1:
                        last = layer_norm(Z, X, "l1_g3", "l1_b3", st)
                    elif what == "ff2":
                        last = layer_norm(Z, O, "l3_g3", "l3_b3", st)
                    elif what == "l2_ln_x":
                        last = layer_norm(X, X1, "l2_g1", "l2_b1", st)
                    else:
                        last = layer_norm(C, CM, "l2_g1", "l2_b1", st)
                elif w == "l2_u":
                    if s == 0:
                        link(dve.memset(u_all[:, 0:B], 0.0))
                    dst = u_all[:, B:B + S * B].rearrange("p (t b) -> p t b", b=B)
                    last = dve.tensor_copy(dst[:, :, s], chain_ps[0:NS, 0:S])
                elif w == "target":
                    link(dve.tensor_tensor(X[:, :, :], X[:, :, :], row("l2_bprog"), ALU.add))
                    last = dve.tensor_tensor(X[:, :, :], product, X[:, :, :], ALU.add)
                last.then_inc(sig[f"step_done{st.lane}"], 1)

        def vector_masks3(dve, link):
            dve.wait_ge(loaded["mask3"], 16)
            link(dve.tensor_copy(key_keep, mask3_in))
            link(dve.tensor_scalar(keep2, causal[:, :, :], 0.0, None, ALU.is_equal))
            link(dve.tensor_tensor(keep2, keep2, key_keep.unsqueeze(1).to_broadcast([P, QT, S]), ALU.mult))
            link(dve.tensor_scalar(self3[:, :, :], keep2, -MASKED, MASKED, ALU.mult, ALU.add))
            link(dve.tensor_scalar(cross3[:, :, :], key_keep.unsqueeze(1).to_broadcast([P, QT, S]),
                                   -MASKED, MASKED, ALU.mult, ALU.add))

        def vector_scan(dve):
            WIDTH = BLOCK * B

            def inputs(ring, at):
                dve.tensor_scalar(u_block[ring][:, :], u_all[:, at], 1.0, None, ALU.mult).then_inc(u_ready, 1)

            def turn(at, columns, last):
                for ring in range(RINGS):
                    if not last:
                        dve.wait_ge(z_ready, at + ring + 1)
                        inputs(ring, columns(RINGS + ring, 0))
                    dve.wait_ge(h_ready, at * BLOCK + ((ring + 1) * BLOCK + 1))
                    dve.tensor_tensor(h_all[:, columns(ring, 0)], h_ring[ring][:, :], u_all[:, columns(ring, B)],
                                      ALU.add).then_inc(h_saved, 1)

            for ring in range(RINGS):
                inputs(ring, slice(ring * WIDTH, (ring + 1) * WIDTH))
            with dve.Fori(0, BLOCKS // RINGS - 1) as i:
                turn(i * RINGS, lambda ring, shift: bass.ds(i * (RINGS * WIDTH) + (ring * WIDTH + shift), WIDTH), False)
            first = (BLOCKS - RINGS) * WIDTH
            turn(BLOCKS - RINGS, lambda ring, shift: slice(first + ring * WIDTH + shift,
                                                           first + (ring + 1) * WIDTH + shift), True)

        @block.vector
        def _(dve):
            dve.wait_ge(loaded["tokens"], 16)
            dve.wait_ge(loaded["ident"], 16)
            dve.wait_ge(loaded["consts"], 3 * 16)
            dve.wait_ge(loaded["vectors"], 2 * 16)
            dve.wait_ge(loaded["masks"], 16)
            dve.wait_ge(consts_made, 10)
            done = [0]

            def link(ins):
                done[0] += 1
                ins.then_inc(vector_link, 1)
                dve.wait_ge(vector_link, done[0])

            dve.tensor_copy(ident16[:, :], ident[:, :]).then_inc(consts_cast, 1)
            dve.tensor_copy(causal[:, :, :], causal_in).then_inc(consts_cast, 1)
            dve.wait_ge(consts_cast, 2)
            for ph, plan, lk in ((1, PLAN1, vector_link1), (3, PLAN3, vector_link3)):
                if ph == 3:
                    for lane in range(LANES):
                        dve.wait_ge(signals[1][f"step_done{lane}"], PLAN1.counts[lane]["step"])
                    vector_scan(dve)
                vector_phase(dve, ph, plan, signals[ph], lk)


def _host_arrays(i):
    c = np.ascontiguousarray

    def tokens(v):
        v = v.reshape(B, QT, P, v.shape[-1]).transpose(2, 0, 1, 3)
        return c(v.reshape(P, B, -1))

    def heads(w):
        return w.transpose(1, 0, 2).reshape(P, P)

    def placed(w):
        v = w.reshape(-1, 2, 2, 2, 2, 8).transpose(0, 1, 4, 2, 3, 5)
        return v.reshape(w.shape)

    def placed8(w):
        v = w.reshape(-1, 2, 2, 2, 16).transpose(0, 1, 3, 2, 4)
        return v.reshape(w.shape)

    def chunks(w):
        return w.reshape(FC, P, P).transpose(1, 0, 2).reshape(P, FF)

    def pair(v):
        return c(v.reshape(16, QT, P, S).transpose(2, 1, 0, 3).reshape(P, QT, 4, 4 * S))

    L0, L1, L2, L3 = ({k[len(p):]: v for k, v in i.items() if k.startswith(p)}
                      for p in ("L0_xattn_", "L1_xattn_", "L2_xattn_", "L3_xattn_"))
    out = {
        "x": tokens(i["x"]), "ctx": tokens(i["ctx_1024"]), "probs": tokens(i["ctxb_2048x64"]),
        "target_mask": tokens(i["mask_BxSxS2_bk1"]), "mask3": c(i["mask_1xS2_if1"].reshape(S)),
        "bias0": pair(i["fside_1x16xSxS2_0"]), "bias1": pair(L1["attn_2d_bias"]),
        "w_l0": np.concatenate([placed(heads(L0["Wq1"])), placed(heads(L0["Wk1"])), heads(L0["Wv1"]), placed(heads(L0["Wq2"])),
                                placed(heads(L0["Wk2"])), heads(L0["Wv2"]), L0["fc1_w"].T, L0["fc2_w"].T], 1),
        "w_l1": np.concatenate([placed(L1["sa_wq"]), placed(L1["sa_wk"]), L1["sa_wv"], L1["sa_wo"], placed(L1["ca_wq"]), placed(L1["ca_wk"]),
                                L1["ca_wv"], L1["ca_wo"], L1["ff_w1"], chunks(L1["ff_w2"])], 1),
        "w_l2": np.concatenate([placed8(L2["W_qkv"][0:P].T), placed8(L2["W_qkv"][P:2 * P].T), L2["W_qkv"][2 * P:].T,
                                L2["W_o"].T, L2["W_in"].T, L2["Bmat"]], 1),
        "w64": np.concatenate([L2["A"].T, np.zeros((NS, P - NS), np.float32), L2["Cmat"], L2["W_prog"].T], 1),
        "w_l3": np.concatenate([placed(L3["Wqkv"][:, 0:P]), placed(L3["Wqkv"][:, P:2 * P]), L3["Wqkv"][:, 2 * P:],
                                L3["Wo1"], placed(L3["Wq"]), placed(L3["Wk"]), L3["Wv"], L3["Wo2"], L3["W1"],
                                chunks(L3["W2"])], 1),
    }
    zero = np.zeros(P, np.float32)
    by_row = {"l0_g1": L0["ln1_g"], "l0_b1": L0["ln1_b"], "l0_g2": L0["ln2_g"], "l0_b2": L0["ln2_b"],
              "l0_g3": L0["ln3_g"], "l0_b3": L0["ln3_b"], "l0_fc2b": L0["fc2_b"],
              "l1_bv1": L1["sa_bv"], "l1_bo1": L1["sa_bo"], "l1_g1": L1["sa_g"], "l1_b1": L1["sa_b"],
              "l1_bv2": L1["ca_bv"], "l1_bo2": L1["ca_bo"], "l1_g2": L1["ca_g"], "l1_b2": L1["ca_b"],
              "l1_ff2b": L1["ff_b2"], "l1_g3": L1["ff_g"], "l1_b3": L1["ff_b"],
              "l2_bv1": L2["b_qkv"][2 * P:], "l2_bo1": L2["b_o"], "l2_g1": L2["g1"], "l2_b1": L2["beta1"],
              "l2_g2": L2["g2"], "l2_b2": L2["beta2"], "l2_bprog": L2["b_prog"],
              "l3_bo1": L3["bo1"], "l3_g1": L3["g1"], "l3_b1": L3["b1"], "l3_bo2": L3["bo2"], "l3_g2": L3["g2"],
              "l3_b2": L3["b2"], "l3_ff2b": L3["bf2"], "l3_g3": L3["g3"], "l3_b3": L3["b3"], "zero": zero}
    by_col = {"l0_fc1b": L0["fc1_b"], "l1_bq1": placed(L1["sa_bq"]), "l1_bk1": placed(L1["sa_bk"]), "l1_bq2": placed(L1["ca_bq"]),
              "l1_bk2": placed(L1["ca_bk"]), "l2_bq1": placed8(L2["b_qkv"][0:P]), "l2_bk1": placed8(L2["b_qkv"][P:2 * P]),
              "l2_bin": L2["b_in"], "zero": zero}
    for f in range(FC):
        by_col[f"l1_ff1b{f}"] = L1["ff_b1"][f * P:(f + 1) * P]
        by_col[f"l3_ff1b{f}"] = L3["bf1"][f * P:(f + 1) * P]
    out["rows"] = np.concatenate([by_row[n] for n in ROWS])
    out["cols"] = np.stack([by_col[n] for n in COLS], 1)
    p, k = np.arange(P), np.arange(S)
    out["ident"] = np.eye(P, dtype=np.float32)
    out["head_blocks"] = ((p // 8)[:, None] == np.arange(16)[None, :]).astype(np.float32)
    out["iota"] = np.tile(k.astype(np.float32), (16, 1))
    q = (np.arange(QT)[None, :] * P + p[:, None])[:, :, None]
    out["causal"] = np.where(k[None, None, :] > q, np.float32(MASKED), np.float32(0))
    return {n: c(v) for n, v in out.items()}


_INPUTS = ["x", "ctx", "probs", "target_mask", "mask3", "bias0", "bias1", "w_l0", "w_l1", "w_l2", "w64", "w_l3",
           "rows", "cols", "ident", "head_blocks", "iota", "causal"]


def kernel(**inputs):
    import concourse.bacc as bacc
    from concourse.bass_utils import run_bass_kernel_spmd

    arrays = _host_arrays({k: np.asarray(v) for k, v in inputs.items()})

    nc = bacc.Bacc("TRN2", target_bir_lowering=False, num_devices=1)
    t = {n: nc.dram_tensor(f"in_{n}", arrays[n].shape, mybir.dt.from_np(arrays[n].dtype),
                           kind="ExternalInput").ap() for n in _INPUTS}
    t["out"] = nc.dram_tensor("out_x", (P, B * S), F32, kind="ExternalOutput").ap()
    build(nc, t)
    r = run_bass_kernel_spmd(nc, [{f"in_{n}": arrays[n] for n in _INPUTS}], core_ids=[0])
    out = r.results[0]["out_x"]
    return np.ascontiguousarray(out.reshape(P, B, QT, P).transpose(1, 2, 0, 3).reshape(B, S, P))
```
